# Optimizing a Trainium2 kernel written in Bass

```python
import numpy as np
import jax
import jax.numpy as jnp

def _softmax(x, axis=-1):
    return jax.nn.softmax(x, axis=axis)
def _gelu(x):
    return jax.nn.gelu(x, approximate=True)
def _silu(x):
    return jax.nn.silu(x)
def _sigmoid(x):
    return jax.nn.sigmoid(x)
def _layernorm(x, axis=-1, eps=1e-5):
    m = jnp.mean(x, axis=axis, keepdims=True)
    v = jnp.var(x, axis=axis, keepdims=True)
    return (x - m) / jnp.sqrt(v + eps)
def _scatter_add(tgt, idx, src, axis=0):
    return tgt.at[idx].add(src)
def _segment_sum(src, seg, n):
    return jax.ops.segment_sum(src, seg, n)

kernel_name = 'mk_conv_seq_d2_conv_nchw64_7a2cd6'

def setup_inputs(seed: int = 0):
    np.random.seed(seed)
    _w = jnp.asarray
    def _rec_inputs():
        import jax
        import jax.numpy as jnp
        _gk = jax.random.key(seed)
        x = 7.22e-05 + 1 * jax.random.normal(jax.random.fold_in(_gk, 1), (2, 64, 256, 256), jnp.float32)
        return x
    x = _rec_inputs()
    def _L0_conv_setup():
        import jax, jax.numpy as jnp
        import numpy as np
        N, C, H, W, D = (2, 64, 256, 256, 2)
        NW, HEADS, TOPK, KVW = (8, 8, 4, 4)

        def _conv(x, w, b, pad, groups=1):
            y = jax.lax.conv_general_dilated(x, w, (1, 1), [(pad, pad), (pad, pad)], dimension_numbers=('NCHW', 'OIHW', 'NCHW'), feature_group_count=groups)
            return y if b is None else y + b[None, :, None, None]

        def _ln(x, g, b):
            m = x.mean(-1, keepdims=True)
            v = ((x - m) ** 2).mean(-1, keepdims=True)
            return (x - m) * jax.lax.rsqrt(v + 1e-06) * g + b

        def _attn(y, qkv_w, qkv_b, lepe_w, lepe_b, wo_w, wo_b):
            n, h, w, c = y.shape
            hw, ww = (h // NW, w // NW)
            p2 = NW * NW
            hd = c // HEADS
            scale = c ** (-0.5)
            qkv = y @ qkv_w + qkv_b
            q, kimg, vimg = jnp.split(qkv, 3, -1)

            def win(t):
                return t.reshape(n, NW, hw, NW, ww, c).transpose(0, 1, 3, 2, 4, 5).reshape(n, p2, hw, ww, c)
            qw, kw, vw = (win(q), win(kimg), win(vimg))
            q_win = qw.mean((2, 3))
            k_win = kw.mean((2, 3))
            logits = jnp.einsum('npc,nqc->npq', q_win * scale, k_win)
            _, r_idx = jax.lax.top_k(logits, TOPK)
            kv = jnp.concatenate([kw, vw], -1)
            kvp = kv.reshape(n, p2, KVW, hw // KVW, KVW, ww // KVW, 2 * c).mean((3, 5))
            kvp = kvp.reshape(n, p2, KVW * KVW, 2 * c)
            kv_sel = jax.vmap(lambda t, i: t[i])(kvp, r_idx)
            k_sel, v_sel = jnp.split(kv_sel, 2, -1)
            kt = TOPK * KVW * KVW
            k_sel = k_sel.reshape(n, p2, kt, HEADS, hd)
            v_sel = v_sel.reshape(n, p2, kt, HEADS, hd)
            qp = qw.reshape(n, p2, hw * ww, HEADS, hd)
            att = jax.nn.softmax(jnp.einsum('npqhc,npkhc->nphqk', qp * scale, k_sel), -1)
            out = jnp.einsum('nphqk,npkhc->npqhc', att, v_sel).reshape(n, p2, hw, ww, c)
            out = out.reshape(n, NW, NW, hw, ww, c).transpose(0, 1, 3, 2, 4, 5).reshape(n, h, w, c)
            lepe = _conv(vimg.transpose(0, 3, 1, 2), lepe_w, lepe_b, 2, groups=c).transpose(0, 2, 3, 1)
            return (out + lepe) @ wo_w + wo_b

        def _glu(y, fc1_w, fc1_b, pw_w, dw_w, dw_b, fc2_w, fc2_b):
            t = y @ fc1_w + fc1_b
            xh, vh = jnp.split(t, 2, -1)
            xh = xh.transpose(0, 3, 1, 2)
            xh = _conv(xh, pw_w, None, 0)
            xh = _conv(xh, dw_w, dw_b, 1, groups=dw_w.shape[0])
            xh = jax.nn.gelu(xh, approximate=False) * vh.transpose(0, 3, 1, 2)
            return xh.transpose(0, 2, 3, 1) @ fc2_w + fc2_b
        key = jax.random.key(seed)
        ks = iter(jax.random.split(key, 32))

        def rn(shape, s=0.05):
            return jax.random.normal(next(ks), shape, jnp.float32) * s
        inp = {'x': jax.random.normal(next(ks), (N, C, H, W), jnp.float32)}
        inp.update(pos_w=rn((D, C, 1, 3, 3)), pos_b=jnp.zeros((D, C), jnp.float32), ln1_g=jnp.ones((D, C), jnp.float32), ln1_b=jnp.zeros((D, C), jnp.float32), qkv_w=rn((D, C, 3 * C)), qkv_b=jnp.zeros((D, 3 * C), jnp.float32), lepe_w=rn((D, C, 1, 5, 5)), lepe_b=jnp.zeros((D, C), jnp.float32), wo_w=rn((D, C, C)), wo_b=jnp.zeros((D, C), jnp.float32), ln2_g=jnp.ones((D, C), jnp.float32), ln2_b=jnp.zeros((D, C), jnp.float32), fc1_w=rn((D, C, 4 * C)), fc1_b=jnp.zeros((D, 4 * C), jnp.float32), pw_w=rn((D, 2 * C, 2 * C, 1, 1)), dw_w=rn((D, 2 * C, 1, 3, 3)), dw_b=jnp.zeros((D, 2 * C), jnp.float32), fc2_w=rn((D, 2 * C, C)), fc2_b=jnp.zeros((D, C), jnp.float32))
        return inp
    _L0_conv_all = _L0_conv_setup()
    _L0_conv_in = {k: v for k, v in _L0_conv_all.items() if k in ('pos_w', 'pos_b', 'ln1_g', 'ln1_b', 'qkv_w', 'qkv_b', 'lepe_w', 'lepe_b', 'wo_w', 'wo_b', 'ln2_g', 'ln2_b', 'fc1_w', 'fc1_b', 'pw_w', 'dw_w', 'dw_b', 'fc2_w', 'fc2_b', )}
    del _L0_conv_all

    def _L1_conv_setup():
        import jax, jax.numpy as jnp
        import numpy as np
        B, C, H, W = (32, 64, 112, 112)
        HID, GROUPS = (128, 8)
        INNER_STEPS, INNER_LR, INNER_MOM = (3, 0.01, 0.9)
        GN_EPS = 1e-05

        def _gelu(v):
            return jax.nn.gelu(v, approximate=False)

        def _modifier(params, x):
            w1, gn_w, gn_b, w2 = params
            h = jnp.einsum('bchw,oc->bohw', x, w1)
            b, o, hh, ww = h.shape
            hg = h.reshape(b, GROUPS, o // GROUPS, hh, ww)
            mu = hg.mean(axis=(2, 3, 4), keepdims=True)
            var = hg.var(axis=(2, 3, 4), keepdims=True)
            hg = (hg - mu) * jax.lax.rsqrt(var + GN_EPS)
            h = hg.reshape(b, o, hh, ww) * gn_w[None, :, None, None] + gn_b[None, :, None, None]
            h = _gelu(h)
            return jnp.einsum('bohw,co->bchw', h, w2)

        def _surprise(y, rm, rv):
            n = y.shape[0] * y.shape[2] * y.shape[3]
            cm = y.mean(axis=(0, 2, 3))
            cv = ((y - cm[None, :, None, None]) ** 2).sum(axis=(0, 2, 3)) / (n - 1)
            return jnp.mean((cm - rm) ** 2) + jnp.mean((cv / (rv + 1e-08) - 1.0) ** 2)
        key = jax.random.key(seed)
        ks = jax.random.split(key, 6)
        return {'x': jax.random.normal(ks[0], (B, C, H, W), jnp.float32), 'w1': jax.random.normal(ks[1], (HID, C), jnp.float32) * C ** (-0.5), 'gn_w': jnp.ones((HID,), jnp.float32), 'gn_b': jnp.zeros((HID,), jnp.float32), 'w2': jax.random.normal(ks[2], (C, HID), jnp.float32) * HID ** (-0.5), 'g1_w': jax.random.normal(ks[3], (16, C), jnp.float32) * C ** (-0.5), 'g1_b': jnp.zeros((16,), jnp.float32), 'g2_w': jax.random.normal(ks[4], (1, 16), jnp.float32) * 0.25, 'g2_b': jnp.zeros((1,), jnp.float32), 'running_mean': jnp.zeros((C,), jnp.float32), 'running_var': jnp.ones((C,), jnp.float32), 'residual_scale': jnp.full((1,), 0.05, jnp.float32)}
    _L1_conv_all = _L1_conv_setup()
    _L1_conv_in = {k: v for k, v in _L1_conv_all.items() if k in ('w1', 'gn_w', 'gn_b', 'w2', 'g1_w', 'g1_b', 'g2_w', 'g2_b', 'running_mean', 'running_var', 'residual_scale', )}
    del _L1_conv_all

    return {
        "x": x,
        "L0_conv_pos_w": _L0_conv_in["pos_w"],
        "L0_conv_pos_b": _L0_conv_in["pos_b"],
        "L0_conv_ln1_g": _L0_conv_in["ln1_g"],
        "L0_conv_ln1_b": _L0_conv_in["ln1_b"],
        "L0_conv_qkv_w": _L0_conv_in["qkv_w"],
        "L0_conv_qkv_b": _L0_conv_in["qkv_b"],
        "L0_conv_lepe_w": _L0_conv_in["lepe_w"],
        "L0_conv_lepe_b": _L0_conv_in["lepe_b"],
        "L0_conv_wo_w": _L0_conv_in["wo_w"],
        "L0_conv_wo_b": _L0_conv_in["wo_b"],
        "L0_conv_ln2_g": _L0_conv_in["ln2_g"],
        "L0_conv_ln2_b": _L0_conv_in["ln2_b"],
        "L0_conv_fc1_w": _L0_conv_in["fc1_w"],
        "L0_conv_fc1_b": _L0_conv_in["fc1_b"],
        "L0_conv_pw_w": _L0_conv_in["pw_w"],
        "L0_conv_dw_w": _L0_conv_in["dw_w"],
        "L0_conv_dw_b": _L0_conv_in["dw_b"],
        "L0_conv_fc2_w": _L0_conv_in["fc2_w"],
        "L0_conv_fc2_b": _L0_conv_in["fc2_b"],
        "L1_conv_w1": _L1_conv_in["w1"],
        "L1_conv_gn_w": _L1_conv_in["gn_w"],
        "L1_conv_gn_b": _L1_conv_in["gn_b"],
        "L1_conv_w2": _L1_conv_in["w2"],
        "L1_conv_g1_w": _L1_conv_in["g1_w"],
        "L1_conv_g1_b": _L1_conv_in["g1_b"],
        "L1_conv_g2_w": _L1_conv_in["g2_w"],
        "L1_conv_g2_b": _L1_conv_in["g2_b"],
        "L1_conv_running_mean": _L1_conv_in["running_mean"],
        "L1_conv_running_var": _L1_conv_in["running_var"],
        "L1_conv_residual_scale": _L1_conv_in["residual_scale"],
    }

def reference(x, L0_conv_pos_w, L0_conv_pos_b, L0_conv_ln1_g, L0_conv_ln1_b, L0_conv_qkv_w, L0_conv_qkv_b, L0_conv_lepe_w, L0_conv_lepe_b, L0_conv_wo_w, L0_conv_wo_b, L0_conv_ln2_g, L0_conv_ln2_b, L0_conv_fc1_w, L0_conv_fc1_b, L0_conv_pw_w, L0_conv_dw_w, L0_conv_dw_b, L0_conv_fc2_w, L0_conv_fc2_b, L1_conv_w1, L1_conv_gn_w, L1_conv_gn_b, L1_conv_w2, L1_conv_g1_w, L1_conv_g1_b, L1_conv_g2_w, L1_conv_g2_b, L1_conv_running_mean, L1_conv_running_var, L1_conv_residual_scale):
    import jax
    import jax.numpy as jnp
    def _L0_conv_ref(x, pos_w, pos_b, ln1_g, ln1_b, qkv_w, qkv_b, lepe_w, lepe_b, wo_w, wo_b, ln2_g, ln2_b, fc1_w, fc1_b, pw_w, dw_w, dw_b, fc2_w, fc2_b):
        import jax, jax.numpy as jnp
        import numpy as np
        N, C, H, W, D = (2, 64, 256, 256, 2)
        NW, HEADS, TOPK, KVW = (8, 8, 4, 4)

        def _conv(x, w, b, pad, groups=1):
            y = jax.lax.conv_general_dilated(x, w, (1, 1), [(pad, pad), (pad, pad)], dimension_numbers=('NCHW', 'OIHW', 'NCHW'), feature_group_count=groups)
            return y if b is None else y + b[None, :, None, None]

        def _ln(x, g, b):
            m = x.mean(-1, keepdims=True)
            v = ((x - m) ** 2).mean(-1, keepdims=True)
            return (x - m) * jax.lax.rsqrt(v + 1e-06) * g + b

        def _attn(y, qkv_w, qkv_b, lepe_w, lepe_b, wo_w, wo_b):
            n, h, w, c = y.shape
            hw, ww = (h // NW, w // NW)
            p2 = NW * NW
            hd = c // HEADS
            scale = c ** (-0.5)
            qkv = y @ qkv_w + qkv_b
            q, kimg, vimg = jnp.split(qkv, 3, -1)

            def win(t):
                return t.reshape(n, NW, hw, NW, ww, c).transpose(0, 1, 3, 2, 4, 5).reshape(n, p2, hw, ww, c)
            qw, kw, vw = (win(q), win(kimg), win(vimg))
            q_win = qw.mean((2, 3))
            k_win = kw.mean((2, 3))
            logits = jnp.einsum('npc,nqc->npq', q_win * scale, k_win)
            _, r_idx = jax.lax.top_k(logits, TOPK)
            kv = jnp.concatenate([kw, vw], -1)
            kvp = kv.reshape(n, p2, KVW, hw // KVW, KVW, ww // KVW, 2 * c).mean((3, 5))
            kvp = kvp.reshape(n, p2, KVW * KVW, 2 * c)
            kv_sel = jax.vmap(lambda t, i: t[i])(kvp, r_idx)
            k_sel, v_sel = jnp.split(kv_sel, 2, -1)
            kt = TOPK * KVW * KVW
            k_sel = k_sel.reshape(n, p2, kt, HEADS, hd)
            v_sel = v_sel.reshape(n, p2, kt, HEADS, hd)
            qp = qw.reshape(n, p2, hw * ww, HEADS, hd)
            att = jax.nn.softmax(jnp.einsum('npqhc,npkhc->nphqk', qp * scale, k_sel), -1)
            out = jnp.einsum('nphqk,npkhc->npqhc', att, v_sel).reshape(n, p2, hw, ww, c)
            out = out.reshape(n, NW, NW, hw, ww, c).transpose(0, 1, 3, 2, 4, 5).reshape(n, h, w, c)
            lepe = _conv(vimg.transpose(0, 3, 1, 2), lepe_w, lepe_b, 2, groups=c).transpose(0, 2, 3, 1)
            return (out + lepe) @ wo_w + wo_b

        def _glu(y, fc1_w, fc1_b, pw_w, dw_w, dw_b, fc2_w, fc2_b):
            t = y @ fc1_w + fc1_b
            xh, vh = jnp.split(t, 2, -1)
            xh = xh.transpose(0, 3, 1, 2)
            xh = _conv(xh, pw_w, None, 0)
            xh = _conv(xh, dw_w, dw_b, 1, groups=dw_w.shape[0])
            xh = jax.nn.gelu(xh, approximate=False) * vh.transpose(0, 3, 1, 2)
            return xh.transpose(0, 2, 3, 1) @ fc2_w + fc2_b
        for i in range(D):
            x = x + _conv(x, pos_w[i], pos_b[i], 1, groups=x.shape[1])
            y = x.transpose(0, 2, 3, 1)
            y = y + _attn(_ln(y, ln1_g[i], ln1_b[i]), qkv_w[i], qkv_b[i], lepe_w[i], lepe_b[i], wo_w[i], wo_b[i])
            y = y + _glu(_ln(y, ln2_g[i], ln2_b[i]), fc1_w[i], fc1_b[i], pw_w[i], dw_w[i], dw_b[i], fc2_w[i], fc2_b[i])
            x = y.transpose(0, 3, 1, 2)
        return x

    def _L1_conv_ref(x, w1, gn_w, gn_b, w2, g1_w, g1_b, g2_w, g2_b, running_mean, running_var, residual_scale):
        import jax, jax.numpy as jnp
        import numpy as np
        B, C, H, W = (32, 64, 112, 112)
        HID, GROUPS = (128, 8)
        INNER_STEPS, INNER_LR, INNER_MOM = (3, 0.01, 0.9)
        GN_EPS = 1e-05

        def _gelu(v):
            return jax.nn.gelu(v, approximate=False)

        def _modifier(params, x):
            w1, gn_w, gn_b, w2 = params
            h = jnp.einsum('bchw,oc->bohw', x, w1)
            b, o, hh, ww = h.shape
            hg = h.reshape(b, GROUPS, o // GROUPS, hh, ww)
            mu = hg.mean(axis=(2, 3, 4), keepdims=True)
            var = hg.var(axis=(2, 3, 4), keepdims=True)
            hg = (hg - mu) * jax.lax.rsqrt(var + GN_EPS)
            h = hg.reshape(b, o, hh, ww) * gn_w[None, :, None, None] + gn_b[None, :, None, None]
            h = _gelu(h)
            return jnp.einsum('bohw,co->bchw', h, w2)

        def _surprise(y, rm, rv):
            n = y.shape[0] * y.shape[2] * y.shape[3]
            cm = y.mean(axis=(0, 2, 3))
            cv = ((y - cm[None, :, None, None]) ** 2).sum(axis=(0, 2, 3)) / (n - 1)
            return jnp.mean((cm - rm) ** 2) + jnp.mean((cv / (rv + 1e-08) - 1.0) ** 2)
        params0 = (w1, gn_w, gn_b, w2)
        feat = jax.lax.stop_gradient(x)
        loss_fn = lambda ps: _surprise(_modifier(ps, feat) + feat, running_mean, running_var)
        params = params0
        moms = jax.tree_util.tree_map(jnp.zeros_like, params0)
        for _ in range(INNER_STEPS - 1):
            grads = jax.grad(loss_fn)(params)
            moms = jax.tree_util.tree_map(lambda m, g: INNER_MOM * m + g, moms, grads)
            params = jax.tree_util.tree_map(lambda p, m: p - INNER_LR * m, params, moms)
        params_f = jax.tree_util.tree_map(lambda p0, p: p0 + jax.lax.stop_gradient(p - p0), params0, params)
        modification = _modifier(params_f, x)
        pooled = x.mean(axis=(2, 3))
        g = _gelu(pooled @ g1_w.T + g1_b)
        gate = jax.nn.sigmoid(g @ g2_w.T + g2_b)[:, :, None, None]
        return x + residual_scale * gate * modification

    def _gn(v, G=32, eps=1e-5):
        B_, C_, H_, W_ = v.shape
        g = v.reshape(B_, G, C_ // G, H_, W_)
        m = jnp.mean(g, axis=(2, 3, 4), keepdims=True)
        s = jnp.var(g, axis=(2, 3, 4), keepdims=True)
        return ((g - m) / jnp.sqrt(s + eps)).reshape(v.shape)

    def _ln_c(v, eps=1e-6):
        m = jnp.mean(v, axis=1, keepdims=True)
        s = jnp.var(v, axis=1, keepdims=True)
        return (v - m) / jnp.sqrt(s + eps)

    def _ln_t(v, eps=1e-5):
        m = jnp.mean(v, axis=-1, keepdims=True)
        s = jnp.var(v, axis=-1, keepdims=True)
        return (v - m) / jnp.sqrt(s + eps)

    def _to_tokens(v):
        B_, C_, H_, W_ = v.shape
        return v.reshape(B_, C_, H_ * W_).transpose(0, 2, 1)
    def _from_tokens(t, like):
        B_, C_, H_, W_ = like.shape
        return t.transpose(0, 2, 1).reshape(B_, C_, H_, W_)

    x = _L0_conv_ref(x, L0_conv_pos_w, L0_conv_pos_b, L0_conv_ln1_g, L0_conv_ln1_b, L0_conv_qkv_w, L0_conv_qkv_b, L0_conv_lepe_w, L0_conv_lepe_b, L0_conv_wo_w, L0_conv_wo_b, L0_conv_ln2_g, L0_conv_ln2_b, L0_conv_fc1_w, L0_conv_fc1_b, L0_conv_pw_w, L0_conv_dw_w, L0_conv_dw_b, L0_conv_fc2_w, L0_conv_fc2_b)
    x = _L1_conv_ref(x, L1_conv_w1, L1_conv_gn_w, L1_conv_gn_b, L1_conv_w2, L1_conv_g1_w, L1_conv_g1_b, L1_conv_g2_w, L1_conv_g2_b, L1_conv_running_mean, L1_conv_running_var, L1_conv_residual_scale)
    return x


_drawn_inputs = setup_inputs


def setup_inputs(seed=0):
    import zlib

    import numpy as np

    out = dict(_drawn_inputs(seed))
    spreads = {'L0_conv_pos_b': (0.0, 0.1),
     'L0_conv_ln1_g': (1.0, 0.6),
     'L0_conv_ln1_b': (0.0, 0.348),
     'L0_conv_qkv_b': (0.0, 0.1),
     'L0_conv_lepe_b': (0.0, 0.1),
     'L0_conv_wo_b': (0.0, 0.1),
     'L0_conv_ln2_g': (1.0, 0.6),
     'L0_conv_ln2_b': (0.0, 0.8),
     'L0_conv_fc1_b': (0.0, 0.8),
     'L0_conv_dw_b': (0.0, 0.444),
     'L0_conv_fc2_b': (0.0, 2.0),
     'L1_conv_gn_w': (1.0, 0.6),
     'L1_conv_gn_b': (0.0, 0.8),
     'L1_conv_g1_b': (0.0, 0.8),
     'L1_conv_running_mean': (0.0, 0.8),
     'L1_conv_running_var': (1.0, 0.6)}
    factors = {'L0_conv_fc1_w': 3.022,
     'L0_conv_pw_w': 8.0,
     'L0_conv_dw_w': 8.0,
     'L0_conv_fc2_w': 3.047,
     'L1_conv_w1': 4.078,
     'L1_conv_w2': 3.502,
     'L1_conv_g1_w': 8.0,
     'L1_conv_g2_w': 8.0}
    for name, (base, spread) in spreads.items():
        noise = np.random.default_rng([zlib.crc32(name.encode()), seed]).standard_normal(out[name].shape)
        drawn = base * np.exp(spread * noise) if base else spread * noise
        out[name] = jnp.asarray(drawn.astype(out[name].dtype))
    for name, factor in factors.items():
        out[name] = (out[name] * factor).astype(out[name].dtype)
    return out
```

```python
import numpy as np
import concourse.bass as bass
from concourse import mybir
from contextlib import ExitStack

N, C, H, W, D = 2, 64, 256, 256, 2
P = 128
RP = H // 2
SRP = 4
STRIPS = RP // SRP
UNIT = 2
UNITS = SRP // UNIT
COLS = UNIT * W
PADW = W + 4
HEADS, TOPK, SUB, NW = 8, 4, 16, 8
WINDOWS = NW * NW
WRP, WW = RP // NW, W // NW
WPIX = WRP * WW
KEYS = TOPK * SUB
LN_EPS, GN_EPS = 1e-6, 1e-5
HID, GROUP = 128, 16
PIX = H * W
TINY = 1e-30
INV_SQRT_2PI = 0.3989422804014327
DEVIATION_MAX = (3.4028234e38 / (GROUP * PIX)) ** 0.5
LR, MOM, STEPS = 0.01, 0.9, 2

fp32 = mybir.dt.float32
u32 = mybir.dt.uint32
ALU = mybir.AluOpType
ACT = mybir.ActivationFunctionType
AX = mybir.AxisListType


def constants():
    p = np.arange(P)
    eye = np.eye(P)
    half = (p[:, None] // 64 == p[None, :] // 64)
    col = np.arange(512)
    parts = {
        "ident": eye,
        "ident2": np.vstack([np.eye(64)] * 2),
        "center": eye - half / 64.0,
        "mean": half / 64.0,
        "pairmean": np.vstack([np.eye(64)] * 2) / 64.0,
        "group": (p[:, None] // GROUP == p[None, :] // GROUP) * 1.0,
        "headmask": np.vstack([(p[:64, None] // 8 == col[None, :] // 64)] * 2) * 1.0,
        "vmask": (col[None, :256] % 64 // 8 == 2 * (col[None, :256] // 64) + p[:, None] // 64) * 1.0,
        "expand": 16.0 * (p[:, None] == (p[None, :] // SUB) % TOPK) + (p[:, None] == 8) * (p[None, :] % SUB),
        "pair": np.tile(np.eye(64), (2, 2)),
        "eps": np.full((P, 1), LN_EPS),
        "tiny": np.full((P, 1), TINY),
        "minus": -1.0 * (p[:, None] - 64 == col[None, :] // 64),
    }
    at, n = {}, 0
    for name, a in parts.items():
        at[name] = (n, n + a.shape[1])
        n += a.shape[1]
    return np.ascontiguousarray(np.hstack(list(parts.values())).astype(np.float32)), at


def build(nc, I, out):
    ctx = ExitStack()
    with ctx:
        build_in(nc, I, out, ctx)


class Link:

    def __init__(self, nc, sem, eng):
        self.sem, self.eng, self.n = sem, eng, 0

    def __call__(self, ins):
        ins.then_inc(self.sem, 1)
        self.n += 1
        self.eng.wait_ge(self.sem, self.n)


def build_in(nc, I, out, ctx):
    _, at = constants()

    def sem(name):
        return ctx.enter_context(nc.semaphore(name))

    def dram(name, shape):
        return nc.dram_tensor(name, shape, fp32, kind="Internal").ap()

    taken = {}

    def fresh(name):
        taken[name] = taken.get(name, 0) + 1
        return f"{name}_{taken[name]}"

    def sbt(c, name, shape, dt=fp32):
        return c.enter_context(nc.sbuf_tensor(fresh(name), shape, dt))

    def pst(c, name, shape):
        return c.enter_context(nc.psum_tensor(fresh(name), shape, fp32))

    def clear(*sems, start={}):
        with nc.Block() as reset:
            @reset.gpsimd
            def _(pool):
                for s in sems:
                    pool.sem_clear(s)
                for s, v in start.items():
                    pool.sem_inc(s, v)

    IMG = dram("IMG", [D + 1, N, P, RP + 2, W])
    X1 = dram("X1", [N, P, RP, W])
    XH = dram("XH", [N, P, RP + 2, W])
    AO = dram("AO", [N, P, RP, W])
    X2 = dram("X2", [N, P, RP, W])
    XH2 = dram("XH2", [N, P, RP + 2, W])
    POOL = dram("POOL", [N, P, STRIPS, W // 8])
    TAB = [dram(f"TAB{n}", [WINDOWS * SUB, P]) for n in range(N)]
    IDX = nc.dram_tensor("IDX", [N, WINDOWS, P], u32, kind="Internal").ap()
    AW = dram("AW", [N, WINDOWS, 64, 512])
    VW = dram("VW", [N, WINDOWS, P, 256])
    STAT = dram("STAT", [N, P, STRIPS, UNITS * 6])

    cst = sbt(ctx, "cst", [P, I["cst"].shape[1]])

    def c(name, p0=0, p1=P):
        return cst[p0:p1, at[name][0]:at[name][1]]

    ident = c("ident")
    s_init = sem("s_init")

    with ExitStack() as ph:
        zero = sbt(ph, "zero", [P, W])
        zeroed = sem("zeroed")
        with nc.Block() as block:
            @block.vector
            def _(dve):
                nc.vector.memset(zero[:, :], 0.0).then_inc(zeroed, 1)

            @block.sync
            def _(sp):
                k = 1
                sp.dma_start(cst[:, :], I["cst"]).then_inc(s_init, 16)
                xv = I["x"].rearrange("n c (r p) w -> n p c r w", p=2)
                for n in range(N):
                    for p in range(2):
                        sp.dma_start(IMG[0, n, 64 * p:64 * p + 64, 1:RP + 1, :], xv[n, p]).then_inc(s_init, 16)
                        k += 1
                sp.wait_ge(zeroed, 1)
                for n in range(N):
                    for a in [IMG[d, n] for d in range(D + 1)] + [XH[n], XH2[n]]:
                        for r in (0, RP + 1):
                            sp.dma_start(a[:, r, :], zero[:, :]).then_inc(s_init, 16)
                            k += 1
                sp.wait_ge(s_init, 16 * k)

    layer0(nc, I, sem, sbt, pst, clear, c, IMG, X1, XH, AO, X2, XH2, POOL, TAB, IDX, AW, VW)
    layer1(nc, I, sem, sbt, pst, clear, c, IMG, STAT, out)


def layer0(nc, I, sem, sbt, pst, clear, c, IMG, X1, XH, AO, X2, XH2, POOL, TAB, IDX, AW, VW):
    ident = c("ident")
    ctx = ExitStack()
    ctx.__enter__()
    posm = sbt(ctx, "posm", [P, 2, 3, P])
    posb = sbt(ctx, "posb", [P, 1])
    lepm = sbt(ctx, "lepm", [P, 3, 5, P])
    glum = sbt(ctx, "glum", [P, 2, 2, 3, HID])
    wn = sbt(ctx, "wn", [P, 448])
    wt = sbt(ctx, "wt", [P, 5, 2, 64])
    wod = sbt(ctx, "wod", [P, P])
    attb = sbt(ctx, "attb", [P, 1])
    fc2 = sbt(ctx, "fc2", [HID, 64])
    fc2b = sbt(ctx, "fc2b", [P, 1])
    dwb = sbt(ctx, "dwb", [HID, 1])
    w_loaded, link = sem("w_loaded"), sem("link")
    S = {k: sem(k) for k in """in_loaded0 in_loaded1 out_stored0 out_stored1
        conv_done x_ready centred squared var_done sd_ready rstd_ready xhat_ready plus_ready pooled_ready
        scored max_ready max_turned max_copied shifted probs_ready av_done recip_ready attn_ready
        idx_loaded0 idx_loaded1 rows_known k_turned k_masked a_done a_copied v_masked
        xbranch_done vbranch_done gelu_ready gated fc2_done out_ready""".split()}
    gathered = [sem(f"gathered{n}") for n in range(N)]
    allsems = [w_loaded, link, *S.values()]

    with nc.Fori(0, D) as d:
        weights(nc, I, d, sbt, pst, clear, c, w_loaded, link, allsems,
                posm, posb, lepm, glum, wn, wt, wod, attb, fc2, fc2b, dwb)
        positional(nc, d, sbt, pst, clear, c, S, allsems, posm, posb, IMG, X1, XH, POOL)
        for n in range(N):
            routing(nc, n, sbt, pst, clear, c, w_loaded, link, wn, POOL, TAB, IDX)
        matrices(nc, d, sbt, pst, clear, c, S, allsems, gathered, wt, TAB, IDX, AW, VW)
        attention(nc, sbt, pst, clear, c, S, allsems, XH, AW, VW, AO)
        mixing(nc, sbt, pst, clear, c, S, allsems, lepm, wod, attb, XH, AO, X1, X2, XH2)
        glu(nc, d, sbt, pst, clear, c, S, allsems, glum, wn, fc2, fc2b, dwb, XH2, X2, IMG)
    ctx.close()


def weights(nc, I, d, sbt, pst, clear, c, w_loaded, link, allsems,
            posm, posb, lepm, glum, wn, wt, wod, attb, fc2, fc2b, dwb):
    ident = c("ident")
    MS = [64, 64, 64, 128, 128]
    AT = [0, 64, 128, 192, 320]
    clear(*allsems)
    with ExitStack() as ph:
        raw = sbt(ph, "raw", [64, 448])
        wg = sbt(ph, "wg", [64, 448])
        lng = sbt(ph, "lng", [64, 2])
        lnb = sbt(ph, "lnb", [64, 2])
        bias = sbt(ph, "bias", [P, 5])
        sh = sbt(ph, "sh", [P, 5])
        rs = sbt(ph, "rs", [P, 5])
        posw = sbt(ph, "posw", [P, 9])
        lepw = sbt(ph, "lepw", [64, 25])
        lepb = sbt(ph, "lepb", [64, 1])
        wo2 = sbt(ph, "wo2", [64, 2, 64])
        wob = sbt(ph, "wob", [P, 1])
        lrhs = sbt(ph, "lrhs", [64, 32, 64])
        lt = sbt(ph, "lt", [P, 32, 64])
        pw = sbt(ph, "pw", [P, P])
        pwt = sbt(ph, "pwt", [P, P])
        wpt = sbt(ph, "wpt", [P, P])
        dw = sbt(ph, "dw", [P, 9])
        dwd = sbt(ph, "dwd", [P, 9, P])
        w9 = sbt(ph, "w9", [P, 9, P])
        ps = pst(ph, "ps_w", [P, 8, 512])

        with nc.Block() as load:
            @load.gpsimd
            def _(pool):
                pool.memset(wod[:, :], 0.0).then_inc(link, 1)
                pool.memset(posm[:, :, :, :], 0.0)
                pool.memset(lepm[:, :, :, :], 0.0)
                pool.memset(glum[:, :, :, :, :], 0.0)
                pool.memset(lrhs[:, :, :], 0.0)
                pool.memset(bias[:, :], 0.0)
                pool.memset(sh[:, :], 0.0)
                pool.memset(wt[:, :, :, :], 0.0).then_inc(link, 1)

            @load.sync
            def _(sp):
                k = [0]

                def get(dst, src):
                    sp.dma_start(dst, src).then_inc(w_loaded, 16)
                    k[0] += 1

                def column(name, a=0, b=None):
                    v = I[name][d, a:b] if b else I[name][d]
                    return v.rearrange("(c o) -> c o", o=1)

                get(raw[:, 0:192], I["qkv_w"][d])
                get(raw[:, 192:448], I["fc1_w"][d])
                for i in range(2):
                    get(lng[:, i:i + 1], column(f"ln{i + 1}_g"))
                    get(lnb[:, i:i + 1], column(f"ln{i + 1}_b"))
                get(lepw[:, :], I["lepe_w"][d].rearrange("c o a b -> c (o a b)"))
                get(lepb[:, :], column("lepe_b"))
                get(pw[:, :], I["pw_w"][d].rearrange("o i a b -> o (i a b)"))
                get(dw[:, :], I["dw_w"][d].rearrange("c o a b -> c (o a b)"))
                get(dwb[:, :], column("dw_b"))
                get(fc2[:, :], I["fc2_w"][d])
                for h in range(2):
                    hp = slice(64 * h, 64 * h + 64)
                    get(posw[hp, :], I["pos_w"][d].rearrange("c o a b -> c (o a b)"))
                    get(posb[hp, :], column("pos_b"))
                    get(wob[hp, :], column("wo_b"))
                    get(fc2b[hp, :], column("fc2_b"))
                    get(wo2[:, h, :], I["wo_w"][d])
                sp.wait_ge(link, 2)
                for h in range(2):
                    hp = slice(64 * h, 64 * h + 64)
                    get(wod[hp, 64 * h:64 * h + 64], I["wo_w"][d])
                for i in range(5):
                    src = column("qkv_b", AT[i], AT[i] + 64) if i < 3 else column("fc1_b", 128 * (i - 3), 128 * (i - 2))
                    get(bias[0:MS[i], i:i + 1], src)
                sp.wait_ge(w_loaded, 16 * k[0])

        clear(link)
        with nc.Block() as fold:
            @fold.vector
            def _(dve):
                step = Link(nc, link, dve)
                nc.vector.tensor_scalar(wg[:, 0:192], raw[:, 0:192], lng[:, 0:1], None, ALU.mult)
                nc.vector.tensor_scalar(wg[:, 192:448], raw[:, 192:448], lng[:, 1:2], None, ALU.mult)
                nc.vector.tensor_tensor(lrhs[:, 0:25, :], wo2[:, 0:1, :].to_broadcast([64, 25, 64]),
                                        lepw[:, :, None].to_broadcast([64, 25, 64]), ALU.mult)
                nc.vector.tensor_tensor(dwd[:, :, :], ident[:, None, :].to_broadcast([P, 9, P]),
                                        dw[:, :, None].to_broadcast([P, 9, P]), ALU.mult)
                step(nc.vector.tensor_scalar_add(posw[:, 4:5], posw[:, 4:5], 1.0))
                for j in range(2):
                    hp = slice(64 * j, 64 * j + 64)
                    for g in range(2):
                        for par in range(2):
                            t = 2 * g + j - par
                            if 0 <= t < 3:
                                nc.vector.tensor_tensor(
                                    posm[hp, g, :, 64 * par:64 * par + 64],
                                    c("ident2")[hp, None, :].to_broadcast([64, 3, 64]),
                                    posw[hp, 3 * t:3 * t + 3, None].to_broadcast([64, 3, 64]), ALU.mult)

        with nc.Block() as turn:
            @turn.tensor
            def _(pe):
                for i in range(5):
                    w = slice(AT[i], AT[i] + MS[i])
                    nc.tensor.transpose(ps[0:MS[i], 0, 64 * i:64 * i + 64], wg[:, w], ident[0:64, 0:64])
                    nc.tensor.matmul(ps[0:MS[i], 1, i:i + 1], raw[:, w], lnb[:, (i > 2):(i > 2) + 1],
                                     start=True, stop=True)
                nc.tensor.matmul(ps[:, 2, 0:1], wo2[:, :, :].rearrange("c a o -> c (a o)"), lepb[:, :],
                                 start=True, stop=True)
                nc.tensor.transpose(ps[:, 3, 0:P], pw[:, :], ident)

        clear(link)
        with nc.Block() as tilde:
            @tilde.vector
            def _(dve):
                step = Link(nc, link, dve)
                nc.vector.tensor_copy(pwt[:, :], ps[:, 3, 0:P])
                nc.vector.tensor_tensor(attb[:, :], ps[:, 2, 0:1], wob[:, :], ALU.add)
                for i in range(5):
                    m = slice(0, MS[i])
                    step(nc.vector.reduce_sum(rs[m, i:i + 1], ps[m, 0, 64 * i:64 * i + 64], AX.X))
                    step(nc.vector.tensor_tensor(sh[m, i:i + 1], ps[m, 1, i:i + 1], rs[m, i:i + 1], ALU.subtract))
                    step(nc.vector.tensor_tensor(sh[m, i:i + 1], sh[m, i:i + 1], bias[m, i:i + 1], ALU.add))
                    step(nc.vector.tensor_scalar_mul(sh[m, i:i + 1], sh[m, i:i + 1], 1.0 / C))
                    for b in range(2):
                        nc.vector.tensor_scalar(wt[m, i, b, :], ps[m, 0, 64 * i:64 * i + 64], sh[m, i:i + 1],
                                                C ** -0.5 if i == 0 else 1.0, ALU.add, ALU.mult)

        with nc.Block() as back:
            @back.tensor
            def _(pe):
                for i in range(5):
                    nc.tensor.transpose(ps[:, 0, AT[i]:AT[i] + MS[i]],
                                        wt[0:MS[i], i, :, :].rearrange("m a c -> m (a c)"), ident[0:MS[i], 0:MS[i]])
                for q in range(4):
                    nc.tensor.matmul(ps[:, 1 + q, :], wt[0:64, 2, :, :].rearrange("m a c -> m (a c)"),
                                     lrhs[:, 8 * q:8 * q + 8, :].rearrange("c t o -> c (t o)"), start=True, stop=True)
                nc.tensor.matmul(ps[:, 5, 0:P], pwt[:, :], wt[:, 3, :, :].rearrange("m a c -> m (a c)"),
                                 start=True, stop=True)

        with nc.Block() as keep:
            @keep.vector
            def _(dve):
                nc.vector.tensor_copy(wn[:, :], ps[:, 0, 0:448])
                nc.vector.tensor_copy(wpt[:, :], ps[:, 5, 0:P])

            @keep.scalar
            def _(act):
                for q in range(4):
                    nc.scalar.copy(lt[:, 8 * q:8 * q + 8, :], ps[:, 1 + q, :].rearrange("p (t o) -> p t o", t=8))

        with nc.Block() as taps:
            @taps.tensor
            def _(pe):
                for t in range(3):
                    nc.tensor.matmul(ps[:, t, 0:384], wpt[:, :],
                                     dwd[:, 3 * t:3 * t + 3, :].rearrange("p t o -> p (t o)"), start=True, stop=True)

            @taps.vector
            def _(dve):
                for j in range(2):
                    hp = slice(64 * j, 64 * j + 64)
                    for g in range(3):
                        for par in range(2):
                            t = 2 * g + j - par
                            if 0 <= t < 5:
                                nc.vector.tensor_copy(lepm[hp, g, :, 64 * par:64 * par + 64],
                                                      lt[hp, 5 * t:5 * t + 5, :])

        with nc.Block() as place:
            @place.vector
            def _(dve):
                for j in range(2):
                    hp = slice(64 * j, 64 * j + 64)
                    for par in range(2):
                        for gi in range(2):
                            t = 2 * (gi - 1 + par) + j - par + 1
                            if 0 <= t < 3:
                                nc.vector.tensor_copy(glum[hp, par, gi, :, :],
                                                      ps[hp, t, 0:384].rearrange("p (x o) -> p x o", x=3))


BODY = N * UNITS
DONE, FREE, LAST = BODY + 1, BODY - 1, UNITS
UNIT_SEMS = "rstd_ready conv_done x_ready centred squared var_done sd_ready xhat_ready plus_ready fc2_done out_ready".split()


def first_unit(s, n):
    return s * BODY + n * UNITS


def run_strips(sp, load, store):
    for n in range(N):
        load(0, n)
    with sp.Fori(0, STRIPS - 1) as s:
        for n in range(N):
            load(s + 1, n)
            store(s, n)
    for n in range(N):
        store(STRIPS - 1, n)


def rows(t, n, k):
    return t[:, n, UNIT * k:UNIT * k + UNIT, :]


def as_rows(a):
    return a.rearrange("p (r w) -> p r w", w=W)


def norm_on_pe(nc, pe, c, S, u, x, sq, pc, pv, n, k, step):
    if step == "centre":
        pe.wait_ge(S["x_ready"], u + DONE)
        pe.wait_ge(S["xhat_ready"], u + FREE)
        nc.tensor.matmul(pc[:, k % 2, :], c("center"), rows(x, n, k), start=True, stop=True).then_inc(S["centred"], 1)
    else:
        pe.wait_ge(S["squared"], u + DONE)
        pe.wait_ge(S["sd_ready"], u + FREE)
        nc.tensor.matmul(pv[:, k % 2, :], c("mean"), sq[:, k % 2, :], start=True, stop=True).then_inc(S["var_done"], 1)


def norm_on_dve(nc, dve, S, u, k, sd, rstd, xr, pc):
    dve.wait_ge(S["sd_ready"], u + DONE)
    dve.wait_ge(S["plus_ready"], u + FREE)
    nc.vector.reciprocal(rstd[:, k % 2, :], sd[:, k % 2, :]).then_inc(S["rstd_ready"], 1)
    dve.wait_ge(S["rstd_ready"], u + DONE)
    nc.vector.tensor_tensor(xr[:, k % 2, :], pc[:, k % 2, :], rstd[:, k % 2, :], ALU.mult).then_inc(S["xhat_ready"], 1)


def sqrt_on_act(nc, act, S, u, k, sd, pv, eps):
    act.wait_ge(S["var_done"], u + DONE)
    act.wait_ge(S["xhat_ready"], u + FREE)
    nc.scalar.activation(sd[:, k % 2, :], pv[:, k % 2, :], ACT.Sqrt, bias=eps).then_inc(S["sd_ready"], 1)


def square_on_act(nc, act, S, u, k, sq, pc):
    act.wait_ge(S["centred"], u + DONE)
    act.wait_ge(S["var_done"], u + FREE)
    nc.scalar.activation(sq[:, k % 2, :], pc[:, k % 2, :], ACT.Square).then_inc(S["squared"], 1)


def plus_on_act(nc, act, S, u, k, n, xr, xh):
    act.wait_ge(S["xhat_ready"], u + DONE)
    nc.scalar.add(rows(xh, n, k), as_rows(xr[:, k % 2, :]), 1.0).then_inc(S["plus_ready"], 1)


def positional(nc, d, sbt, pst, clear, c, S, allsems, posm, posb, IMG, X1, XH, POOL):
    clear(*allsems, start={**{S[k]: BODY for k in UNIT_SEMS}, S["out_stored0"]: 48, S["out_stored1"]: 48})
    with ExitStack() as ph:
        xs = sbt(ph, "p_xs", [P, N, SRP + 1, PADW])
        x1 = sbt(ph, "p_x1", [P, N, SRP, W])
        sq = sbt(ph, "p_sq", [P, 2, COLS])
        sd = sbt(ph, "p_sd", [P, 2, COLS])
        rstd = sbt(ph, "p_rstd", [P, 2, COLS])
        xr = sbt(ph, "p_xr", [P, 2, COLS])
        xh = sbt(ph, "p_xh", [P, N, SRP, W])
        pooled = sbt(ph, "p_pool", [P, N, W // 8])
        px = pst(ph, "ps_x", [P, 2, COLS])
        pc = pst(ph, "ps_c", [P, 2, COLS])
        pv = pst(ph, "ps_v", [P, 2, COLS])
        with nc.Block() as border:
            @border.vector
            def _(dve):
                nc.vector.memset(xs[:, :, :, 0:2], 0.0)
                nc.vector.memset(xs[:, :, :, PADW - 2:PADW], 0.0)

        with nc.Block() as block:
            @block.sync
            def _(sp):
                def load(s, n):
                    sp.wait_ge(S["conv_done"], first_unit(s, n) + LAST)
                    for j in range(2):
                        sp.dma_start(xs[64 * j:64 * j + 64, n, :, 2:2 + W],
                                     IMG[d, n, 64 - 64 * j:128 - 64 * j, bass.ds(s * SRP + j, SRP + 1), :]
                                     ).then_inc(S[f"in_loaded{n}"], 16)

                def store(s, n):
                    sp.wait_ge(S["x_ready"], first_unit(s, n) + UNITS - 1 + DONE)
                    sp.dma_start(X1[n, :, bass.ds(s * SRP, SRP), :], x1[:, n, :, :]).then_inc(S[f"out_stored{n}"], 16)
                    sp.wait_ge(S["plus_ready"], first_unit(s, n) + UNITS - 1 + DONE)
                    sp.dma_start(XH[n, :, bass.ds(s * SRP + 1, SRP), :], xh[:, n, :, :]).then_inc(S[f"out_stored{n}"], 16)
                    sp.wait_ge(S["pooled_ready"], s * N + n + 1)
                    sp.dma_start(POOL[n, :, s, :], pooled[:, n, :]).then_inc(S[f"out_stored{n}"], 16)

                run_strips(sp, load, store)
                for n in range(N):
                    sp.wait_ge(S[f"out_stored{n}"], 48 * (STRIPS + 1))

            @block.tensor
            def _(pe):
                def conv(s, n, k):
                    u = first_unit(s, n) + k
                    if k == 0:
                        pe.wait_ge(S[f"in_loaded{n}"], s * 32 + 32)
                    pe.wait_ge(S["x_ready"], u + FREE)
                    for g in range(2):
                        for dx in range(3):
                            mm = nc.tensor.matmul(px[:, k % 2, :], posm[:, g, dx, :],
                                                  xs[:, n, UNIT * k + g:UNIT * k + g + UNIT, 1 + dx:1 + dx + W],
                                                  start=(g + dx == 0), stop=(g == 1 and dx == 2))
                    mm.then_inc(S["conv_done"], 1)

                with pe.Fori(0, STRIPS) as s:
                    for i in range(BODY + 2):
                        if i < BODY:
                            conv(s, i // UNITS, i % UNITS)
                        for back, step in ((1, "centre"), (2, "var")):
                            if 0 <= i - back < BODY:
                                n, k = divmod(i - back, UNITS)
                                norm_on_pe(nc, pe, c, S, first_unit(s, n) + k, x1, sq, pc, pv, n, k, step)

            @block.scalar
            def _(act):
                with act.Fori(0, STRIPS) as s:
                    for i in range(BODY + 3):
                        if i < BODY:
                            n, k = divmod(i, UNITS)
                            u = first_unit(s, n) + k
                            act.wait_ge(S["conv_done"], u + DONE)
                            if k == 0:
                                act.wait_ge(S[f"out_stored{n}"], s * 48 + 48)
                            nc.scalar.activation(rows(x1, n, k), as_rows(px[:, k % 2, :]), ACT.Identity,
                                                 bias=posb[:, 0:1]).then_inc(S["x_ready"], 1)
                        if 0 <= i - 1 < BODY:
                            n, k = divmod(i - 1, UNITS)
                            square_on_act(nc, act, S, first_unit(s, n) + k, k, sq, pc)
                        if 0 <= i - 2 < BODY:
                            n, k = divmod(i - 2, UNITS)
                            sqrt_on_act(nc, act, S, first_unit(s, n) + k, k, sd, pv, c("eps"))
                        if 0 <= i - 3 < BODY:
                            n, k = divmod(i - 3, UNITS)
                            plus_on_act(nc, act, S, first_unit(s, n) + k, k, n, xr, xh)

            @block.vector
            def _(dve):
                with dve.Fori(0, STRIPS) as s:
                    for n in range(N):
                        for k in range(UNITS):
                            norm_on_dve(nc, dve, S, first_unit(s, n) + k, k, sd, rstd, xr, pc)
                    for n in range(N):
                        dve.wait_ge(S["plus_ready"], first_unit(s, n) + UNITS - 1 + DONE)
                        dve.wait_ge(S[f"out_stored{n}"], s * 48 + 48)
                        nc.vector.tensor_reduce(pooled[:, n, :], xh[:, n, :, :].rearrange("p r (b x) -> p b r x", x=8),
                                                AX.XY, ALU.add).then_inc(S["pooled_ready"], 1)



def routing(nc, n, sbt, pst, clear, c, w_loaded, link, wn, POOL, TAB, IDX):
    ident = c("ident")
    with ExitStack() as ph:
        sums = sbt(ph, "r_sums", [P, 1024])
        pm = sbt(ph, "r_pm", [64, WINDOWS, SUB])
        win = sbt(ph, "r_win", [64, WINDOWS])
        tab = sbt(ph, "r_tab", [P, 8, P])
        qk = sbt(ph, "r_qk", [64, 2, WINDOWS])
        lg = sbt(ph, "r_lg", [64, WINDOWS])
        top = sbt(ph, "r_top", [64, 8])
        best = sbt(ph, "r_best", [64, 8], u32)
        bestf = sbt(ph, "r_bestf", [64, 8])
        bt = sbt(ph, "r_bt", [P, WINDOWS])
        idx = sbt(ph, "r_idx", [WINDOWS, P], u32)
        ps = pst(ph, "ps_r", [P, 8, 512])
        clear(w_loaded)
        with nc.Block() as load:
            @load.sync
            def _(sp):
                sp.dma_start(sums[:, :], POOL[n].rearrange("p s b -> p (s b)")).then_inc(w_loaded, 16)
                sp.wait_ge(w_loaded, 16)

            @load.gpsimd
            def _(pool):
                pool.memset(bt[:, :], 1.0)
        with nc.Block() as mean:
            @mean.tensor
            def _(pe):
                for h in range(2):
                    nc.tensor.matmul(ps[0:64, h, :], c("pairmean"), sums[:, 512 * h:512 * h + 512], start=True, stop=True)
        clear(link)
        with nc.Block() as sort:
            @sort.vector
            def _(dve):
                step = Link(nc, link, dve)
                for wy in range(NW):
                    src = ps[0:64, wy // 4, 128 * (wy % 4):128 * (wy % 4) + 128]
                    ins = nc.vector.tensor_copy(
                        pm[:, NW * wy:NW * wy + NW, :].rearrange("c w (y x) -> c w y x", x=4),
                        src.rearrange("c (y w x) -> c w y x", y=4, x=4))
                    step(ins)
                step(nc.vector.reduce_sum(win[:, :], pm[:, :, :], AX.X))
                nc.vector.tensor_scalar_mul(win[:, :], win[:, :], 1.0 / SUB)
        with nc.Block() as project:
            @project.tensor
            def _(pe):
                rows_of = pm[:, :, :].rearrange("c w s -> c (w s)")
                for i in range(8):
                    nc.tensor.matmul(ps[:, i // 4, P * (i % 4):P * (i % 4) + P], rows_of[:, P * i:P * i + P],
                                     wn[0:64, 64:192], start=True, stop=True)
                for i in range(2):
                    nc.tensor.matmul(ps[0:64, 2 + i, 0:WINDOWS], wn[0:64, 64 * i:64 * i + 64], win[:, :],
                                     start=True, stop=True)
        clear(w_loaded)
        with nc.Block() as keep:
            @keep.vector
            def _(dve):
                for i in range(2):
                    nc.vector.tensor_copy(tab[:, 4 * i:4 * i + 4, :], ps[:, i, :].rearrange("p (t c) -> p t c", t=4))
                    nc.vector.tensor_copy(qk[:, i, :], ps[0:64, 2 + i, 0:WINDOWS])
        with nc.Block() as logits:
            @logits.sync
            def _(sp):
                sp.dma_start(TAB[n].rearrange("(t p) c -> p t c", p=P), tab[:, :, :]).then_inc(w_loaded, 16)
                sp.wait_ge(w_loaded, 16)

            @logits.tensor
            def _(pe):
                nc.tensor.matmul(ps[0:64, 4, 0:WINDOWS], qk[:, 0, :], qk[:, 1, :], start=True, stop=True)
        clear(link)
        with nc.Block() as choose:
            @choose.vector
            def _(dve):
                step = Link(nc, link, dve)
                step(nc.vector.tensor_copy(lg[:, :], ps[0:64, 4, 0:WINDOWS]))
                step(nc.vector.max(top[:, :], lg[:, :]))
                step(nc.vector.max_index(best[:, :], top[:, :], lg[:, :]))
                nc.vector.tensor_copy(bestf[:, :], best[:, :])
        with nc.Block() as turn:
            @turn.tensor
            def _(pe):
                nc.tensor.transpose(ps[0:8, 5, 0:64], bestf[:, :], ident[0:64, 0:64])
        with nc.Block() as keep_turned:
            @keep_turned.vector
            def _(dve):
                nc.vector.tensor_copy(bt[0:8, :], ps[0:8, 5, 0:64])
        with nc.Block() as expand:
            @expand.tensor
            def _(pe):
                nc.tensor.matmul(ps[0:WINDOWS, 6, 0:P], bt[:, :], c("expand"), start=True, stop=True)
        with nc.Block() as number:
            @number.vector
            def _(dve):
                nc.vector.tensor_copy(idx[:, :], ps[0:WINDOWS, 6, 0:P])
        clear(w_loaded)
        with nc.Block() as store:
            @store.sync
            def _(sp):
                sp.dma_start(IDX[n], idx[:, :]).then_inc(w_loaded, 16)
                sp.wait_ge(w_loaded, 16)


def matrices(nc, d, sbt, pst, clear, c, S, allsems, gathered, wt, TAB, IDX, AW, VW):
    per_window = "k_turned k_masked a_done a_copied v_masked".split()
    clear(*allsems, start={**{S[k]: N for k in per_window},
                           **{S[f"out_stored{n}"]: 32 for n in range(N)}})
    with ExitStack() as ph:
        idc = sbt(ph, "m_idc", [P, N, 1], u32)
        kv = [sbt(ph, f"m_kv{n}", [P, P]) for n in range(N)]
        kb = sbt(ph, "m_kb", [64, N, 512])
        aw = sbt(ph, "m_aw", [64, N, 512])
        vw = sbt(ph, "m_vw", [P, N, 4, 64])
        pk = pst(ph, "ps_k", [P, N, 512])
        pa = pst(ph, "ps_a", [P, N, 512])
        idx1 = [sbt(ph, f"m_idx{n}", [P, 1], u32) for n in range(N)]

        with nc.Block() as block:
            @block.sync
            def _(sp):
                with sp.Fori(0, WINDOWS) as w:
                    for n in range(N):
                        sp.wait_ge(S["k_turned"], w * N + n + 1)
                        sp.dma_start(idx1[n][:, :], IDX[n, w].rearrange("(p o) -> p o", o=1)).then_inc(S[f"idx_loaded{n}"], 16)

            @block.gpsimd
            def _(pool):
                with pool.Fori(0, WINDOWS) as w:
                    for n in range(N):
                        pool.wait_ge(S["v_masked"], w * N + n + 1)
                        pool.wait_ge(S["k_turned"], w * N + n + 1)
                        pool.wait_ge(S[f"idx_loaded{n}"], w * 16 + 16)
                        pool.sem_inc(S["rows_known"], 1)
                        pool.indirect_dma_start(kv[n][:, :], None, TAB[n],
                                                bass.IndirectOffsetOnAxis(ap=idx1[n][:, 0:1], axis=0)
                                                ).then_inc(gathered[n], 16)

            @block.tensor
            def _(pe):
                with pe.Fori(0, WINDOWS) as w:
                    for n in range(N):
                        pe.wait_ge(gathered[n], (d * WINDOWS + w) * 16 + 16)
                        pe.wait_ge(S["k_masked"], w * N + n + 1)
                        nc.tensor.transpose(pk[:, n, 0:P], kv[n][:, :], c("ident")).then_inc(S["k_turned"], 1)
                    for n in range(N):
                        pe.wait_ge(S["k_masked"], w * N + n + 1 + N)
                        pe.wait_ge(S["a_copied"], w * N + n + 1)
                        nc.tensor.matmul(pa[:, n, :], wt[0:64, 0, :, :].rearrange("m a c -> m (a c)"), kb[:, n, :], start=True, stop=True
                                         ).then_inc(S["a_done"], 1)

            @block.vector
            def _(dve):
                with dve.Fori(0, WINDOWS) as w:
                    for n in range(N):
                        dve.wait_ge(S["k_turned"], w * N + n + 1 + N)
                        dve.wait_ge(S["a_done"], w * N + n + 1)
                        nc.vector.tensor_tensor(kb[:, n, :].rearrange("c (h k) -> c h k", h=HEADS),
                                                pk[0:64, n, None, 0:64].to_broadcast([64, HEADS, 64]),
                                                c("headmask", 0, 64).rearrange("c (h k) -> c h k", h=HEADS), ALU.mult
                                                ).then_inc(S["k_masked"], 1)
                    for n in range(N):
                        dve.wait_ge(gathered[n], (d * WINDOWS + w) * 16 + 16)
                        dve.wait_ge(S[f"out_stored{n}"], w * 32 + 32)
                        nc.vector.tensor_tensor(vw[:, n, :, :], kv[n][:, None, 64:128].to_broadcast([P, 4, 64]),
                                                c("vmask").rearrange("p (j c) -> p j c", j=4), ALU.mult
                                                ).then_inc(S["v_masked"], 1)

            @block.scalar
            def _(act):
                with act.Fori(0, WINDOWS) as w:
                    for n in range(N):
                        act.wait_ge(S["a_done"], w * N + n + 1 + N)
                        act.wait_ge(S[f"out_stored{n}"], w * 32 + 32)
                        nc.scalar.copy(aw[:, n, :], pa[0:64, n, :]).then_inc(S["a_copied"], 1)
                        act.wait_ge(S["a_copied"], w * N + n + 1 + N)
                        act.dma_start(AW[n, w], aw[:, n, :]).then_inc(S[f"out_stored{n}"], 16)
                        act.wait_ge(S["v_masked"], w * N + n + 1 + N)
                        act.dma_start(VW[n, w], vw[:, n, :, :].rearrange("p j c -> p (j c)")).then_inc(S[f"out_stored{n}"], 16)
                for n in range(N):
                    act.wait_ge(S[f"out_stored{n}"], 32 * (WINDOWS + 1))


def attention(nc, sbt, pst, clear, c, S, allsems, XH, AW, VW, AO):
    T, HALF = 8, 2
    TD, TF = N * T + 1, N * T - 1
    HD, HF = N * HALF + 1, N * HALF - 1
    QD, QF = 2 * N * HALF + 1, 2 * N * HALF - 1
    clear(*allsems, start={**{S[k]: N * T for k in ("scored", "max_ready")},
                           **{S[k]: N * HALF for k in "max_turned max_copied av_done recip_ready attn_ready".split()},
                           **{S[k]: 2 * N * HALF for k in ("shifted", "probs_ready")},
                           S["out_stored0"]: 32, S["out_stored1"]: 32})
    with ExitStack() as ph:
        xw = sbt(ph, "a_xw", [72, N, HALF * WPIX])
        aw = sbt(ph, "a_aw", [72, N, 512])
        vw = sbt(ph, "a_vw", [P, N, 4, P])
        mx = sbt(ph, "a_mx", [P, N, T, HEADS])
        pr = sbt(ph, "a_pr", [P, HALF, 4, WPIX])
        rc = sbt(ph, "a_rc", [64, WPIX])
        ao = sbt(ph, "a_ao", [64, N, HALF, WPIX])
        ps = pst(ph, "ps_s", [P, 2, 512])
        pk = pst(ph, "ps_t", [P, 2, 2, WPIX])
        pm = pst(ph, "ps_m", [P, WPIX])
        po = pst(ph, "ps_o", [P, WPIX])
        with nc.Block() as fixed:
            @fixed.vector
            def _(dve):
                for n in range(N):
                    nc.vector.tensor_copy(aw[64:72, n, :], c("minus", 64, 72))
                    nc.vector.tensor_copy(vw[:, n, :, 64:128], c("vmask").rearrange("p (j c) -> p j c", j=4))

        with nc.Block() as block:
            def half(w, n, h):
                return w * (N * HALF) + n * HALF + h

            @block.sync
            def _(sp):
                def load(wy, wx, n):
                    w = sp.snap(wy * NW + wx)
                    sp.wait_ge(S["av_done"], half(w, n, 0) + 2)
                    sp.dma_start(aw[0:64, n, :], AW[n, w]).then_inc(S[f"in_loaded{n}"], 16)
                    sp.dma_start(vw[:, n, :, 0:64], VW[n, w].rearrange("p (j c) -> p j c", j=4)
                                 ).then_inc(S[f"in_loaded{n}"], 16)
                    for h in range(HALF):
                        sp.dma_start(xw[0:64, n, WPIX * h:WPIX * h + WPIX].rearrange("c (r x) -> c r x", x=WW),
                                     XH[n, 64 * h:64 * h + 64, bass.ds(wy * WRP + 1, WRP), bass.ds(wx * WW, WW)]
                                     ).then_inc(S[f"in_loaded{n}"], 16)

                with sp.Fori(0, NW) as wy:
                    with sp.Fori(0, NW) as wx:
                        for n in range(N):
                            load(wy, wx, n)

            @block.scalar
            def _(act):
                def copy_max(w, n, h):
                    act.wait_ge(S["max_turned"], half(w, n, h) + HD)
                    nc.scalar.copy(xw[64:72, n, WPIX * h:WPIX * h + WPIX], pm[0:8, :]).then_inc(S["max_copied"], 1)

                def exps(w, n, h):
                    act.wait_ge(S["av_done"], half(w, n, h) + HF)
                    for b in range(2):
                        act.wait_ge(S["shifted"], 2 * half(w, n, h) + b + QD)
                        nc.scalar.activation(pr[:, h, 2 * b:2 * b + 2, :], pk[:, b, :, :], ACT.Exp
                                             ).then_inc(S["probs_ready"], 1)

                def store(w, wy, wx, n):
                    for h in range(HALF):
                        act.wait_ge(S["attn_ready"], half(w, n, h) + HD)
                        act.dma_start(AO[n, 64 * h:64 * h + 64, bass.ds(wy * WRP, WRP), bass.ds(wx * WW, WW)],
                                      ao[:, n, h, :].rearrange("c (r x) -> c r x", x=WW)
                                      ).then_inc(S[f"out_stored{n}"], 16)

                with act.Fori(0, NW) as wy:
                    with act.Fori(0, NW) as wx:
                        w = act.snap(wy * NW + wx)
                        copy_max(w, 0, 0)
                        copy_max(w, 0, 1)
                        exps(w, 0, 0)
                        copy_max(w, 1, 0)
                        exps(w, 0, 1)
                        copy_max(w, 1, 1)
                        exps(w, 1, 0)
                        store(w, wy, wx, 0)
                        exps(w, 1, 1)
                        store(w, wy, wx, 1)
                for n in range(N):
                    act.wait_ge(S[f"out_stored{n}"], 32 * (WINDOWS + 1))

            @block.tensor
            def _(pe):
                def by_pixel(w, n, t):
                    i = w * (N * T) + n * T + t
                    if t == 0:
                        pe.wait_ge(S[f"in_loaded{n}"], w * 64 + 64)
                    pe.wait_ge(S["max_ready"], i + TF)
                    nc.tensor.matmul(ps[:, t % 2, :], xw[0:64, n, P * t:P * t + P], aw[0:64, n, :], start=True, stop=True
                                     ).then_inc(S["scored"], 1)

                def turn(w, n, h):
                    pe.wait_ge(S["max_ready"], w * (N * T) + n * T + 4 * h + 3 + TD)
                    pe.wait_ge(S["max_copied"], half(w, n, h) - 1 + HD)
                    for q in range(4):
                        mm = nc.tensor.transpose(pm[0:8, P * q:P * q + P], mx[:, n, 4 * h + q, :], c("ident"))
                    mm.then_inc(S["max_turned"], 1)

                def by_key(w, n, h):
                    pe.wait_ge(S["max_copied"], half(w, n, h) + HD)
                    for b in range(2):
                        pe.wait_ge(S["probs_ready"], 2 * half(w, n, h) + b + QF)
                        for q in range(2):
                            j = 2 * b + q
                            mm = nc.tensor.matmul(pk[:, b, q, :], aw[:, n, P * j:P * j + P],
                                                  xw[:, n, WPIX * h:WPIX * h + WPIX], start=True, stop=True)
                        mm.then_inc(S["shifted"], 1)

                def sum_up(w, n, h):
                    pe.wait_ge(S["probs_ready"], 2 * half(w, n, h) + 1 + QD)
                    pe.wait_ge(S["attn_ready"], half(w, n, h) - 1 + HD)
                    for j in range(4):
                        mm = nc.tensor.matmul(po[:, :], vw[:, n, j, :], pr[:, h, j, :], start=(j == 0), stop=(j == 3))
                    mm.then_inc(S["av_done"], 1)

                with pe.Fori(0, WINDOWS) as w:
                    for t in range(T):
                        by_pixel(w, 0, t)
                    for t in range(2):
                        by_pixel(w, 1, t)
                    turn(w, 0, 0)
                    by_pixel(w, 1, 2)
                    by_pixel(w, 1, 3)
                    turn(w, 0, 1)
                    for t in range(4, T):
                        by_pixel(w, 1, t)
                    by_key(w, 0, 0)
                    turn(w, 1, 0)
                    by_key(w, 0, 1)
                    turn(w, 1, 1)
                    sum_up(w, 0, 0)
                    sum_up(w, 0, 1)
                    by_key(w, 1, 0)
                    by_key(w, 1, 1)
                    sum_up(w, 1, 0)
                    sum_up(w, 1, 1)

            @block.vector
            def _(dve):
                with dve.Fori(0, WINDOWS) as w:
                    for n in range(N):
                        for t in range(T):
                            dve.wait_ge(S["scored"], w * (N * T) + n * T + t + TD)
                            nc.vector.reduce_max(mx[:, n, t, :], ps[:, t % 2, :].rearrange("p (h k) -> p h k", h=HEADS), AX.X
                                                 ).then_inc(S["max_ready"], 1)
                    for n in range(N):
                        for h in range(HALF):
                            v = half(w, n, h)
                            dve.wait_ge(S["av_done"], v + HD)
                            if h == 0:
                                dve.wait_ge(S[f"out_stored{n}"], w * 32 + 32)
                            dve.wait_ge(S["attn_ready"], v - 1 + HD)
                            nc.vector.reciprocal(rc[:, :], po[64:128, :]).then_inc(S["recip_ready"], 1)
                            dve.wait_ge(S["recip_ready"], v + HD)
                            nc.vector.tensor_tensor(ao[:, n, h, :], po[0:64, :], rc[:, :], ALU.mult
                                                    ).then_inc(S["attn_ready"], 1)



def mixing(nc, sbt, pst, clear, c, S, allsems, lepm, wod, attb, XH, AO, X1, X2, XH2):
    clear(*allsems, start={**{S[k]: BODY for k in UNIT_SEMS}, S["out_stored0"]: 32, S["out_stored1"]: 32})
    with ExitStack() as ph:
        xs = sbt(ph, "x_xs", [P, N, SRP + 2, PADW])
        ao = sbt(ph, "x_ao", [P, N, SRP, W])
        x1 = sbt(ph, "x_x1", [P, N, SRP, W])
        x2 = sbt(ph, "x_x2", [P, N, SRP, W])
        sq = sbt(ph, "x_sq", [P, 2, COLS])
        sd = sbt(ph, "x_sd", [P, 2, COLS])
        rstd = sbt(ph, "x_rstd", [P, 2, COLS])
        xr = sbt(ph, "x_xr", [P, 2, COLS])
        xh = sbt(ph, "x_xh", [P, N, SRP, W])
        px = pst(ph, "ps_x", [P, 2, COLS])
        pc = pst(ph, "ps_c", [P, 2, COLS])
        pv = pst(ph, "ps_v", [P, 2, COLS])
        with nc.Block() as border:
            @border.vector
            def _(dve):
                nc.vector.memset(xs[:, :, :, 0:2], 0.0)
                nc.vector.memset(xs[:, :, :, PADW - 2:PADW], 0.0)

        with nc.Block() as block:
            @block.sync
            def _(sp):
                def load(s, n):
                    sp.wait_ge(S["conv_done"], first_unit(s, n) + LAST)
                    sp.wait_ge(S["x_ready"], first_unit(s, n) + LAST)
                    for dst, src in ((xs[:, n, :, 2:2 + W], XH[n, :, bass.ds(s * SRP, SRP + 2), :]),
                                     (ao[:, n, :, :], AO[n, :, bass.ds(s * SRP, SRP), :]),
                                     (x1[:, n, :, :], X1[n, :, bass.ds(s * SRP, SRP), :])):
                        sp.dma_start(dst, src).then_inc(S[f"in_loaded{n}"], 16)

                def store(s, n):
                    sp.wait_ge(S["x_ready"], first_unit(s, n) + UNITS - 1 + DONE)
                    sp.dma_start(X2[n, :, bass.ds(s * SRP, SRP), :], x2[:, n, :, :]).then_inc(S[f"out_stored{n}"], 16)
                    sp.wait_ge(S["plus_ready"], first_unit(s, n) + UNITS - 1 + DONE)
                    sp.dma_start(XH2[n, :, bass.ds(s * SRP + 1, SRP), :], xh[:, n, :, :]).then_inc(S[f"out_stored{n}"], 16)

                run_strips(sp, load, store)
                for n in range(N):
                    sp.wait_ge(S[f"out_stored{n}"], 32 * (STRIPS + 1))

            @block.tensor
            def _(pe):
                def conv(s, n, k):
                    u = first_unit(s, n) + k
                    if k == 0:
                        pe.wait_ge(S[f"in_loaded{n}"], s * 48 + 48)
                    pe.wait_ge(S["x_ready"], u + FREE)
                    for g in range(3):
                        for dx in range(5):
                            nc.tensor.matmul(px[:, k % 2, :], lepm[:, g, dx, :],
                                             xs[:, n, UNIT * k + g:UNIT * k + g + UNIT, dx:dx + W],
                                             start=(g + dx == 0), stop=False)
                    nc.tensor.matmul(px[:, k % 2, :], wod[:, :], rows(ao, n, k), start=False, stop=True
                                     ).then_inc(S["conv_done"], 1)

                with pe.Fori(0, STRIPS) as s:
                    for i in range(BODY + 2):
                        if i < BODY:
                            conv(s, i // UNITS, i % UNITS)
                        for back, step in ((1, "centre"), (2, "var")):
                            if 0 <= i - back < BODY:
                                n, k = divmod(i - back, UNITS)
                                norm_on_pe(nc, pe, c, S, first_unit(s, n) + k, x2, sq, pc, pv, n, k, step)

            @block.scalar
            def _(act):
                with act.Fori(0, STRIPS) as s:
                    for i in range(BODY + 2):
                        if i < BODY:
                            n, k = divmod(i, UNITS)
                            square_on_act(nc, act, S, first_unit(s, n) + k, k, sq, pc)
                        if 0 <= i - 1 < BODY:
                            n, k = divmod(i - 1, UNITS)
                            sqrt_on_act(nc, act, S, first_unit(s, n) + k, k, sd, pv, c("eps"))
                        if i >= 2:
                            n, k = divmod(i - 2, UNITS)
                            if k == 0:
                                act.wait_ge(S[f"out_stored{n}"], s * 32 + 32)
                            plus_on_act(nc, act, S, first_unit(s, n) + k, k, n, xr, xh)

            @block.vector
            def _(dve):
                with dve.Fori(0, STRIPS) as s:
                    for i in range(BODY + 2):
                        if i < BODY:
                            n, k = divmod(i, UNITS)
                            u = first_unit(s, n) + k
                            dve.wait_ge(S["conv_done"], u + DONE)
                            if k == 0:
                                dve.wait_ge(S[f"out_stored{n}"], s * 32 + 32)
                            nc.vector.scalar_tensor_tensor(rows(x2, n, k), as_rows(px[:, k % 2, :]), attb[:, 0:1],
                                                           rows(x1, n, k), ALU.add, ALU.add).then_inc(S["x_ready"], 1)
                        if i >= 2:
                            n, k = divmod(i - 2, UNITS)
                            norm_on_dve(nc, dve, S, first_unit(s, n) + k, k, sd, rstd, xr, pc)



def glu(nc, d, sbt, pst, clear, c, S, allsems, glum, wn, fc2, fc2b, dwb, XH2, X2, IMG):
    PBODY = 2 * BODY
    PD, PF = PBODY + 1, PBODY - 1
    clear(*allsems, start={**{S[k]: BODY for k in ("fc2_done", "out_ready")},
                           **{S[k]: PBODY for k in "xbranch_done vbranch_done gelu_ready gated".split()},
                           S["out_stored0"]: 16, S["out_stored1"]: 16})
    with ExitStack() as ph:
        xs = sbt(ph, "g_xs", [P, N, SRP + 2, PADW])
        x2 = sbt(ph, "g_x2", [P, N, SRP, W])
        ge = sbt(ph, "g_ge", [HID, 2, COLS])
        gv = sbt(ph, "g_gv", [HID, 2, COLS])
        xo = sbt(ph, "g_xo", [P, N, SRP, W])
        px = pst(ph, "ps_x", [HID, 2, COLS])
        pv = pst(ph, "ps_v", [HID, 2, COLS])
        po = pst(ph, "ps_o", [P, 2, COLS])
        with nc.Block() as border:
            @border.vector
            def _(dve):
                nc.vector.memset(xs[:, :, :, 0:2], 0.0)
                nc.vector.memset(xs[:, :, :, PADW - 2:PADW], 0.0)

        with nc.Block() as block:
            @block.sync
            def _(sp):
                def load(s, n):
                    sp.wait_ge(S["out_ready"], first_unit(s, n) + LAST)
                    for dst, src in ((xs[:, n, :, 2:2 + W], XH2[n, :, bass.ds(s * SRP, SRP + 2), :]),
                                     (x2[:, n, :, :], X2[n, :, bass.ds(s * SRP, SRP), :])):
                        sp.dma_start(dst, src).then_inc(S[f"in_loaded{n}"], 16)

                def store(s, n):
                    sp.wait_ge(S["out_ready"], first_unit(s, n) + UNITS - 1 + DONE)
                    sp.dma_start(IMG[d + 1, n, :, bass.ds(s * SRP + 1, SRP), :], xo[:, n, :, :]
                                 ).then_inc(S[f"out_stored{n}"], 16)

                run_strips(sp, load, store)
                for n in range(N):
                    sp.wait_ge(S[f"out_stored{n}"], 16 * (STRIPS + 1))

            @block.tensor
            def _(pe):
                def branches(s, n, k, par):
                    v = 2 * (first_unit(s, n) + k) + par
                    if k + par == 0:
                        pe.wait_ge(S[f"in_loaded{n}"], s * 32 + 32)
                    pe.wait_ge(S["gelu_ready"], v + PF)
                    for g in range(2):
                        r = UNIT * k + g + par
                        for dx in range(3):
                            mm = nc.tensor.matmul(px[:, par, :], glum[:, par, g, dx, :],
                                                  xs[:, n, r:r + UNIT, 1 + dx:1 + dx + W],
                                                  start=(g + dx == 0), stop=(g == 1 and dx == 2))
                    mm.then_inc(S["xbranch_done"], 1)
                    pe.wait_ge(S["gated"], v + PF)
                    hp = slice(64 * par, 64 * par + 64)
                    nc.tensor.matmul(pv[:, par, :], wn[hp, 320:448],
                                     xs[hp, n, UNIT * k + 1:UNIT * k + 1 + UNIT, 2:2 + W], start=True, stop=True
                                     ).then_inc(S["vbranch_done"], 1)

                def project(s, n, k):
                    u = first_unit(s, n) + k
                    pe.wait_ge(S["out_ready"], u + FREE)
                    for par in range(2):
                        pe.wait_ge(S["gated"], 2 * u + par + PD)
                        mm = nc.tensor.matmul(po[64 * par:64 * par + 64, k % 2, :], fc2[:, :], gv[:, par, :],
                                              start=True, stop=True)
                    mm.then_inc(S["fc2_done"], 1)

                with pe.Fori(0, STRIPS) as s:
                    for i in range(BODY + 1):
                        if i < BODY:
                            branches(s, i // UNITS, i % UNITS, 0)
                        if i >= 1:
                            project(s, (i - 1) // UNITS, (i - 1) % UNITS)
                        if i < BODY:
                            branches(s, i // UNITS, i % UNITS, 1)

            @block.scalar
            def _(act):
                with act.Fori(0, STRIPS) as s:
                    for n in range(N):
                        for k in range(UNITS):
                            for par in range(2):
                                v = 2 * (first_unit(s, n) + k) + par
                                act.wait_ge(S["xbranch_done"], v + PD)
                                act.wait_ge(S["gated"], v + PF)
                                nc.scalar.activation(ge[:, par, :], px[:, par, :], ACT.Gelu, bias=dwb[:, 0:1]
                                                     ).then_inc(S["gelu_ready"], 1)

            @block.vector
            def _(dve):
                def gate(s, n, k, par):
                    u = first_unit(s, n) + k
                    dve.wait_ge(S["gelu_ready"], 2 * u + par + PD)
                    dve.wait_ge(S["vbranch_done"], 2 * u + par + PD)
                    dve.wait_ge(S["fc2_done"], u - 1 + DONE)
                    nc.vector.tensor_tensor(gv[:, par, :], pv[:, par, :], ge[:, par, :], ALU.mult
                                            ).then_inc(S["gated"], 1)

                with dve.Fori(0, STRIPS) as s:
                    for i in range(BODY + 1):
                        if i >= 1:
                            n, k = divmod(i - 1, UNITS)
                            u = first_unit(s, n) + k
                            dve.wait_ge(S["fc2_done"], u + DONE)
                            if k == 0:
                                dve.wait_ge(S[f"out_stored{n}"], s * 16 + 16)
                            nc.vector.scalar_tensor_tensor(rows(xo, n, k), as_rows(po[:, k % 2, :]), fc2b[:, 0:1],
                                                           rows(x2, n, k), ALU.add, ALU.add).then_inc(S["out_ready"], 1)
                        if i < BODY:
                            for par in range(2):
                                gate(s, i // UNITS, i % UNITS, par)



def layer1(nc, I, sem, sbt, pst, clear, c, IMG, STAT, out):
    ctx = ExitStack()
    ctx.__enter__()
    x_in = IMG[D]
    W1, W2, GW, GB = slice(0, 64), slice(64, 128), slice(128, 129), slice(129, 130)
    prm = sbt(ctx, "prm", [P, 130])
    mom = sbt(ctx, "mom", [P, 130])
    w1t = sbt(ctx, "w1t", [P, HID])
    w2n = sbt(ctx, "w2n", [P, HID])
    w2b = sbt(ctx, "w2b", [P, HID])
    gram = sbt(ctx, "gram", [P, N, P + 1])
    gm = sbt(ctx, "gm", [P, N, 65])
    cov = sbt(ctx, "cov", [P, N, 64])
    mub = sbt(ctx, "mub", [P, N, 64])
    mg = sbt(ctx, "mg", [P, N])
    rstd = sbt(ctx, "rstd", [P, N])
    sc = sbt(ctx, "sc", [P, N])
    bi = sbt(ctx, "bi", [P, N])
    coef = sbt(ctx, "coef", [P, N])
    run = sbt(ctx, "run", [P, 2])
    ab = sbt(ctx, "ab", [P, 2])
    abb = sbt(ctx, "abb", [P, 2, 64])
    dbias = sbt(ctx, "dbias", [P, 1])
    acc = sbt(ctx, "acc", [P, N, 130])
    m_loaded, m_link = sem("m_loaded"), sem("m_link")
    S = {k: sem("m_" + k) for k in """in_loaded0 in_loaded1 out_stored0 out_stored1 turned copied gram_done summed
        h_done gelu_ready z_ready zz_ready den_ready tanh_ready onep_ready gz_ready r1_ready slope_ready tail_ready r2_ready
        phi_ready dgelu_ready y_done y_ready stats_ready d_done dh_ready ef_done
        copied_dve copied_act out_ready""".split()}
    allsems = [m_loaded, m_link, *S.values()]
    env = (nc, sbt, pst, clear, c, S, allsems)

    clear(*allsems)
    with ExitStack() as ph:
        w2 = sbt(ph, "w2", [64, HID])
        g1 = sbt(ph, "g1", [16, 64])
        g1t = sbt(ph, "g1t", [64, 16])
        g1b = sbt(ph, "g1b", [16, 1])
        g2 = sbt(ph, "g2", [16, 1])
        g2r = sbt(ph, "g2r", [16, P])
        g2b = sbt(ph, "g2b", [P, 1])
        res = sbt(ph, "res", [P, 1])
        own = sbt(ph, "own", [P, N, 65])
        mur = sbt(ph, "mur", [64, N, P])
        gg = sbt(ph, "gg", [16, N])
        mm = sbt(ph, "mm", [P, 64])
        first = ExitStack()
        ps = pst(first, "ps_m", [P, 2, 512])
        with nc.Block() as load:
            @load.sync
            def _(sp):
                k = [0]

                def get(dst, src):
                    sp.dma_start(dst, src).then_inc(m_loaded, 16)
                    k[0] += 1

                def column(name):
                    return I[name].rearrange("(c o) -> c o", o=1)

                get(prm[:, W1], I["m_w1"])
                get(prm[:, GW], column("m_gn_w"))
                get(prm[:, GB], column("m_gn_b"))
                get(w2[:, :], I["m_w2"])
                get(g1[:, :], I["m_g1_w"])
                get(g1b[:, :], column("m_g1_b"))
                get(g2[:, :], I["m_g2_w"].rearrange("a c -> c a"))
                get(g2b[:, :], column("m_g2_b").to_broadcast([P, 1]))
                get(res[:, :], column("m_residual_scale").to_broadcast([P, 1]))
                for h in range(2):
                    get(run[64 * h:64 * h + 64, 0:1], column("m_running_mean"))
                    get(run[64 * h:64 * h + 64, 1:2], column("m_running_var"))
                sp.wait_ge(m_loaded, 16 * k[0])

            @load.gpsimd
            def _(pool):
                pool.memset(mom[:, :], 0.0)
                pool.memset(gram[:, :, :], 0.0)

        with nc.Block() as turn:
            @turn.tensor
            def _(pe):
                nc.tensor.transpose(ps[:, 0, 0:64], w2[:, :], c("ident", 0, 64)[:, 0:64])
                nc.tensor.transpose(ps[0:64, 1, 0:16], g1[:, :], c("ident", 0, 16)[:, 0:16])

        with nc.Block() as keep:
            @keep.vector
            def _(dve):
                nc.vector.tensor_copy(prm[:, W2], ps[:, 0, 0:64])
                nc.vector.tensor_copy(g1t[:, :], ps[0:64, 1, 0:16])
                nc.vector.tensor_copy(g2r[:, :], g2[:, 0:1].to_broadcast([16, P]))

        first.close()
        gram_pass(*env, x_in, gram)
        ps = pst(ph, "ps_m", [P, 8, 512])

        clear(m_link)
        with nc.Block() as blocks:
            @blocks.vector
            def _(dve):
                for n in range(N):
                    for h in range(2):
                        hp = slice(64 * h, 64 * h + 64)
                        nc.vector.tensor_copy(own[hp, n, 0:64], gram[hp, n, 64 * h:64 * h + 64])
                    nc.vector.tensor_copy(own[:, n, 64:65], gram[:, n, P:P + 1])

        with nc.Block() as parities:
            @parities.tensor
            def _(pe):
                for n in range(N):
                    nc.tensor.matmul(ps[:, n, 0:65], c("pair"), own[:, n, :], start=True, stop=True)

        clear(m_link)
        with nc.Block() as means:
            @means.vector
            def _(dve):
                step = Link(nc, m_link, dve)
                for n in range(N):
                    step(nc.vector.tensor_scalar_mul(gm[:, n, :], ps[:, n, 0:65], 1.0 / PIX))
                    nc.vector.tensor_copy(mur[:, n, :], gm[0:64, n, 64:65].to_broadcast([64, P]))

        with nc.Block() as spread:
            @spread.tensor
            def _(pe):
                for n in range(N):
                    nc.tensor.matmul(ps[:, 2 + n, 0:64], mur[:, n, :], c("ident", 0, 64)[:, 0:64], start=True, stop=True)
                    nc.tensor.matmul(ps[0:16, 4, n:n + 1], g1t[:, :], gm[0:64, n, 64:65], start=True, stop=True)

        clear(m_link)
        with nc.Block() as covariance:
            @covariance.vector
            def _(dve):
                step = Link(nc, m_link, dve)
                for n in range(N):
                    step(nc.vector.tensor_copy(mub[:, n, :], ps[:, 2 + n, 0:64]))
                    step(nc.vector.tensor_scalar(mm[:, :], mub[:, n, :], gm[:, n, 64:65], None, ALU.mult))
                    step(nc.vector.tensor_tensor(cov[:, n, :], gm[:, n, 0:64], mm[:, :], ALU.subtract))

            @covariance.scalar
            def _(act):
                nc.scalar.activation(gg[:, :], ps[0:16, 4, 0:N], ACT.Gelu, bias=g1b[:, 0:1])

        with nc.Block() as gate:
            @gate.tensor
            def _(pe):
                nc.tensor.matmul(ps[:, 5, 0:N], g2r[:, :], gg[:, :], start=True, stop=True)

        with nc.Block() as sigmoid:
            @sigmoid.scalar
            def _(act):
                nc.scalar.activation(coef[:, :], ps[:, 5, 0:N], ACT.Sigmoid, bias=g2b[:, 0:1])

        with nc.Block() as scale:
            @scale.vector
            def _(dve):
                nc.vector.tensor_scalar(coef[:, :], coef[:, :], res[:, 0:1], None, ALU.mult)

    def prepare():
        with ExitStack() as ph:
            dup = sbt(ph, "dup", [P, 2, 2, 64])
            hm = sbt(ph, "hm", [P, N])
            wc = sbt(ph, "wc", [P, N, 64])
            wh = sbt(ph, "wh", [P, 64])
            size = sbt(ph, "size", [P, 4])
            t = sbt(ph, "t", [P, N])
            ps = pst(ph, "ps_p", [P, 8, 512])
            clear(m_link)
            with nc.Block() as double:
                @double.vector
                def _(dve):
                    step = Link(nc, m_link, dve)
                    for i, w in enumerate((W1, W2)):
                        nc.vector.tensor_copy(dup[:, i, :, :], prm[:, None, w].to_broadcast([P, 2, 64]))
                    step(nc.vector.tensor_reduce(size[:, 0:1], prm[:, W1], AX.X, ALU.max))
                    step(nc.vector.tensor_reduce(size[:, 1:2], prm[:, W1], AX.X, ALU.min))
                    step(nc.vector.tensor_scalar_mul(size[:, 1:2], size[:, 1:2], -1.0))
                    nc.vector.tensor_tensor(size[:, 0:1], size[:, 0:1], size[:, 1:2], ALU.max)
            with nc.Block() as turn:
                @turn.tensor
                def _(pe):
                    for i in range(2):
                        nc.tensor.transpose(ps[:, i, 0:P], dup[:, i, :, :].rearrange("o a c -> o (a c)"), c("ident"))
                    nc.tensor.matmul(ps[:, 7, 0:1], c("group"), size[:, 0:1], start=True, stop=True)
            clear(m_link)
            with nc.Block() as keep:
                @keep.vector
                def _(dve):
                    step = Link(nc, m_link, dve)
                    nc.vector.tensor_copy(w1t[:, :], ps[:, 0, 0:P])
                    nc.vector.tensor_copy(w2n[:, :], ps[:, 1, 0:P])
                    step(nc.vector.tensor_scalar(size[:, 1:2], ps[:, 7, 0:1], 1e-15, None, ALU.max))
                    step(nc.vector.reciprocal(size[:, 2:3], size[:, 1:2]))
                    nc.vector.tensor_scalar(wh[:, :], prm[:, W1], size[:, 2:3], None, ALU.mult)
                    nc.vector.tensor_scalar(size[:, 3:4], size[:, 2:3], size[:, 2:3], GN_EPS, ALU.mult, ALU.mult)
            with nc.Block() as moments:
                @moments.tensor
                def _(pe):
                    for n in range(N):
                        nc.tensor.matmul(ps[:, 2, n:n + 1], w1t[0:64, :], gm[0:64, n, 64:65], start=True, stop=True)
                        nc.tensor.matmul(ps[:, 3 + n, 0:64], w1t[0:64, :], cov[0:64, n, :], start=True, stop=True)
            clear(m_link)
            with nc.Block() as own_variance:
                @own_variance.vector
                def _(dve):
                    step = Link(nc, m_link, dve)
                    nc.vector.tensor_scalar(hm[:, :], ps[:, 2, 0:N], size[:, 2:3], None, ALU.mult)
                    for n in range(N):
                        step(nc.vector.scalar_tensor_tensor(wc[:, n, :], ps[:, 3 + n, 0:64], size[:, 2:3], wh[:, :],
                                                            ALU.mult, ALU.mult))
                    nc.vector.reduce_sum(rstd[:, :], wc[:, :, :], AX.X)
            with nc.Block() as group_mean:
                @group_mean.tensor
                def _(pe):
                    nc.tensor.matmul(ps[:, 5, 0:N], c("group"), hm[:, :], start=True, stop=True)
            clear(m_link)
            with nc.Block() as spread:
                @spread.vector
                def _(dve):
                    step = Link(nc, m_link, dve)
                    step(nc.vector.tensor_scalar_mul(mg[:, :], ps[:, 5, 0:N], 1.0 / GROUP))
                    step(nc.vector.tensor_tensor(t[:, :], hm[:, :], mg[:, :], ALU.subtract))
                    step(nc.vector.tensor_tensor(t[:, :], t[:, :], t[:, :], ALU.mult))
                    step(nc.vector.tensor_tensor(t[:, :], t[:, :], rstd[:, :], ALU.add))
                    nc.vector.tensor_scalar(mg[:, :], mg[:, :], size[:, 1:2], None, ALU.mult)
            with nc.Block() as group_variance:
                @group_variance.tensor
                def _(pe):
                    nc.tensor.matmul(ps[:, 6, 0:N], c("group"), t[:, :], start=True, stop=True)
            clear(m_link)
            with nc.Block() as positive:
                @positive.vector
                def _(dve):
                    nc.vector.tensor_scalar(t[:, :], ps[:, 6, 0:N], 1.0 / GROUP, 0.0, ALU.mult, ALU.max)
            with nc.Block() as root:
                @root.scalar
                def _(act):
                    nc.scalar.activation(t[:, :], t[:, :], ACT.Sqrt, bias=size[:, 3:4])
            clear(m_link)
            with nc.Block() as affine:
                @affine.vector
                def _(dve):
                    step = Link(nc, m_link, dve)
                    step(nc.vector.tensor_scalar(t[:, :], t[:, :], size[:, 1:2], None, ALU.mult))
                    step(nc.vector.reciprocal(rstd[:, :], t[:, :]))
                    step(nc.vector.tensor_scalar(t[:, :], t[:, :], DEVIATION_MAX, None, ALU.is_le))
                    step(nc.vector.tensor_tensor(rstd[:, :], rstd[:, :], t[:, :], ALU.mult))
                    step(nc.vector.tensor_scalar(sc[:, :], rstd[:, :], prm[:, GW], None, ALU.mult))
                    step(nc.vector.tensor_tensor(t[:, :], mg[:, :], sc[:, :], ALU.mult))
                    step(nc.vector.tensor_scalar(bi[:, :], t[:, :], prm[:, GB], -1.0, ALU.subtract, ALU.mult))

    def loss_gradient():
        with ExitStack() as ph:
            st = sbt(ph, "st", [P, N, STRIPS * UNITS * 6])
            mv = sbt(ph, "mv", [P, N, 2])
            t = sbt(ph, "t", [P, 8])
            q = sbt(ph, "q", [P, N])
            abr = sbt(ph, "abr", [64, 2, P])
            ps = pst(ph, "ps_l", [P, 8, 512])
            clear(m_loaded)
            with nc.Block() as load:
                @load.sync
                def _(sp):
                    for n in range(N):
                        sp.dma_start(st[:, n, :], STAT[n].rearrange("p s k -> p (s k)")).then_inc(m_loaded, 16)
                    sp.wait_ge(m_loaded, 16 * N)
            with nc.Block() as merge:
                @merge.vector
                def _(dve):
                    for n in range(N):
                        nc.vector.bn_aggr(mv[:, n, :], st[:, n, :])
            with nc.Block() as mean:
                @mean.tensor
                def _(pe):
                    nc.tensor.matmul(ps[:, 0, 0:N], c("pair"), mv[:, :, 0], start=True, stop=True)
            clear(m_link)
            with nc.Block() as deviations:
                @deviations.vector
                def _(dve):
                    step = Link(nc, m_link, dve)
                    step(nc.vector.reduce_sum(t[:, 0:1], ps[:, 0, 0:N], AX.X))
                    step(nc.vector.tensor_scalar_mul(t[:, 0:1], t[:, 0:1], 1.0 / (2 * N)))
                    step(nc.vector.tensor_scalar(q[:, :], mv[:, :, 0], t[:, 0:1], None, ALU.subtract))
                    step(nc.vector.tensor_tensor(q[:, :], q[:, :], q[:, :], ALU.mult))
                    step(nc.vector.tensor_tensor(q[:, :], q[:, :], mv[:, :, 1], ALU.add))
            with nc.Block() as variance:
                @variance.tensor
                def _(pe):
                    nc.tensor.matmul(ps[:, 1, 0:N], c("pair"), q[:, :], start=True, stop=True)
            clear(m_link)
            count = N * PIX
            with nc.Block() as coefficients:
                @coefficients.vector
                def _(dve):
                    step = Link(nc, m_link, dve)
                    step(nc.vector.reduce_sum(t[:, 1:2], ps[:, 1, 0:N], AX.X))
                    step(nc.vector.tensor_scalar_mul(t[:, 1:2], t[:, 1:2], count / (count - 1.0) / (2 * N)))
                    step(nc.vector.tensor_scalar_add(t[:, 2:3], run[:, 1:2], 1e-8))
                    step(nc.vector.reciprocal(t[:, 3:4], t[:, 2:3]))
                    step(nc.vector.tensor_tensor(t[:, 4:5], t[:, 1:2], t[:, 3:4], ALU.mult))
                    step(nc.vector.tensor_scalar_add(t[:, 4:5], t[:, 4:5], -1.0))
                    step(nc.vector.tensor_tensor(t[:, 4:5], t[:, 4:5], t[:, 3:4], ALU.mult))
                    step(nc.vector.tensor_scalar_mul(ab[:, 1:2], t[:, 4:5], 4.0 / C / (count - 1)))
                    step(nc.vector.tensor_tensor(t[:, 5:6], t[:, 0:1], run[:, 0:1], ALU.subtract))
                    step(nc.vector.tensor_scalar_mul(t[:, 5:6], t[:, 5:6], 2.0 / C / count))
                    step(nc.vector.tensor_tensor(t[:, 6:7], ab[:, 1:2], t[:, 0:1], ALU.mult))
                    step(nc.vector.tensor_tensor(ab[:, 0:1], t[:, 5:6], t[:, 6:7], ALU.subtract))
                    for i in range(2):
                        nc.vector.tensor_copy(abr[:, i, :], ab[0:64, i:i + 1].to_broadcast([64, P]))
                    nc.vector.tensor_scalar(w2b[:, :], w2n[:, :], ab[:, 1:2], None, ALU.mult)
                    nc.vector.memset(acc[:, :, :], 0.0)
            with nc.Block() as spread:
                @spread.tensor
                def _(pe):
                    for i in range(2):
                        nc.tensor.matmul(ps[:, 2 + i, 0:64], abr[:, i, :], c("ident", 0, 64)[:, 0:64], start=True, stop=True)
                    nc.tensor.matmul(ps[:, 4, 0:1], w2n[0:64, :], ab[0:64, 0:1], start=True, stop=True)
            with nc.Block() as keep:
                @keep.vector
                def _(dve):
                    nc.vector.tensor_copy(abb[:, :, :], ps[:, 2:4, 0:64])
                    nc.vector.tensor_copy(dbias[:, :], ps[:, 4, 0:1])

    def descend():
        with ExitStack() as ph:
            gr = sbt(ph, "gr", [P, 130])
            t = sbt(ph, "t", [P, N, 64])
            u = sbt(ph, "u", [P, N, 64])
            q = sbt(ph, "q", [P, N])
            th = sbt(ph, "th", [P, N])
            gs = sbt(ph, "gs", [P, 2, N])
            ms = sbt(ph, "ms", [P, 2, N])
            ps = pst(ph, "ps_d", [P, 8, 512])
            clear(m_link)
            with nc.Block() as outer:
                @outer.vector
                def _(dve):
                    step = Link(nc, m_link, dve)
                    step(nc.vector.tensor_tensor(gr[:, W2], acc[:, 0, 65:129], acc[:, 1, 65:129], ALU.add))
                    step(nc.vector.tensor_tensor(q[:, 0:1], acc[:, 0, 129:130], acc[:, 1, 129:130], ALU.add))
                    step(nc.vector.tensor_tensor(gr[:, W2], gr[:, W2], abb[:, 1, :], ALU.mult))
                    step(nc.vector.tensor_scalar(t[:, 0, :], abb[:, 0, :], q[:, 0:1], None, ALU.mult))
                    step(nc.vector.tensor_tensor(gr[:, W2], gr[:, W2], t[:, 0, :], ALU.add))
                    step(nc.vector.tensor_tensor(gr[:, GB], acc[:, 0, 64:65], acc[:, 1, 64:65], ALU.add))
                    for n in range(N):
                        step(nc.vector.tensor_tensor(t[:, n, :], acc[:, n, 0:64], prm[:, W1], ALU.mult))
                    step(nc.vector.reduce_sum(q[:, :], t[:, :, :], AX.X))
                    step(nc.vector.tensor_tensor(th[:, :], mg[:, :], acc[:, :, 64], ALU.mult))
                    step(nc.vector.tensor_tensor(th[:, :], q[:, :], th[:, :], ALU.subtract))
                    step(nc.vector.tensor_tensor(th[:, :], th[:, :], rstd[:, :], ALU.mult))
                    step(nc.vector.reduce_sum(gr[:, GW], th[:, :], AX.X))
                    step(nc.vector.tensor_scalar(gs[:, 0, :], acc[:, :, 64], prm[:, GW], None, ALU.mult))
                    step(nc.vector.tensor_scalar(gs[:, 1, :], th[:, :], prm[:, GW], None, ALU.mult))
            with nc.Block() as groups:
                @groups.tensor
                def _(pe):
                    nc.tensor.matmul(ps[:, 0, 0:2 * N], c("group"), gs[:, :, :].rearrange("p a n -> p (a n)"),
                                     start=True, stop=True)
                    for n in range(N):
                        nc.tensor.matmul(ps[:, 1 + n, 0:64], w1t[0:64, :], gm[0:64, n, 0:64], start=True, stop=True)
            clear(m_link)
            with nc.Block() as inner:
                @inner.vector
                def _(dve):
                    step = Link(nc, m_link, dve)
                    step(nc.vector.tensor_scalar_mul(ms[:, :, :].rearrange("p a n -> p (a n)"), ps[:, 0, 0:2 * N], 1.0 / GROUP))
                    for n in range(N):
                        step(nc.vector.tensor_scalar(u[:, n, :], mub[:, n, :], mg[:, n:n + 1], None, ALU.mult))
                        step(nc.vector.tensor_tensor(u[:, n, :], ps[:, 1 + n, 0:64], u[:, n, :], ALU.subtract))
                        step(nc.vector.tensor_scalar(u[:, n, :], u[:, n, :], rstd[:, n:n + 1], ms[:, 1, n:n + 1],
                                                     ALU.mult, ALU.mult))
                        step(nc.vector.tensor_scalar(t[:, n, :], mub[:, n, :], ms[:, 0, n:n + 1], None, ALU.mult))
                        step(nc.vector.tensor_tensor(u[:, n, :], u[:, n, :], t[:, n, :], ALU.add))
                        step(nc.vector.tensor_scalar(t[:, n, :], acc[:, n, 0:64], prm[:, GW], None, ALU.mult))
                        step(nc.vector.tensor_tensor(t[:, n, :], t[:, n, :], u[:, n, :], ALU.subtract))
                        step(nc.vector.tensor_scalar(t[:, n, :], t[:, n, :], rstd[:, n:n + 1], None, ALU.mult))
                    step(nc.vector.tensor_tensor(gr[:, W1], t[:, 0, :], t[:, 1, :], ALU.add))
                    step(nc.vector.tensor_scalar_mul(mom[:, :], mom[:, :], MOM))
                    step(nc.vector.tensor_tensor(mom[:, :], mom[:, :], gr[:, :], ALU.add))
                    step(nc.vector.tensor_scalar_mul(gr[:, :], mom[:, :], LR))
                    step(nc.vector.tensor_tensor(prm[:, :], prm[:, :], gr[:, :], ALU.subtract))

    with nc.Fori(0, STEPS):
        prepare()
        forward(*env, x_in, prm, w1t, sc, bi, STAT, None, None)
        loss_gradient()
        backward(*env, x_in, prm, w1t, w2b, sc, bi, dbias, acc)
        descend()
    prepare()
    forward(*env, x_in, prm, w1t, sc, bi, None, coef, out)
    ctx.close()


def gram_pass(nc, sbt, pst, clear, c, S, allsems, x_in, gram):
    clear(*allsems, start={S[k]: BODY for k in ("turned", "copied", "gram_done", "summed")})
    with ExitStack() as ph:
        xs = sbt(ph, "xs", [P, N, SRP, W])
        xt = sbt(ph, "xt", [P, 2, 4, P + 1])
        pt = pst(ph, "ps_t", [P, 2, 512])
        pg = pst(ph, "ps_g", [P, 2, 512])
        with nc.Block() as ones:
            @ones.vector
            def _(dve):
                nc.vector.memset(xt[:, :, :, P:P + 1], 1.0)
        with nc.Block() as block:
            @block.sync
            def _(sp):
                with sp.Fori(0, STRIPS) as s:
                    for n in range(N):
                        sp.wait_ge(S["turned"], first_unit(s, n) + LAST)
                        sp.dma_start(xs[:, n, :, :], x_in[n, :, bass.ds(s * SRP + 1, SRP), :]
                                     ).then_inc(S[f"in_loaded{n}"], 16)

            @block.tensor
            def _(pe):
                def turn(s, n, k):
                    if k == 0:
                        pe.wait_ge(S[f"in_loaded{n}"], s * 16 + 16)
                    pe.wait_ge(S["copied"], first_unit(s, n) + k + FREE)
                    cols = rows(xs, n, k).rearrange("p r w -> p (r w)")
                    for b in range(4):
                        mm = nc.tensor.transpose(pt[:, k % 2, P * b:P * b + P], cols[:, P * b:P * b + P], c("ident"))
                    mm.then_inc(S["turned"], 1)

                def product(s, n, k):
                    u = first_unit(s, n) + k
                    pe.wait_ge(S["copied"], u + DONE)
                    if k == 0:
                        pe.wait_ge(S["summed"], s * N + n - 1 + BODY)
                    for b in range(4):
                        mm = nc.tensor.matmul(pg[:, n, 0:P + 1], xt[:, k % 2, b, 0:P], xt[:, k % 2, b, :],
                                              start=(k + b == 0), stop=(k == UNITS - 1 and b == 3))
                    mm.then_inc(S["gram_done"], 1)

                with pe.Fori(0, STRIPS) as s:
                    for i in range(BODY + 1):
                        if i < BODY:
                            turn(s, i // UNITS, i % UNITS)
                        if i >= 1:
                            product(s, (i - 1) // UNITS, (i - 1) % UNITS)

            @block.scalar
            def _(act):
                with act.Fori(0, STRIPS) as s:
                    for n in range(N):
                        for k in range(UNITS):
                            u = first_unit(s, n) + k
                            act.wait_ge(S["turned"], u + DONE)
                            act.wait_ge(S["gram_done"], u + FREE)
                            nc.scalar.copy(xt[:, k % 2, :, 0:P], pt[:, k % 2, :].rearrange("p (b c) -> p b c", b=4)
                                           ).then_inc(S["copied"], 1)

            @block.vector
            def _(dve):
                with dve.Fori(0, STRIPS) as s:
                    for n in range(N):
                        dve.wait_ge(S["gram_done"], first_unit(s, n) + UNITS - 1 + DONE)
                        dve.wait_ge(S["summed"], s * N + n - 1 + BODY)
                        nc.vector.tensor_tensor(gram[:, n, :], gram[:, n, :], pg[:, n, 0:P + 1], ALU.add
                                                ).then_inc(S["summed"], 1)


def hidden_on_pe(nc, pe, S, u, s, n, k, w1t, xs, ph):
    if k == 0:
        pe.wait_ge(S[f"in_loaded{n}"], s * 16 + 16)
    for par in range(2):
        hp = slice(64 * par, 64 * par + 64)
        mm = nc.tensor.matmul(ph[:, par, :], w1t[hp, :], xs[hp, n, UNIT * k:UNIT * k + UNIT, :], start=True, stop=True)
    mm.then_inc(S["h_done"], 1)


def forward(nc, sbt, pst, clear, c, S, allsems, x_in, prm, w1t, sc, bi, STAT, coef, out):
    names = "h_done gelu_ready y_done y_ready stats_ready out_ready".split()
    last = out is not None
    clear(*allsems, start={**{S[k]: BODY for k in names}, S["out_stored0"]: 32, S["out_stored1"]: 32})
    per_store = 32 if last else 16
    if not last:
        clear(S["out_stored0"], S["out_stored1"], start={S["out_stored0"]: 16, S["out_stored1"]: 16})
    with ExitStack() as ctx:
        xs = sbt(ctx, "xs", [P, N, SRP, W])
        g = sbt(ctx, "g", [P, 2, 2, COLS])
        ys = sbt(ctx, "ys", [P, N, SRP, W])
        st = sbt(ctx, "stats", [P, N, UNITS * 6])
        ph = pst(ctx, "ps_h", [P, 2, 2, COLS])
        py = pst(ctx, "ps_y", [P, 2, COLS])
        with nc.Block() as block:
            @block.sync
            def _(sp):
                def load(s, n):
                    sp.wait_ge(S["y_ready"], first_unit(s, n) + LAST)
                    sp.dma_start(xs[:, n, :, :], x_in[n, :, bass.ds(s * SRP + 1, SRP), :]
                                 ).then_inc(S[f"in_loaded{n}"], 16)

                def store(s, n):
                    if last:
                        sp.wait_ge(S["y_ready"], first_unit(s, n) + UNITS - 1 + DONE)
                        image = out[n].rearrange("c (r p) w -> p c r w", p=2)
                        for par in range(2):
                            sp.dma_start(image[par, :, bass.ds(s * SRP, SRP), :], ys[64 * par:64 * par + 64, n, :, :]
                                         ).then_inc(S[f"out_stored{n}"], 16)
                    else:
                        sp.wait_ge(S["stats_ready"], first_unit(s, n) + UNITS - 1 + DONE)
                        sp.dma_start(STAT[n, :, s, :], st[:, n, :]).then_inc(S[f"out_stored{n}"], 16)

                run_strips(sp, load, store)
                for n in range(N):
                    sp.wait_ge(S[f"out_stored{n}"], per_store * (STRIPS + 1))

            @block.tensor
            def _(pe):
                def hidden(s, n, k):
                    u = first_unit(s, n) + k
                    pe.wait_ge(S["gelu_ready"], u + FREE)
                    hidden_on_pe(nc, pe, S, u, s, n, k, w1t, xs, ph[:, k % 2, :, :])

                def project(s, n, k):
                    u = first_unit(s, n) + k
                    pe.wait_ge(S["gelu_ready"], u + DONE)
                    pe.wait_ge(S["y_ready"], u + FREE)
                    for par in range(2):
                        mm = nc.tensor.matmul(py[64 * par:64 * par + 64, k % 2, :], prm[:, 64:128], g[:, k % 2, par, :],
                                              start=True, stop=True)
                    mm.then_inc(S["y_done"], 1)

                with pe.Fori(0, STRIPS) as s:
                    for i in range(BODY + 1):
                        if i < BODY:
                            hidden(s, i // UNITS, i % UNITS)
                        if i >= 1:
                            project(s, (i - 1) // UNITS, (i - 1) % UNITS)

            @block.scalar
            def _(act):
                with act.Fori(0, STRIPS) as s:
                    for n in range(N):
                        for k in range(UNITS):
                            u = first_unit(s, n) + k
                            act.wait_ge(S["h_done"], u + DONE)
                            act.wait_ge(S["y_done"], u + FREE)
                            nc.scalar.activation(g[:, k % 2, :, :], ph[:, k % 2, :, :], ACT.Gelu, bias=bi[:, n:n + 1],
                                                 scale=sc[:, n:n + 1]).then_inc(S["gelu_ready"], 1)

            @block.vector
            def _(dve):
                with dve.Fori(0, STRIPS) as s:
                    for n in range(N):
                        for k in range(UNITS):
                            u = first_unit(s, n) + k
                            dve.wait_ge(S["y_done"], u + DONE)
                            if k == 0 and last:
                                dve.wait_ge(S[f"out_stored{n}"], s * 32 + 32)
                            if last:
                                nc.vector.scalar_tensor_tensor(rows(ys, n, k), as_rows(py[:, k % 2, :]), coef[:, n:n + 1],
                                                               rows(xs, n, k), ALU.mult, ALU.add).then_inc(S["y_ready"], 1)
                            else:
                                dve.wait_ge(S["stats_ready"], u + FREE)
                                nc.vector.tensor_tensor(rows(ys, n, k), as_rows(py[:, k % 2, :]), rows(xs, n, k), ALU.add
                                                        ).then_inc(S["y_ready"], 1)
                                dve.wait_ge(S["y_ready"], u + DONE)
                                if k == 0:
                                    dve.wait_ge(S[f"out_stored{n}"], s * 16 + 16)
                                nc.vector.bn_stats(st[:, n, 6 * k:6 * k + 6], rows(ys, n, k).rearrange("p r w -> p (r w)")
                                                   ).then_inc(S["stats_ready"], 1)


def backward(nc, sbt, pst, clear, c, S, allsems, x_in, prm, w1t, w2b, sc, bi, dbias, acc):
    names = """h_done gelu_ready z_ready zz_ready den_ready tanh_ready onep_ready gz_ready r1_ready slope_ready
        tail_ready r2_ready phi_ready dgelu_ready y_done y_ready d_done dh_ready ef_done summed""".split()
    clear(*allsems, start={**{S[k]: BODY for k in names}, S["copied_dve"]: 1, S["copied_act"]: 1})
    X, G0, G1, Y, D0, D1 = range(6)
    with ExitStack() as ctx:
        xs = sbt(ctx, "xs", [P, N, SRP, W])
        g = sbt(ctx, "g", [P, 2, 2, COLS])
        z = sbt(ctx, "z", [P, 2, 2, COLS])
        zz = sbt(ctx, "zz", [P, 2, 2, COLS])
        den = sbt(ctx, "den", [P, 2, 2, COLS])
        th = sbt(ctx, "th", [P, 2, 2, COLS])
        gz = sbt(ctx, "gz", [P, 2, 2, COLS])
        tail = sbt(ctx, "tail", [P, 2, 2, COLS])
        gp = sbt(ctx, "gp", [P, 2, COLS])
        ys = sbt(ctx, "ys", [P, 2, COLS])
        dh = sbt(ctx, "dh", [P, 2, 2, COLS])
        xt = sbt(ctx, "xt", [P, 4, 2, 65])
        yt = sbt(ctx, "yt", [P, 4, 2, 65])
        gt = sbt(ctx, "gt", [P, 2, 4, HID])
        dt = sbt(ctx, "dt", [P, 2, 4, HID])
        ph = pst(ctx, "ps_h", [P, 2, COLS])
        pd = pst(ctx, "ps_d", [P, 2, COLS])
        py = pst(ctx, "ps_y", [P, COLS])
        pt = pst(ctx, "ps_t", [P, 2, 512])
        pe_ = pst(ctx, "ps_e", [P, 512])
        with nc.Block() as ones:
            @ones.vector
            def _(dve):
                nc.vector.memset(xt[:, :, :, 64:65], 1.0)
                nc.vector.memset(yt[:, :, :, 64:65], 1.0)

        def copied(u, j):
            return 3 * u + j // 2 + 2

        with nc.Block() as block:
            @block.sync
            def _(sp):
                with sp.Fori(0, STRIPS) as s:
                    for n in range(N):
                        sp.wait_ge(S["ef_done"], first_unit(s, n) + LAST)
                        sp.dma_start(xs[:, n, :, :], x_in[n, :, bass.ds(s * SRP + 1, SRP), :]
                                     ).then_inc(S[f"in_loaded{n}"], 16)

            @block.tensor
            def _(pe):
                def turn(u, n, k, j):
                    sem = S["copied_dve"] if j % 2 == 0 else S["copied_act"]
                    pe.wait_ge(sem, copied(u, j) - 1)
                    if j == D0:
                        pe.wait_ge(S["dh_ready"], u + DONE)
                    src = {X: lambda: rows(xs, n, k).rearrange("p r w -> p (r w)"), Y: lambda: ys[:, k % 2, :],
                           G0: lambda: g[:, k % 2, 0, :], G1: lambda: g[:, k % 2, 1, :],
                           D0: lambda: dh[:, k % 2, 0, :], D1: lambda: dh[:, k % 2, 1, :]}[j]()
                    for b in range(4):
                        mm = nc.tensor.transpose(pt[:, j % 2, P * b:P * b + P], src[:, P * b:P * b + P], c("ident"))
                    mm.then_inc(S["turned"], 1)

                def hidden(s, n, k):
                    u = first_unit(s, n) + k
                    pe.wait_ge(S["zz_ready"], u - 1 + DONE)
                    hidden_on_pe(nc, pe, S, u, s, n, k, w1t, xs, ph)

                def project(s, n, k):
                    u = first_unit(s, n) + k
                    pe.wait_ge(S["gelu_ready"], u + DONE)
                    pe.wait_ge(S["y_ready"], u - 1 + DONE)
                    for par in range(2):
                        mm = nc.tensor.matmul(py[64 * par:64 * par + 64, :], prm[:, 64:128], g[:, k % 2, par, :],
                                              start=True, stop=True)
                    mm.then_inc(S["y_done"], 1)

                def back(s, n, k):
                    u = first_unit(s, n) + k
                    pe.wait_ge(S["y_ready"], u + DONE)
                    pe.wait_ge(S["dh_ready"], u - 1 + DONE)
                    for par in range(2):
                        hp = slice(64 * par, 64 * par + 64)
                        mm = nc.tensor.matmul(pd[:, par, :], w2b[hp, :], ys[hp, k % 2, :], start=True, stop=True)
                    mm.then_inc(S["d_done"], 1)

                def sums(s, n, k):
                    u = first_unit(s, n) + k
                    pe.wait_ge(S["copied_dve"], copied(u, D0))
                    pe.wait_ge(S["copied_act"], copied(u, D1))
                    if k == 0:
                        pe.wait_ge(S["summed"], s * N + n - 1 + DONE)
                    for par in range(2):
                        for b in range(4):
                            nc.tensor.matmul(pe_[:, 0:65], dt[:, par, b, :], xt[:, b, par, :],
                                             start=(k + par + b == 0), stop=False, skip_group_check=True)
                            mm = nc.tensor.matmul(pe_[:, 65:130], gt[:, par, b, :], yt[:, b, par, :], start=False,
                                                  stop=(k == UNITS - 1 and par == 1 and b == 3), skip_group_check=True)
                    mm.then_inc(S["ef_done"], 1)

                with pe.Fori(0, STRIPS) as s:
                    for i in range(BODY + 1):
                        a = divmod(i, UNITS)
                        if i < BODY:
                            hidden(s, *a)
                        if i >= 1:
                            z = divmod(i - 1, UNITS)
                            back(s, *z)
                            for j in (X, G0, G1, Y):
                                turn(first_unit(s, z[0]) + z[1], *z, j)
                        if i < BODY:
                            project(s, *a)
                        if i >= 1:
                            for j in (D0, D1):
                                turn(first_unit(s, z[0]) + z[1], *z, j)
                            sums(s, *z)

            def copy_turned(eng, copy, u, j):
                eng.wait_ge(S["turned"], 6 * u + j + 1)
                if j in (X, G0):
                    eng.wait_ge(S["ef_done"], u - 1 + DONE)
                blocks = pt[:, j % 2, :].rearrange("p (b c) -> p b c", b=4)
                if j in (X, Y):
                    dst = (xt if j == X else yt)[:, :, :, 0:64]
                    blocks = pt[:, j % 2, :].rearrange("p (b a c) -> p b a c", b=4, a=2)
                else:
                    dst = (gt if j in (G0, G1) else dt)[:, j in (G1, D1), :, :]
                copy(dst, blocks).then_inc(S["copied_dve"] if j % 2 == 0 else S["copied_act"], 1)

            @block.scalar
            def _(act):
                with act.Fori(0, STRIPS) as s:
                    for i in range(BODY + 1):
                        if i < BODY:
                            n, k = divmod(i, UNITS)
                            u = first_unit(s, n) + k
                            act.wait_ge(S["h_done"], u + DONE)
                            act.wait_ge(S["ef_done"], u + FREE)
                            nc.scalar.activation(g[:, k % 2, :, :], ph[:, :, :], ACT.Gelu, bias=bi[:, n:n + 1],
                                                 scale=sc[:, n:n + 1]).then_inc(S["gelu_ready"], 1)
                            act.wait_ge(S["dh_ready"], u + FREE)
                            for name, dst, func in (("z_ready", z, ACT.Identity), ("zz_ready", zz, ACT.Square)):
                                nc.scalar.activation(dst[:, k % 2, :, :], ph[:, :, :], func, bias=bi[:, n:n + 1],
                                                     scale=sc[:, n:n + 1]).then_inc(S[name], 1)
                            act.wait_ge(S["zz_ready"], u + DONE)
                            nc.scalar.activation(th[:, k % 2, :, :], zz[:, k % 2, :, :], ACT.Tanh, scale=0.25
                                                 ).then_inc(S["tanh_ready"], 1)
                            nc.scalar.activation(den[:, k % 2, :, :], zz[:, k % 2, :, :], ACT.Identity, bias=c("tiny")
                                                 ).then_inc(S["den_ready"], 1)
                            act.wait_ge(S["tanh_ready"], u + DONE)
                            nc.scalar.add(th[:, k % 2, :, :], th[:, k % 2, :, :], 1.0).then_inc(S["onep_ready"], 1)
                        if i >= 1:
                            n, k = divmod(i - 1, UNITS)
                            for j in (G0, Y, D1):
                                copy_turned(act, nc.scalar.copy, first_unit(s, n) + k, j)

            @block.gpsimd
            def _(pool):
                with pool.Fori(0, STRIPS) as s:
                    for n in range(N):
                        for k in range(UNITS):
                            u = first_unit(s, n) + k
                            pool.wait_ge(S["gelu_ready"], u + DONE)
                            pool.wait_ge(S["z_ready"], u + DONE)
                            pool.wait_ge(S["dh_ready"], u + FREE)
                            nc.gpsimd.tensor_tensor(gz[:, k % 2, :, :], g[:, k % 2, :, :], z[:, k % 2, :, :], ALU.mult
                                                    ).then_inc(S["gz_ready"], 1)
                            pool.wait_ge(S["slope_ready"], u + DONE)
                            nc.gpsimd.tensor_tensor(tail[:, k % 2, :, :], th[:, k % 2, :, :], z[:, k % 2, :, :], ALU.mult
                                                    ).then_inc(S["tail_ready"], 1)

            @block.vector
            def _(dve):
                def slope(u, k):
                    t, r, q = (a[:, k % 2, :, :] for a in (th, den, gz))
                    dve.wait_ge(S["onep_ready"], u + DONE)
                    nc.vector.reciprocal(t, t).then_inc(S["r1_ready"], 1)
                    dve.wait_ge(S["r1_ready"], u + DONE)
                    nc.vector.tensor_scalar(t, t, 2 * INV_SQRT_2PI, -INV_SQRT_2PI, ALU.mult, ALU.add
                                            ).then_inc(S["slope_ready"], 1)
                    dve.wait_ge(S["den_ready"], u + DONE)
                    nc.vector.reciprocal(r, r).then_inc(S["r2_ready"], 1)
                    dve.wait_ge(S["r2_ready"], u + DONE)
                    dve.wait_ge(S["gz_ready"], u + DONE)
                    nc.vector.scalar_tensor_tensor(q, q, TINY / 2, r, ALU.add, ALU.mult).then_inc(S["phi_ready"], 1)
                    dve.wait_ge(S["phi_ready"], u + DONE)
                    dve.wait_ge(S["tail_ready"], u + DONE)
                    dve.wait_ge(S["dh_ready"], u - 1 + DONE)
                    nc.vector.tensor_tensor(gp[:, :, :], q, tail[:, k % 2, :, :], ALU.add).then_inc(S["dgelu_ready"], 1)

                with dve.Fori(0, STRIPS) as s:
                    for i in range(BODY + 1):
                        if i >= 1:
                            n, k = divmod(i - 1, UNITS)
                            v = first_unit(s, n) + k
                            slope(v, k)
                            dve.wait_ge(S["d_done"], v + DONE)
                            dve.wait_ge(S["dgelu_ready"], v + DONE)
                            dve.wait_ge(S["ef_done"], v + FREE)
                            nc.vector.scalar_tensor_tensor(dh[:, k % 2, :, :].rearrange("p a c -> p (a c)"),
                                                           pd[:, :, :].rearrange("p a c -> p (a c)"), dbias[:, 0:1],
                                                           gp[:, :, :].rearrange("p a c -> p (a c)"),
                                                           ALU.add, ALU.mult).then_inc(S["dh_ready"], 1)
                            copy_turned(dve, nc.vector.tensor_copy, v, X)
                            copy_turned(dve, nc.vector.tensor_copy, v, G1)
                        if i < BODY:
                            n, k = divmod(i, UNITS)
                            u = first_unit(s, n) + k
                            dve.wait_ge(S["y_done"], u + DONE)
                            dve.wait_ge(S["ef_done"], u + FREE)
                            nc.vector.tensor_tensor(as_rows(ys[:, k % 2, :]), as_rows(py[:, :]), rows(xs, n, k), ALU.add
                                                    ).then_inc(S["y_ready"], 1)
                        if i >= 1:
                            n, k = divmod(i - 1, UNITS)
                            copy_turned(dve, nc.vector.tensor_copy, v, D0)
                            if k == UNITS - 1:
                                dve.wait_ge(S["ef_done"], v + DONE)
                                dve.wait_ge(S["summed"], s * N + n - 1 + DONE)
                                nc.vector.tensor_tensor(acc[:, n, :], acc[:, n, :], pe_[:, 0:130], ALU.add
                                                        ).then_inc(S["summed"], 1)


_INS = ["x"] + [f"L0_conv_{k}" for k in "pos_w pos_b ln1_g ln1_b qkv_w qkv_b lepe_w lepe_b wo_w wo_b ln2_g ln2_b fc1_w fc1_b pw_w dw_w dw_b fc2_w fc2_b".split()] + [
    f"L1_conv_{k}" for k in "w1 gn_w gn_b w2 g1_w g1_b g2_w g2_b running_mean running_var residual_scale".split()]


def kernel(**inputs):
    import concourse.bacc as _bacc
    from concourse import mybir as _mybir
    from concourse.bass_utils import run_bass_kernel_spmd as _run

    nc = _bacc.Bacc("TRN2", target_bir_lowering=False, num_devices=1)
    arrays, args = {}, {}
    for name in _INS:
        a = np.ascontiguousarray(inputs[name])
        arrays[f"in_{name}"] = a
        args[name.replace("L0_conv_", "").replace("L1_conv_", "m_")] = nc.dram_tensor(
            f"in_{name}", a.shape, _mybir.dt.from_np(a.dtype), kind="ExternalInput").ap()
    cst, _ = constants()
    arrays["in_constants"] = cst
    args["cst"] = nc.dram_tensor("in_constants", cst.shape, _mybir.dt.float32, kind="ExternalInput").ap()
    out = nc.dram_tensor("out_image", [N, C, H, W], _mybir.dt.float32, kind="ExternalOutput").ap()
    build(nc, args, out)
    r = _run(nc, [arrays], core_ids=[0])
    return r.results[0]["out_image"]
```

```python
import numpy as np
import concourse.bass as bass
from concourse import mybir
from contextlib import ExitStack

N, C, H, W, D = 2, 64, 256, 256, 2
P = 128
RP = H // 2
SRP = 4
STRIPS = RP // SRP
UNIT = 2
UNITS = SRP // UNIT
COLS = UNIT * W
PADW = W + 4
HEADS, TOPK, SUB, NW = 8, 4, 16, 8
WINDOWS = NW * NW
WRP, WW = RP // NW, W // NW
WPIX = WRP * WW
KEYS = TOPK * SUB
LN_EPS, GN_EPS = 1e-6, 1e-5
HID, GROUP = 128, 16
PIX = H * W
TINY = 1e-30
INV_SQRT_2PI = 0.3989422804014327
DEVIATION_MAX = (3.4028234e38 / (GROUP * PIX)) ** 0.5
LR, MOM, STEPS = 0.01, 0.9, 2

fp32 = mybir.dt.float32
u32 = mybir.dt.uint32
ALU = mybir.AluOpType
ACT = mybir.ActivationFunctionType
AX = mybir.AxisListType


def constants():
    p = np.arange(P)
    eye = np.eye(P)
    half = (p[:, None] // 64 == p[None, :] // 64)
    col = np.arange(512)
    parts = {
        "ident": eye,
        "ident2": np.vstack([np.eye(64)] * 2),
        "center": eye - half / 64.0,
        "mean": half / 64.0,
        "pairmean": np.vstack([np.eye(64)] * 2) / 64.0,
        "group": (p[:, None] // GROUP == p[None, :] // GROUP) * 1.0,
        "headmask": np.vstack([(p[:64, None] // 8 == col[None, :] // 64)] * 2) * 1.0,
        "vmask": (col[None, :64] % 16 // 8 == p[:, None] // 64) * 1.0,
        "expand": 16.0 * (p[:, None] == (p[None, :] // SUB) % TOPK) + (p[:, None] == 8) * (p[None, :] % SUB),
        "pair": np.tile(np.eye(64), (2, 2)),
        "eps": np.full((P, 1), LN_EPS),
        "tiny": np.full((P, 1), TINY),
        "log_peak": np.full((P, 1), np.log(INV_SQRT_2PI)),
        "minus": -1.0 * (p[:, None] - 96 == col[None, :] // 64),
    }
    at, n = {}, 0
    for name, a in parts.items():
        at[name] = (n, n + a.shape[1])
        n += a.shape[1]
    return np.ascontiguousarray(np.hstack(list(parts.values())).astype(np.float32)), at


def build(nc, I, out):
    ctx = ExitStack()
    with ctx:
        build_in(nc, I, out, ctx)


class Link:

    def __init__(self, nc, sem, eng):
        self.sem, self.eng, self.n = sem, eng, 0

    def __call__(self, ins):
        ins.then_inc(self.sem, 1)
        self.n += 1
        self.eng.wait_ge(self.sem, self.n)


def build_in(nc, I, out, ctx):
    _, at = constants()

    def sem(name):
        return ctx.enter_context(nc.semaphore(name))

    def dram(name, shape):
        return nc.dram_tensor(name, shape, fp32, kind="Internal").ap()

    taken = {}

    def fresh(name):
        taken[name] = taken.get(name, 0) + 1
        return f"{name}_{taken[name]}"

    def sbt(c, name, shape, dt=fp32):
        return c.enter_context(nc.sbuf_tensor(fresh(name), shape, dt))

    def pst(c, name, shape):
        return c.enter_context(nc.psum_tensor(fresh(name), shape, fp32))

    def clear(*sems, start={}):
        with nc.Block() as reset:
            @reset.gpsimd
            def _(pool):
                for s in sems:
                    pool.sem_clear(s)
                for s, v in start.items():
                    pool.sem_inc(s, v)

    IMG = dram("IMG", [D + 1, N, P, RP + 2, W])
    X1 = dram("X1", [N, P, RP, W])
    XH = dram("XH", [N, P, RP + 2, W])
    AO = dram("AO", [N, P, RP, W])
    X2 = dram("X2", [N, P, RP, W])
    XH2 = dram("XH2", [N, P, RP + 2, W])
    POOL = dram("POOL", [N, P, STRIPS, W // 8])
    TAB = [dram(f"TAB{n}", [WINDOWS * SUB, P]) for n in range(N)]
    IDX = nc.dram_tensor("IDX", [N, WINDOWS, P], u32, kind="Internal").ap()
    AW = dram("AW", [N, WINDOWS, 64, 512])
    VW = dram("VW", [N, WINDOWS, P, 256])
    STAT = dram("STAT", [N, P, STRIPS, UNITS * 6])

    cst = sbt(ctx, "cst", [P, I["cst"].shape[1]])

    def c(name, p0=0, p1=P):
        return cst[p0:p1, at[name][0]:at[name][1]]

    ident = c("ident")
    s_init = sem("s_init")

    with ExitStack() as ph:
        zero = sbt(ph, "zero", [P, W])
        zeroed = sem("zeroed")
        with nc.Block() as block:
            @block.vector
            def _(dve):
                nc.vector.memset(zero[:, :], 0.0).then_inc(zeroed, 1)

            @block.sync
            def _(sp):
                k = 1
                sp.dma_start(cst[:, :], I["cst"]).then_inc(s_init, 16)
                xv = I["x"].rearrange("n c (r p) w -> n p c r w", p=2)
                for n in range(N):
                    for p in range(2):
                        sp.dma_start(IMG[0, n, 64 * p:64 * p + 64, 1:RP + 1, :], xv[n, p]).then_inc(s_init, 16)
                        k += 1
                sp.wait_ge(zeroed, 1)
                for n in range(N):
                    for a in [IMG[d, n] for d in range(D + 1)] + [XH[n], XH2[n]]:
                        for r in (0, RP + 1):
                            sp.dma_start(a[:, r, :], zero[:, :]).then_inc(s_init, 16)
                            k += 1
                sp.wait_ge(s_init, 16 * k)

    layer0(nc, I, sem, sbt, pst, clear, c, IMG, X1, XH, AO, X2, XH2, POOL, TAB, IDX, AW, VW)
    layer1(nc, I, sem, sbt, pst, clear, c, IMG, STAT, out)


def layer0(nc, I, sem, sbt, pst, clear, c, IMG, X1, XH, AO, X2, XH2, POOL, TAB, IDX, AW, VW):
    ident = c("ident")
    ctx = ExitStack()
    ctx.__enter__()
    posm = sbt(ctx, "posm", [P, 2, 3, P])
    posb = sbt(ctx, "posb", [P, 1])
    lepm = sbt(ctx, "lepm", [P, 3, 5, P])
    glum = sbt(ctx, "glum", [P, 2, 2, 3, HID])
    wn = sbt(ctx, "wn", [P, 448])
    wt = sbt(ctx, "wt", [P, 5, 2, 64])
    wod = sbt(ctx, "wod", [P, P])
    gvm = sbt(ctx, "gvm", [P, 2, HID])
    attb = sbt(ctx, "attb", [P, 1])
    fc2 = sbt(ctx, "fc2", [HID, 64])
    fc2b = sbt(ctx, "fc2b", [P, 1])
    dwb = sbt(ctx, "dwb", [HID, 1])
    w_loaded, link = sem("w_loaded"), sem("link")
    S = {k: sem(k) for k in """in_loaded0 in_loaded1 out_stored0 out_stored1
        conv_done x_ready centred squared var_done sd_ready rstd_ready xhat_ready plus_ready pooled_ready
        scored max_ready max_turned max_copied shifted probs_ready av_done recip_ready attn_ready
        idx_loaded0 idx_loaded1 rows_known k_turned k_masked a_done a_copied v_masked
        xbranch_done vbranch_done gelu_ready gated fc2_done out_ready""".split()}
    gathered = [sem(f"gathered{n}") for n in range(N)]
    allsems = [w_loaded, link, *S.values()]

    with nc.Fori(0, D) as d:
        weights(nc, I, d, sbt, pst, clear, c, w_loaded, link, allsems,
                posm, posb, lepm, glum, gvm, wn, wt, wod, attb, fc2, fc2b, dwb)
        positional(nc, d, sbt, pst, clear, c, S, allsems, posm, posb, IMG, X1, XH, POOL)
        for n in range(N):
            routing(nc, n, sbt, pst, clear, c, w_loaded, link, wn, POOL, TAB, IDX)
        matrices(nc, d, sbt, pst, clear, c, S, allsems, gathered, wt, TAB, IDX, AW, VW)
        attention(nc, sbt, pst, clear, c, S, allsems, XH, AW, VW, AO)
        mixing(nc, sbt, pst, clear, c, S, allsems, lepm, wod, attb, XH, AO, X1, X2, XH2)
        glu(nc, d, sbt, pst, clear, c, S, allsems, glum, gvm, fc2, fc2b, dwb, XH2, X2, IMG)
    ctx.close()


def weights(nc, I, d, sbt, pst, clear, c, w_loaded, link, allsems,
            posm, posb, lepm, glum, gvm, wn, wt, wod, attb, fc2, fc2b, dwb):
    ident = c("ident")
    MS = [64, 64, 64, 128, 128]
    AT = [0, 64, 128, 192, 320]
    clear(*allsems)
    with ExitStack() as ph:
        raw = sbt(ph, "raw", [64, 448])
        wg = sbt(ph, "wg", [64, 448])
        lng = sbt(ph, "lng", [64, 2])
        lnb = sbt(ph, "lnb", [64, 2])
        bias = sbt(ph, "bias", [P, 5])
        sh = sbt(ph, "sh", [P, 5])
        rs = sbt(ph, "rs", [P, 5])
        posw = sbt(ph, "posw", [P, 9])
        lepw = sbt(ph, "lepw", [64, 25])
        lepb = sbt(ph, "lepb", [64, 1])
        wo2 = sbt(ph, "wo2", [64, 2, 64])
        wob = sbt(ph, "wob", [P, 1])
        lrhs = sbt(ph, "lrhs", [64, 32, 64])
        lt = sbt(ph, "lt", [P, 32, 64])
        pw = sbt(ph, "pw", [P, P])
        pwt = sbt(ph, "pwt", [P, P])
        wpt = sbt(ph, "wpt", [P, P])
        dw = sbt(ph, "dw", [P, 9])
        dwd = sbt(ph, "dwd", [P, 9, P])
        w9 = sbt(ph, "w9", [P, 9, P])
        ps = pst(ph, "ps_w", [P, 8, 512])

        with nc.Block() as load:
            @load.gpsimd
            def _(pool):
                pool.memset(wod[:, :], 0.0).then_inc(link, 1)
                pool.memset(posm[:, :, :, :], 0.0)
                pool.memset(lepm[:, :, :, :], 0.0)
                pool.memset(glum[:, :, :, :, :], 0.0)
                pool.memset(gvm[:, :, :], 0.0)
                pool.memset(lrhs[:, :, :], 0.0)
                pool.memset(bias[:, :], 0.0)
                pool.memset(sh[:, :], 0.0)
                pool.memset(wt[:, :, :, :], 0.0).then_inc(link, 1)

            @load.sync
            def _(sp):
                k = [0]

                def get(dst, src):
                    sp.dma_start(dst, src).then_inc(w_loaded, 16)
                    k[0] += 1

                def column(name, a=0, b=None):
                    v = I[name][d, a:b] if b else I[name][d]
                    return v.rearrange("(c o) -> c o", o=1)

                get(raw[:, 0:192], I["qkv_w"][d])
                get(raw[:, 192:448], I["fc1_w"][d])
                for i in range(2):
                    get(lng[:, i:i + 1], column(f"ln{i + 1}_g"))
                    get(lnb[:, i:i + 1], column(f"ln{i + 1}_b"))
                get(lepw[:, :], I["lepe_w"][d].rearrange("c o a b -> c (o a b)"))
                get(lepb[:, :], column("lepe_b"))
                get(pw[:, :], I["pw_w"][d].rearrange("o i a b -> o (i a b)"))
                get(dw[:, :], I["dw_w"][d].rearrange("c o a b -> c (o a b)"))
                get(dwb[:, :], column("dw_b"))
                get(fc2[:, :], I["fc2_w"][d])
                for h in range(2):
                    hp = slice(64 * h, 64 * h + 64)
                    get(posw[hp, :], I["pos_w"][d].rearrange("c o a b -> c (o a b)"))
                    get(posb[hp, :], column("pos_b"))
                    get(wob[hp, :], column("wo_b"))
                    get(fc2b[hp, :], column("fc2_b"))
                    get(wo2[:, h, :], I["wo_w"][d])
                sp.wait_ge(link, 2)
                for h in range(2):
                    for j in range(4):
                        q = 32 * j + 16 * h
                        get(wod[q:q + 16, 64 * h:64 * h + 64], I["wo_w"][d, 16 * j:16 * j + 16, :])
                for i in range(5):
                    src = column("qkv_b", AT[i], AT[i] + 64) if i < 3 else column("fc1_b", 128 * (i - 3), 128 * (i - 2))
                    get(bias[0:MS[i], i:i + 1], src)
                sp.wait_ge(w_loaded, 16 * k[0])

        clear(link)
        with nc.Block() as fold:
            @fold.vector
            def _(dve):
                step = Link(nc, link, dve)
                nc.vector.tensor_scalar(wg[:, 0:192], raw[:, 0:192], lng[:, 0:1], None, ALU.mult)
                nc.vector.tensor_scalar(wg[:, 192:448], raw[:, 192:448], lng[:, 1:2], None, ALU.mult)
                nc.vector.tensor_tensor(lrhs[:, 0:25, :], wo2[:, 0:1, :].to_broadcast([64, 25, 64]),
                                        lepw[:, :, None].to_broadcast([64, 25, 64]), ALU.mult)
                nc.vector.tensor_tensor(dwd[:, :, :], ident[:, None, :].to_broadcast([P, 9, P]),
                                        dw[:, :, None].to_broadcast([P, 9, P]), ALU.mult)
                step(nc.vector.tensor_scalar_add(posw[:, 4:5], posw[:, 4:5], 1.0))
                for j in range(2):
                    hp = slice(64 * j, 64 * j + 64)
                    for g in range(2):
                        for par in range(2):
                            t = 2 * g + j - par
                            if 0 <= t < 3:
                                nc.vector.tensor_tensor(
                                    posm[hp, g, :, 64 * par:64 * par + 64],
                                    c("ident2")[hp, None, :].to_broadcast([64, 3, 64]),
                                    posw[hp, 3 * t:3 * t + 3, None].to_broadcast([64, 3, 64]), ALU.mult)

        with nc.Block() as turn:
            @turn.tensor
            def _(pe):
                for i in range(5):
                    w = slice(AT[i], AT[i] + MS[i])
                    nc.tensor.transpose(ps[0:MS[i], 0, 64 * i:64 * i + 64], wg[:, w], ident[0:64, 0:64])
                    nc.tensor.matmul(ps[0:MS[i], 1, i:i + 1], raw[:, w], lnb[:, (i > 2):(i > 2) + 1],
                                     start=True, stop=True)
                nc.tensor.matmul(ps[:, 2, 0:1], wo2[:, :, :].rearrange("c a o -> c (a o)"), lepb[:, :],
                                 start=True, stop=True)
                nc.tensor.transpose(ps[:, 3, 0:P], pw[:, :], ident)

        clear(link)
        with nc.Block() as tilde:
            @tilde.vector
            def _(dve):
                step = Link(nc, link, dve)
                nc.vector.tensor_copy(pwt[:, :], ps[:, 3, 0:P])
                nc.vector.tensor_tensor(attb[:, :], ps[:, 2, 0:1], wob[:, :], ALU.add)
                for i in range(5):
                    m = slice(0, MS[i])
                    step(nc.vector.reduce_sum(rs[m, i:i + 1], ps[m, 0, 64 * i:64 * i + 64], AX.X))
                    step(nc.vector.tensor_tensor(sh[m, i:i + 1], ps[m, 1, i:i + 1], rs[m, i:i + 1], ALU.subtract))
                    step(nc.vector.tensor_tensor(sh[m, i:i + 1], sh[m, i:i + 1], bias[m, i:i + 1], ALU.add))
                    step(nc.vector.tensor_scalar_mul(sh[m, i:i + 1], sh[m, i:i + 1], 1.0 / C))
                    for b in range(2):
                        nc.vector.tensor_scalar(wt[m, i, b, :], ps[m, 0, 64 * i:64 * i + 64], sh[m, i:i + 1],
                                                C ** -0.5 if i == 0 else 1.0, ALU.add, ALU.mult)

        with nc.Block() as back:
            @back.tensor
            def _(pe):
                for i in range(5):
                    nc.tensor.transpose(ps[:, 0, AT[i]:AT[i] + MS[i]],
                                        wt[0:MS[i], i, :, :].rearrange("m a c -> m (a c)"), ident[0:MS[i], 0:MS[i]])
                for q in range(4):
                    nc.tensor.matmul(ps[:, 1 + q, :], wt[0:64, 2, :, :].rearrange("m a c -> m (a c)"),
                                     lrhs[:, 8 * q:8 * q + 8, :].rearrange("c t o -> c (t o)"), start=True, stop=True)
                nc.tensor.matmul(ps[:, 5, 0:P], pwt[:, :], wt[:, 3, :, :].rearrange("m a c -> m (a c)"),
                                 start=True, stop=True)

        with nc.Block() as keep:
            @keep.vector
            def _(dve):
                nc.vector.tensor_copy(wn[:, :], ps[:, 0, 0:448])
                nc.vector.tensor_copy(wpt[:, :], ps[:, 5, 0:P])

            @keep.scalar
            def _(act):
                for q in range(4):
                    nc.scalar.copy(lt[:, 8 * q:8 * q + 8, :], ps[:, 1 + q, :].rearrange("p (t o) -> p t o", t=8))

        with nc.Block() as taps:
            @taps.tensor
            def _(pe):
                for t in range(3):
                    nc.tensor.matmul(ps[:, t, 0:384], wpt[:, :],
                                     dwd[:, 3 * t:3 * t + 3, :].rearrange("p t o -> p (t o)"), start=True, stop=True)

            @taps.vector
            def _(dve):
                for j in range(2):
                    hp = slice(64 * j, 64 * j + 64)
                    for g in range(3):
                        for par in range(2):
                            t = 2 * g + j - par
                            if 0 <= t < 5:
                                nc.vector.tensor_copy(lepm[hp, g, :, 64 * par:64 * par + 64],
                                                      lt[hp, 5 * t:5 * t + 5, :])

        with nc.Block() as place:
            @place.vector
            def _(dve):
                for j in range(2):
                    hp = slice(64 * j, 64 * j + 64)
                    nc.vector.tensor_copy(gvm[hp, j, :], wn[hp, 320:448])
                    for par in range(2):
                        for gi in range(2):
                            t = 2 * (gi - 1 + par) + j - par + 1
                            if 0 <= t < 3:
                                nc.vector.tensor_copy(glum[hp, par, gi, :, :],
                                                      ps[hp, t, 0:384].rearrange("p (x o) -> p x o", x=3))


BODY = N * UNITS
DONE, FREE, LAST = BODY + 1, BODY - 1, UNITS
UNIT_SEMS = "rstd_ready conv_done x_ready centred squared var_done sd_ready xhat_ready plus_ready fc2_done out_ready".split()


def first_unit(s, n):
    return s * BODY + n * UNITS


def run_strips(sp, load, store):
    for n in range(N):
        load(0, n)
    with sp.Fori(0, STRIPS - 1) as s:
        for n in range(N):
            load(s + 1, n)
            store(s, n)
    for n in range(N):
        store(STRIPS - 1, n)


def rows(t, n, k):
    return t[:, n, UNIT * k:UNIT * k + UNIT, :]


def as_rows(a):
    return a.rearrange("p (r w) -> p r w", w=W)


def norm_on_pe(nc, pe, c, S, u, x, sq, pc, pv, n, k, step):
    if step == "centre":
        pe.wait_ge(S["x_ready"], u + DONE)
        pe.wait_ge(S["xhat_ready"], u + FREE)
        nc.tensor.matmul(pc[:, k % 2, :], c("center"), rows(x, n, k), start=True, stop=True).then_inc(S["centred"], 1)
    else:
        pe.wait_ge(S["squared"], u + DONE)
        pe.wait_ge(S["sd_ready"], u + FREE)
        nc.tensor.matmul(pv[:, k % 2, :], c("mean"), sq[:, k % 2, :], start=True, stop=True).then_inc(S["var_done"], 1)


def norm_on_dve(nc, dve, S, u, k, sd, rstd, xr, pc):
    dve.wait_ge(S["sd_ready"], u + DONE)
    dve.wait_ge(S["plus_ready"], u + FREE)
    nc.vector.reciprocal(rstd[:, k % 2, :], sd[:, k % 2, :]).then_inc(S["rstd_ready"], 1)
    dve.wait_ge(S["rstd_ready"], u + DONE)
    nc.vector.tensor_tensor(xr[:, k % 2, :], pc[:, k % 2, :], rstd[:, k % 2, :], ALU.mult).then_inc(S["xhat_ready"], 1)


def sqrt_on_act(nc, act, S, u, k, sd, pv, eps):
    act.wait_ge(S["var_done"], u + DONE)
    act.wait_ge(S["xhat_ready"], u + FREE)
    nc.scalar.activation(sd[:, k % 2, :], pv[:, k % 2, :], ACT.Sqrt, bias=eps).then_inc(S["sd_ready"], 1)


def square_on_act(nc, act, S, u, k, sq, pc):
    act.wait_ge(S["centred"], u + DONE)
    act.wait_ge(S["var_done"], u + FREE)
    nc.scalar.activation(sq[:, k % 2, :], pc[:, k % 2, :], ACT.Square).then_inc(S["squared"], 1)


def plus_on_act(nc, act, S, u, k, n, xr, xh):
    act.wait_ge(S["xhat_ready"], u + DONE)
    nc.scalar.add(rows(xh, n, k), as_rows(xr[:, k % 2, :]), 1.0).then_inc(S["plus_ready"], 1)


def positional(nc, d, sbt, pst, clear, c, S, allsems, posm, posb, IMG, X1, XH, POOL):
    clear(*allsems, start={**{S[k]: BODY for k in UNIT_SEMS}, S["out_stored0"]: 48, S["out_stored1"]: 48})
    with ExitStack() as ph:
        xs = sbt(ph, "p_xs", [P, N, SRP + 1, PADW])
        x1 = sbt(ph, "p_x1", [P, N, SRP, W])
        sq = sbt(ph, "p_sq", [P, 2, COLS])
        sd = sbt(ph, "p_sd", [P, 2, COLS])
        rstd = sbt(ph, "p_rstd", [P, 2, COLS])
        xr = sbt(ph, "p_xr", [P, 2, COLS])
        xh = sbt(ph, "p_xh", [P, N, SRP, W])
        pooled = sbt(ph, "p_pool", [P, N, W // 8])
        px = pst(ph, "ps_x", [P, 2, COLS])
        pc = pst(ph, "ps_c", [P, 2, COLS])
        pv = pst(ph, "ps_v", [P, 2, COLS])
        with nc.Block() as border:
            @border.vector
            def _(dve):
                nc.vector.memset(xs[:, :, :, 0:2], 0.0)
                nc.vector.memset(xs[:, :, :, PADW - 2:PADW], 0.0)

        with nc.Block() as block:
            @block.sync
            def _(sp):
                def load(s, n):
                    sp.wait_ge(S["conv_done"], first_unit(s, n) + LAST)
                    for j in range(2):
                        sp.dma_start(xs[64 * j:64 * j + 64, n, :, 2:2 + W],
                                     IMG[d, n, 64 - 64 * j:128 - 64 * j, bass.ds(s * SRP + j, SRP + 1), :]
                                     ).then_inc(S[f"in_loaded{n}"], 16)

                def store(s, n):
                    sp.wait_ge(S["x_ready"], first_unit(s, n) + UNITS - 1 + DONE)
                    sp.dma_start(X1[n, :, bass.ds(s * SRP, SRP), :], x1[:, n, :, :]).then_inc(S[f"out_stored{n}"], 16)
                    sp.wait_ge(S["plus_ready"], first_unit(s, n) + UNITS - 1 + DONE)
                    sp.dma_start(XH[n, :, bass.ds(s * SRP + 1, SRP), :], xh[:, n, :, :]).then_inc(S[f"out_stored{n}"], 16)
                    sp.wait_ge(S["pooled_ready"], s * N + n + 1)
                    sp.dma_start(POOL[n, :, s, :], pooled[:, n, :]).then_inc(S[f"out_stored{n}"], 16)

                run_strips(sp, load, store)
                for n in range(N):
                    sp.wait_ge(S[f"out_stored{n}"], 48 * (STRIPS + 1))

            @block.tensor
            def _(pe):
                def conv(s, n, k):
                    u = first_unit(s, n) + k
                    if k == 0:
                        pe.wait_ge(S[f"in_loaded{n}"], s * 32 + 32)
                    pe.wait_ge(S["x_ready"], u + FREE)
                    for g in range(2):
                        for dx in range(3):
                            mm = nc.tensor.matmul(px[:, k % 2, :], posm[:, g, dx, :],
                                                  xs[:, n, UNIT * k + g:UNIT * k + g + UNIT, 1 + dx:1 + dx + W],
                                                  start=(g + dx == 0), stop=(g == 1 and dx == 2))
                    mm.then_inc(S["conv_done"], 1)

                with pe.Fori(0, STRIPS) as s:
                    for i in range(BODY + 2):
                        if i < BODY:
                            conv(s, i // UNITS, i % UNITS)
                        for back, step in ((1, "centre"), (2, "var")):
                            if 0 <= i - back < BODY:
                                n, k = divmod(i - back, UNITS)
                                norm_on_pe(nc, pe, c, S, first_unit(s, n) + k, x1, sq, pc, pv, n, k, step)

            @block.scalar
            def _(act):
                with act.Fori(0, STRIPS) as s:
                    for i in range(BODY + 3):
                        if i < BODY:
                            n, k = divmod(i, UNITS)
                            u = first_unit(s, n) + k
                            act.wait_ge(S["conv_done"], u + DONE)
                            if k == 0:
                                act.wait_ge(S[f"out_stored{n}"], s * 48 + 48)
                            nc.scalar.activation(rows(x1, n, k), as_rows(px[:, k % 2, :]), ACT.Identity,
                                                 bias=posb[:, 0:1]).then_inc(S["x_ready"], 1)
                        if 0 <= i - 1 < BODY:
                            n, k = divmod(i - 1, UNITS)
                            square_on_act(nc, act, S, first_unit(s, n) + k, k, sq, pc)
                        if 0 <= i - 2 < BODY:
                            n, k = divmod(i - 2, UNITS)
                            sqrt_on_act(nc, act, S, first_unit(s, n) + k, k, sd, pv, c("eps"))
                        if 0 <= i - 3 < BODY:
                            n, k = divmod(i - 3, UNITS)
                            plus_on_act(nc, act, S, first_unit(s, n) + k, k, n, xr, xh)

            @block.vector
            def _(dve):
                with dve.Fori(0, STRIPS) as s:
                    for n in range(N):
                        for k in range(UNITS):
                            norm_on_dve(nc, dve, S, first_unit(s, n) + k, k, sd, rstd, xr, pc)
                    for n in range(N):
                        dve.wait_ge(S["plus_ready"], first_unit(s, n) + UNITS - 1 + DONE)
                        dve.wait_ge(S[f"out_stored{n}"], s * 48 + 48)
                        nc.vector.tensor_reduce(pooled[:, n, :], xh[:, n, :, :].rearrange("p r (b x) -> p b r x", x=8),
                                                AX.XY, ALU.add).then_inc(S["pooled_ready"], 1)



def routing(nc, n, sbt, pst, clear, c, w_loaded, link, wn, POOL, TAB, IDX):
    ident = c("ident")
    with ExitStack() as ph:
        sums = sbt(ph, "r_sums", [P, 1024])
        pm = sbt(ph, "r_pm", [64, WINDOWS, SUB])
        win = sbt(ph, "r_win", [64, WINDOWS])
        tab = sbt(ph, "r_tab", [P, 8, P])
        qk = sbt(ph, "r_qk", [64, 2, WINDOWS])
        lg = sbt(ph, "r_lg", [64, WINDOWS])
        top = sbt(ph, "r_top", [64, 8])
        best = sbt(ph, "r_best", [64, 8], u32)
        bestf = sbt(ph, "r_bestf", [64, 8])
        bt = sbt(ph, "r_bt", [P, WINDOWS])
        idx = sbt(ph, "r_idx", [WINDOWS, P], u32)
        ps = pst(ph, "ps_r", [P, 8, 512])
        clear(w_loaded)
        with nc.Block() as load:
            @load.sync
            def _(sp):
                sp.dma_start(sums[:, :], POOL[n].rearrange("p s b -> p (s b)")).then_inc(w_loaded, 16)
                sp.wait_ge(w_loaded, 16)

            @load.gpsimd
            def _(pool):
                pool.memset(bt[:, :], 1.0)
        with nc.Block() as mean:
            @mean.tensor
            def _(pe):
                for h in range(2):
                    nc.tensor.matmul(ps[0:64, h, :], c("pairmean"), sums[:, 512 * h:512 * h + 512], start=True, stop=True)
        clear(link)
        with nc.Block() as sort:
            @sort.vector
            def _(dve):
                step = Link(nc, link, dve)
                for wy in range(NW):
                    src = ps[0:64, wy // 4, 128 * (wy % 4):128 * (wy % 4) + 128]
                    ins = nc.vector.tensor_copy(
                        pm[:, NW * wy:NW * wy + NW, :].rearrange("c w (y x) -> c w y x", x=4),
                        src.rearrange("c (y w x) -> c w y x", y=4, x=4))
                    step(ins)
                step(nc.vector.reduce_sum(win[:, :], pm[:, :, :], AX.X))
                nc.vector.tensor_scalar_mul(win[:, :], win[:, :], 1.0 / SUB)
        with nc.Block() as project:
            @project.tensor
            def _(pe):
                rows_of = pm[:, :, :].rearrange("c w s -> c (w s)")
                for i in range(8):
                    nc.tensor.matmul(ps[:, i // 4, P * (i % 4):P * (i % 4) + P], rows_of[:, P * i:P * i + P],
                                     wn[0:64, 64:192], start=True, stop=True)
                for i in range(2):
                    nc.tensor.matmul(ps[0:64, 2 + i, 0:WINDOWS], wn[0:64, 64 * i:64 * i + 64], win[:, :],
                                     start=True, stop=True)
        clear(w_loaded)
        with nc.Block() as keep:
            @keep.vector
            def _(dve):
                for i in range(2):
                    nc.vector.tensor_copy(tab[:, 4 * i:4 * i + 4, :], ps[:, i, :].rearrange("p (t c) -> p t c", t=4))
                    nc.vector.tensor_copy(qk[:, i, :], ps[0:64, 2 + i, 0:WINDOWS])
        with nc.Block() as logits:
            @logits.sync
            def _(sp):
                sp.dma_start(TAB[n].rearrange("(t p) c -> p t c", p=P), tab[:, :, :]).then_inc(w_loaded, 16)
                sp.wait_ge(w_loaded, 16)

            @logits.tensor
            def _(pe):
                nc.tensor.matmul(ps[0:64, 4, 0:WINDOWS], qk[:, 0, :], qk[:, 1, :], start=True, stop=True)
        clear(link)
        with nc.Block() as choose:
            @choose.vector
            def _(dve):
                step = Link(nc, link, dve)
                step(nc.vector.tensor_copy(lg[:, :], ps[0:64, 4, 0:WINDOWS]))
                step(nc.vector.max(top[:, :], lg[:, :]))
                step(nc.vector.max_index(best[:, :], top[:, :], lg[:, :]))
                nc.vector.tensor_copy(bestf[:, :], best[:, :])
        with nc.Block() as turn:
            @turn.tensor
            def _(pe):
                nc.tensor.transpose(ps[0:8, 5, 0:64], bestf[:, :], ident[0:64, 0:64])
        with nc.Block() as keep_turned:
            @keep_turned.vector
            def _(dve):
                nc.vector.tensor_copy(bt[0:8, :], ps[0:8, 5, 0:64])
        with nc.Block() as expand:
            @expand.tensor
            def _(pe):
                nc.tensor.matmul(ps[0:WINDOWS, 6, 0:P], bt[:, :], c("expand"), start=True, stop=True)
        with nc.Block() as number:
            @number.vector
            def _(dve):
                nc.vector.tensor_copy(idx[:, :], ps[0:WINDOWS, 6, 0:P])
        clear(w_loaded)
        with nc.Block() as store:
            @store.sync
            def _(sp):
                sp.dma_start(IDX[n], idx[:, :]).then_inc(w_loaded, 16)
                sp.wait_ge(w_loaded, 16)


def matrices(nc, d, sbt, pst, clear, c, S, allsems, gathered, wt, TAB, IDX, AW, VW):
    per_window = "k_turned k_masked a_done a_copied v_masked".split()
    clear(*allsems, start={**{S[k]: N for k in per_window},
                           **{S[f"out_stored{n}"]: 32 for n in range(N)}})
    with ExitStack() as ph:
        idc = sbt(ph, "m_idc", [P, N, 1], u32)
        kv = [sbt(ph, f"m_kv{n}", [P, P]) for n in range(N)]
        kb = sbt(ph, "m_kb", [64, N, 512])
        aw = sbt(ph, "m_aw", [64, N, 512])
        vw = sbt(ph, "m_vw", [P, N, 2, 4, 32])
        pk = pst(ph, "ps_k", [P, N, 512])
        pa = pst(ph, "ps_a", [P, N, 512])
        idx1 = [sbt(ph, f"m_idx{n}", [P, 1], u32) for n in range(N)]
        with nc.Block() as zero:
            @zero.vector
            def _(dve):
                nc.vector.memset(vw[:, :, :, :, :], 0.0)

        with nc.Block() as block:
            @block.sync
            def _(sp):
                with sp.Fori(0, WINDOWS) as w:
                    for n in range(N):
                        sp.wait_ge(S["k_turned"], w * N + n + 1)
                        sp.dma_start(idx1[n][:, :], IDX[n, w].rearrange("(p o) -> p o", o=1)).then_inc(S[f"idx_loaded{n}"], 16)

            @block.gpsimd
            def _(pool):
                with pool.Fori(0, WINDOWS) as w:
                    for n in range(N):
                        pool.wait_ge(S["v_masked"], w * N + n + 1)
                        pool.wait_ge(S["k_turned"], w * N + n + 1)
                        pool.wait_ge(S[f"idx_loaded{n}"], w * 16 + 16)
                        pool.sem_inc(S["rows_known"], 1)
                        pool.indirect_dma_start(kv[n][:, :], None, TAB[n],
                                                bass.IndirectOffsetOnAxis(ap=idx1[n][:, 0:1], axis=0)
                                                ).then_inc(gathered[n], 16)

            @block.tensor
            def _(pe):
                with pe.Fori(0, WINDOWS) as w:
                    for n in range(N):
                        pe.wait_ge(gathered[n], (d * WINDOWS + w) * 16 + 16)
                        pe.wait_ge(S["k_masked"], w * N + n + 1)
                        nc.tensor.transpose(pk[:, n, 0:P], kv[n][:, :], c("ident")).then_inc(S["k_turned"], 1)
                    for n in range(N):
                        pe.wait_ge(S["k_masked"], w * N + n + 1 + N)
                        pe.wait_ge(S["a_copied"], w * N + n + 1)
                        nc.tensor.matmul(pa[:, n, :], wt[0:64, 0, :, :].rearrange("m a c -> m (a c)"), kb[:, n, :], start=True, stop=True
                                         ).then_inc(S["a_done"], 1)

            @block.vector
            def _(dve):
                with dve.Fori(0, WINDOWS) as w:
                    for n in range(N):
                        dve.wait_ge(S["k_turned"], w * N + n + 1 + N)
                        dve.wait_ge(S["a_done"], w * N + n + 1)
                        nc.vector.tensor_tensor(kb[:, n, :].rearrange("c (h k) -> c h k", h=HEADS),
                                                pk[0:64, n, None, 0:64].to_broadcast([64, HEADS, 64]),
                                                c("headmask", 0, 64).rearrange("c (h k) -> c h k", h=HEADS), ALU.mult
                                                ).then_inc(S["k_masked"], 1)
                    for n in range(N):
                        dve.wait_ge(gathered[n], (d * WINDOWS + w) * 16 + 16)
                        dve.wait_ge(S[f"out_stored{n}"], w * 32 + 32)
                        for h in range(2):
                            ins = nc.vector.tensor_tensor(vw[:, n, h, :, 16 * h:16 * h + 16],
                                                          kv[n][:, 64:128].rearrange("p (j i) -> p j i", j=4),
                                                          c("vmask").rearrange("p (j i) -> p j i", j=4), ALU.mult)
                        ins.then_inc(S["v_masked"], 1)

            @block.scalar
            def _(act):
                with act.Fori(0, WINDOWS) as w:
                    for n in range(N):
                        act.wait_ge(S["a_done"], w * N + n + 1 + N)
                        act.wait_ge(S[f"out_stored{n}"], w * 32 + 32)
                        nc.scalar.copy(aw[:, n, :], pa[0:64, n, :]).then_inc(S["a_copied"], 1)
                        act.wait_ge(S["a_copied"], w * N + n + 1 + N)
                        act.dma_start(AW[n, w], aw[:, n, :]).then_inc(S[f"out_stored{n}"], 16)
                        act.wait_ge(S["v_masked"], w * N + n + 1 + N)
                        act.dma_start(VW[n, w], vw[:, n, :, :, :].rearrange("p h j c -> p (h j c)")).then_inc(S[f"out_stored{n}"], 16)
                for n in range(N):
                    act.wait_ge(S[f"out_stored{n}"], 32 * (WINDOWS + 1))


def attention(nc, sbt, pst, clear, c, S, allsems, XH, AW, VW, AO):
    T, HALF = 8, 2
    TD, TF = N * T + 1, N * T - 1
    HD = N * HALF + 1
    QD, QF = 2 * N * HALF + 1, 2 * N * HALF - 1
    ND = N + 1
    MR = 96
    clear(*allsems, start={**{S[k]: N * T for k in ("scored", "max_ready")},
                           **{S[k]: N * HALF for k in "max_turned max_copied av_done".split()},
                           **{S[k]: N for k in "recip_ready attn_ready".split()},
                           **{S[k]: 2 * N * HALF for k in ("shifted", "probs_ready")},
                           S["out_stored0"]: 16, S["out_stored1"]: 16})
    with ExitStack() as ph:
        xw = sbt(ph, "a_xw", [MR + HEADS, N, HALF * WPIX])
        aw = sbt(ph, "a_aw", [MR + HEADS, N, 512])
        vw = sbt(ph, "a_vw", [P, N, HALF, 4, 32])
        ones = sbt(ph, "a_ones", [P, HALF, 4, 32])
        mx = sbt(ph, "a_mx", [P, N, T, HEADS])
        pr = sbt(ph, "a_pr", [P, HALF, 4, WPIX])
        rc = sbt(ph, "a_rc", [P, WPIX])
        ao = sbt(ph, "a_ao", [P, N, WPIX])
        ps = pst(ph, "ps_s", [P, 2, 512])
        pk = pst(ph, "ps_t", [P, 2, 2, WPIX])
        po = pst(ph, "ps_o", [P, 2, WPIX])
        pm = ps
        with nc.Block() as fixed:
            @fixed.vector
            def _(dve):
                nc.vector.memset(xw[64:MR, :, :], 0.0)
                nc.vector.memset(aw[64:MR, :, :], 0.0)
                nc.vector.memset(ones[:, :, :, :], 0.0)

        with nc.Block() as masks:
            @masks.vector
            def _(dve):
                for n in range(N):
                    nc.vector.tensor_copy(aw[MR:MR + HEADS, n, :], c("minus", MR, MR + HEADS))
                for h in range(HALF):
                    nc.vector.tensor_copy(ones[:, h, :, 16 * h:16 * h + 16], c("vmask").rearrange("p (j i) -> p j i", j=4))

        with nc.Block() as block:
            def half(w, n, h):
                return w * (N * HALF) + n * HALF + h

            @block.sync
            def _(sp):
                def load(wy, wx, n):
                    w = sp.snap(wy * NW + wx)
                    sp.wait_ge(S["av_done"], half(w, n, 0) + 2)
                    sp.dma_start(aw[0:64, n, :], AW[n, w]).then_inc(S[f"in_loaded{n}"], 16)
                    sp.dma_start(vw[:, n, :, :, :].rearrange("p h j c -> p (h j c)"), VW[n, w]
                                 ).then_inc(S[f"in_loaded{n}"], 16)
                    for h in range(HALF):
                        sp.dma_start(xw[0:64, n, WPIX * h:WPIX * h + WPIX].rearrange("c (r x) -> c r x", x=WW),
                                     XH[n, 64 * h:64 * h + 64, bass.ds(wy * WRP + 1, WRP), bass.ds(wx * WW, WW)]
                                     ).then_inc(S[f"in_loaded{n}"], 16)

                with sp.Fori(0, NW) as wy:
                    with sp.Fori(0, NW) as wx:
                        for n in range(N):
                            load(wy, wx, n)

            @block.scalar
            def _(act):
                def copy_max(w, n, h):
                    act.wait_ge(S["max_turned"], half(w, n, h) + HD)
                    nc.scalar.copy(xw[MR:MR + HEADS, n, WPIX * h:WPIX * h + WPIX], pm[0:8, h, :]
                                   ).then_inc(S["max_copied"], 1)

                def exps(w, n, h):
                    act.wait_ge(S["av_done"], half(w, n, h) - 2 + HD)
                    for b in range(2):
                        act.wait_ge(S["shifted"], 2 * half(w, n, h) + b + QD)
                        nc.scalar.activation(pr[:, h, 2 * b:2 * b + 2, :], pk[:, b, :, :], ACT.Exp
                                             ).then_inc(S["probs_ready"], 1)

                def store(w, wy, wx, n):
                    act.wait_ge(S["attn_ready"], w * N + n + ND)
                    act.dma_start(AO[n, :, bass.ds(wy * WRP, WRP), bass.ds(wx * WW, WW)],
                                  ao[:, n, :].rearrange("c (r x) -> c r x", x=WW)).then_inc(S[f"out_stored{n}"], 16)

                with act.Fori(0, NW) as wy:
                    with act.Fori(0, NW) as wx:
                        w = act.snap(wy * NW + wx)
                        copy_max(w, 0, 0)
                        copy_max(w, 0, 1)
                        exps(w, 0, 0)
                        exps(w, 0, 1)
                        copy_max(w, 1, 0)
                        copy_max(w, 1, 1)
                        exps(w, 1, 0)
                        store(w, wy, wx, 0)
                        exps(w, 1, 1)
                        store(w, wy, wx, 1)
                for n in range(N):
                    act.wait_ge(S[f"out_stored{n}"], 16 * (WINDOWS + 1))

            @block.tensor
            def _(pe):
                def by_pixel(w, n, t):
                    i = w * (N * T) + n * T + t
                    if t == 0:
                        pe.wait_ge(S[f"in_loaded{n}"], w * 64 + 64)
                        pe.wait_ge(S["max_copied"], half(w, n, 0) - 1 + HD)
                    pe.wait_ge(S["max_ready"], i + TF)
                    nc.tensor.matmul(ps[:, t % 2, :], xw[0:MR, n, P * t:P * t + P], aw[0:MR, n, :], start=True, stop=True
                                     ).then_inc(S["scored"], 1)

                def turn(w, n, h):
                    pe.wait_ge(S["max_ready"], w * (N * T) + n * T + T - 1 + TD)
                    for q in range(4):
                        mm = nc.tensor.transpose(pm[0:8, h, P * q:P * q + P], mx[:, n, 4 * h + q, :], c("ident"))
                    mm.then_inc(S["max_turned"], 1)

                def by_key(w, n, h):
                    pe.wait_ge(S["max_copied"], half(w, n, h) + HD)
                    for b in range(2):
                        pe.wait_ge(S["probs_ready"], 2 * half(w, n, h) + b + QF)
                        for q in range(2):
                            j = 2 * b + q
                            mm = nc.tensor.matmul(pk[:, b, q, :], aw[:, n, P * j:P * j + P],
                                                  xw[:, n, WPIX * h:WPIX * h + WPIX], start=True, stop=True)
                        mm.then_inc(S["shifted"], 1)

                def sum_up(w, n, h):
                    pe.wait_ge(S["probs_ready"], 2 * half(w, n, h) + 1 + QD)
                    if h == 0:
                        pe.wait_ge(S["attn_ready"], w * N + n - 1 + ND)
                    for kind, matrix in enumerate((vw[:, n, :, :, :], ones)):
                        for j in range(4):
                            mm = nc.tensor.matmul(po[32 * j:32 * j + 32, kind, :], matrix[:, h, j, :], pr[:, h, j, :],
                                                  start=(h == 0), stop=(h == 1))
                    mm.then_inc(S["av_done"], 1)

                with pe.Fori(0, WINDOWS) as w:
                    for t in range(T):
                        by_pixel(w, 0, t)
                    for h in range(HALF):
                        turn(w, 0, h)
                    by_key(w, 0, 0)
                    for t in range(2):
                        by_pixel(w, 1, t)
                    by_key(w, 0, 1)
                    for t in range(2, 5):
                        by_pixel(w, 1, t)
                    sum_up(w, 0, 0)
                    for t in range(5, T):
                        by_pixel(w, 1, t)
                    sum_up(w, 0, 1)
                    for h in range(HALF):
                        turn(w, 1, h)
                    by_key(w, 1, 0)
                    by_key(w, 1, 1)
                    sum_up(w, 1, 0)
                    sum_up(w, 1, 1)

            @block.vector
            def _(dve):
                with dve.Fori(0, WINDOWS) as w:
                    for n in range(N):
                        for t in range(T):
                            dve.wait_ge(S["scored"], w * (N * T) + n * T + t + TD)
                            nc.vector.reduce_max(mx[:, n, t, :], ps[:, t % 2, :].rearrange("p (h k) -> p h k", h=HEADS), AX.X
                                                 ).then_inc(S["max_ready"], 1)
                    for n in range(N):
                        i = w * N + n
                        dve.wait_ge(S["av_done"], half(w, n, 1) + HD)
                        dve.wait_ge(S[f"out_stored{n}"], w * 16 + 16)
                        dve.wait_ge(S["attn_ready"], i - 1 + ND)
                        nc.vector.reciprocal(rc[:, :], po[:, 1, :]).then_inc(S["recip_ready"], 1)
                        dve.wait_ge(S["recip_ready"], i + ND)
                        nc.vector.tensor_tensor(ao[:, n, :], po[:, 0, :], rc[:, :], ALU.mult
                                                ).then_inc(S["attn_ready"], 1)


def mixing(nc, sbt, pst, clear, c, S, allsems, lepm, wod, attb, XH, AO, X1, X2, XH2):
    clear(*allsems, start={**{S[k]: BODY for k in UNIT_SEMS}, S["out_stored0"]: 32, S["out_stored1"]: 32})
    with ExitStack() as ph:
        xs = sbt(ph, "x_xs", [P, N, SRP + 2, PADW])
        ao = sbt(ph, "x_ao", [P, N, SRP, W])
        x1 = sbt(ph, "x_x1", [P, N, SRP, W])
        x2 = sbt(ph, "x_x2", [P, N, SRP, W])
        sq = sbt(ph, "x_sq", [P, 2, COLS])
        sd = sbt(ph, "x_sd", [P, 2, COLS])
        rstd = sbt(ph, "x_rstd", [P, 2, COLS])
        xr = sbt(ph, "x_xr", [P, 2, COLS])
        xh = sbt(ph, "x_xh", [P, N, SRP, W])
        px = pst(ph, "ps_x", [P, 2, COLS])
        pc = pst(ph, "ps_c", [P, 2, COLS])
        pv = pst(ph, "ps_v", [P, 2, COLS])
        with nc.Block() as border:
            @border.vector
            def _(dve):
                nc.vector.memset(xs[:, :, :, 0:2], 0.0)
                nc.vector.memset(xs[:, :, :, PADW - 2:PADW], 0.0)

        with nc.Block() as block:
            @block.sync
            def _(sp):
                def load(s, n):
                    sp.wait_ge(S["conv_done"], first_unit(s, n) + LAST)
                    sp.wait_ge(S["x_ready"], first_unit(s, n) + LAST)
                    for dst, src in ((xs[:, n, :, 2:2 + W], XH[n, :, bass.ds(s * SRP, SRP + 2), :]),
                                     (ao[:, n, :, :], AO[n, :, bass.ds(s * SRP, SRP), :]),
                                     (x1[:, n, :, :], X1[n, :, bass.ds(s * SRP, SRP), :])):
                        sp.dma_start(dst, src).then_inc(S[f"in_loaded{n}"], 16)

                def store(s, n):
                    sp.wait_ge(S["x_ready"], first_unit(s, n) + UNITS - 1 + DONE)
                    sp.dma_start(X2[n, :, bass.ds(s * SRP, SRP), :], x2[:, n, :, :]).then_inc(S[f"out_stored{n}"], 16)
                    sp.wait_ge(S["plus_ready"], first_unit(s, n) + UNITS - 1 + DONE)
                    sp.dma_start(XH2[n, :, bass.ds(s * SRP + 1, SRP), :], xh[:, n, :, :]).then_inc(S[f"out_stored{n}"], 16)

                run_strips(sp, load, store)
                for n in range(N):
                    sp.wait_ge(S[f"out_stored{n}"], 32 * (STRIPS + 1))

            @block.tensor
            def _(pe):
                def conv(s, n, k):
                    u = first_unit(s, n) + k
                    if k == 0:
                        pe.wait_ge(S[f"in_loaded{n}"], s * 48 + 48)
                    pe.wait_ge(S["x_ready"], u + FREE)
                    for g in range(3):
                        for dx in range(5):
                            nc.tensor.matmul(px[:, k % 2, :], lepm[:, g, dx, :],
                                             xs[:, n, UNIT * k + g:UNIT * k + g + UNIT, dx:dx + W],
                                             start=(g + dx == 0), stop=False)
                    nc.tensor.matmul(px[:, k % 2, :], wod[:, :], rows(ao, n, k), start=False, stop=True
                                     ).then_inc(S["conv_done"], 1)

                with pe.Fori(0, STRIPS) as s:
                    for i in range(BODY + 2):
                        if i < BODY:
                            conv(s, i // UNITS, i % UNITS)
                        for back, step in ((1, "centre"), (2, "var")):
                            if 0 <= i - back < BODY:
                                n, k = divmod(i - back, UNITS)
                                norm_on_pe(nc, pe, c, S, first_unit(s, n) + k, x2, sq, pc, pv, n, k, step)

            @block.scalar
            def _(act):
                with act.Fori(0, STRIPS) as s:
                    for i in range(BODY + 2):
                        if i < BODY:
                            n, k = divmod(i, UNITS)
                            square_on_act(nc, act, S, first_unit(s, n) + k, k, sq, pc)
                        if 0 <= i - 1 < BODY:
                            n, k = divmod(i - 1, UNITS)
                            sqrt_on_act(nc, act, S, first_unit(s, n) + k, k, sd, pv, c("eps"))
                        if i >= 2:
                            n, k = divmod(i - 2, UNITS)
                            if k == 0:
                                act.wait_ge(S[f"out_stored{n}"], s * 32 + 32)
                            plus_on_act(nc, act, S, first_unit(s, n) + k, k, n, xr, xh)

            @block.vector
            def _(dve):
                with dve.Fori(0, STRIPS) as s:
                    for i in range(BODY + 2):
                        if i < BODY:
                            n, k = divmod(i, UNITS)
                            u = first_unit(s, n) + k
                            dve.wait_ge(S["conv_done"], u + DONE)
                            if k == 0:
                                dve.wait_ge(S[f"out_stored{n}"], s * 32 + 32)
                            nc.vector.scalar_tensor_tensor(rows(x2, n, k), as_rows(px[:, k % 2, :]), attb[:, 0:1],
                                                           rows(x1, n, k), ALU.add, ALU.add).then_inc(S["x_ready"], 1)
                        if i >= 2:
                            n, k = divmod(i - 2, UNITS)
                            norm_on_dve(nc, dve, S, first_unit(s, n) + k, k, sd, rstd, xr, pc)



def glu(nc, d, sbt, pst, clear, c, S, allsems, glum, gvm, fc2, fc2b, dwb, XH2, X2, IMG):
    PBODY = 2 * BODY
    PD, PF = PBODY + 1, PBODY - 1
    clear(*allsems, start={**{S[k]: BODY for k in ("fc2_done", "out_ready")},
                           **{S[k]: PBODY for k in "xbranch_done vbranch_done gelu_ready gated".split()},
                           S["out_stored0"]: 16, S["out_stored1"]: 16})
    with ExitStack() as ph:
        xs = sbt(ph, "g_xs", [P, N, SRP + 2, PADW])
        x2 = sbt(ph, "g_x2", [P, N, SRP, W])
        ge = sbt(ph, "g_ge", [HID, 2, COLS])
        gv = sbt(ph, "g_gv", [HID, 2, COLS])
        xo = sbt(ph, "g_xo", [P, N, SRP, W])
        px = pst(ph, "ps_x", [HID, 2, COLS])
        pv = pst(ph, "ps_v", [HID, 2, COLS])
        po = pst(ph, "ps_o", [P, 2, COLS])
        with nc.Block() as border:
            @border.vector
            def _(dve):
                nc.vector.memset(xs[:, :, :, 0:2], 0.0)
                nc.vector.memset(xs[:, :, :, PADW - 2:PADW], 0.0)

        with nc.Block() as block:
            @block.sync
            def _(sp):
                def load(s, n):
                    sp.wait_ge(S["out_ready"], first_unit(s, n) + LAST)
                    for dst, src in ((xs[:, n, :, 2:2 + W], XH2[n, :, bass.ds(s * SRP, SRP + 2), :]),
                                     (x2[:, n, :, :], X2[n, :, bass.ds(s * SRP, SRP), :])):
                        sp.dma_start(dst, src).then_inc(S[f"in_loaded{n}"], 16)

                def store(s, n):
                    sp.wait_ge(S["out_ready"], first_unit(s, n) + UNITS - 1 + DONE)
                    sp.dma_start(IMG[d + 1, n, :, bass.ds(s * SRP + 1, SRP), :], xo[:, n, :, :]
                                 ).then_inc(S[f"out_stored{n}"], 16)

                run_strips(sp, load, store)
                for n in range(N):
                    sp.wait_ge(S[f"out_stored{n}"], 16 * (STRIPS + 1))

            @block.tensor
            def _(pe):
                def branches(s, n, k, par):
                    v = 2 * (first_unit(s, n) + k) + par
                    if k + par == 0:
                        pe.wait_ge(S[f"in_loaded{n}"], s * 32 + 32)
                    pe.wait_ge(S["gelu_ready"], v + PF)
                    for g in range(2):
                        r = UNIT * k + g + par
                        for dx in range(3):
                            mm = nc.tensor.matmul(px[:, par, :], glum[:, par, g, dx, :],
                                                  xs[:, n, r:r + UNIT, 1 + dx:1 + dx + W],
                                                  start=(g + dx == 0), stop=(g == 1 and dx == 2))
                    mm.then_inc(S["xbranch_done"], 1)
                    pe.wait_ge(S["gated"], v + PF)
                    nc.tensor.matmul(pv[:, par, :], gvm[:, par, :],
                                     xs[:, n, UNIT * k + 1:UNIT * k + 1 + UNIT, 2:2 + W], start=True, stop=True
                                     ).then_inc(S["vbranch_done"], 1)

                def project(s, n, k):
                    u = first_unit(s, n) + k
                    pe.wait_ge(S["out_ready"], u + FREE)
                    for par in range(2):
                        pe.wait_ge(S["gated"], 2 * u + par + PD)
                        mm = nc.tensor.matmul(po[64 * par:64 * par + 64, k % 2, :], fc2[:, :], gv[:, par, :],
                                              start=True, stop=True)
                    mm.then_inc(S["fc2_done"], 1)

                with pe.Fori(0, STRIPS) as s:
                    for i in range(BODY + 1):
                        if i < BODY:
                            branches(s, i // UNITS, i % UNITS, 0)
                        if i >= 1:
                            project(s, (i - 1) // UNITS, (i - 1) % UNITS)
                        if i < BODY:
                            branches(s, i // UNITS, i % UNITS, 1)

            @block.scalar
            def _(act):
                with act.Fori(0, STRIPS) as s:
                    for n in range(N):
                        for k in range(UNITS):
                            for par in range(2):
                                v = 2 * (first_unit(s, n) + k) + par
                                act.wait_ge(S["xbranch_done"], v + PD)
                                act.wait_ge(S["gated"], v + PF)
                                nc.scalar.activation(ge[:, par, :], px[:, par, :], ACT.Gelu, bias=dwb[:, 0:1]
                                                     ).then_inc(S["gelu_ready"], 1)

            @block.vector
            def _(dve):
                def gate(s, n, k, par):
                    u = first_unit(s, n) + k
                    dve.wait_ge(S["gelu_ready"], 2 * u + par + PD)
                    dve.wait_ge(S["vbranch_done"], 2 * u + par + PD)
                    dve.wait_ge(S["fc2_done"], u - 1 + DONE)
                    nc.vector.tensor_tensor(gv[:, par, :], pv[:, par, :], ge[:, par, :], ALU.mult
                                            ).then_inc(S["gated"], 1)

                with dve.Fori(0, STRIPS) as s:
                    for i in range(BODY + 1):
                        if i >= 1:
                            n, k = divmod(i - 1, UNITS)
                            u = first_unit(s, n) + k
                            dve.wait_ge(S["fc2_done"], u + DONE)
                            if k == 0:
                                dve.wait_ge(S[f"out_stored{n}"], s * 16 + 16)
                            nc.vector.scalar_tensor_tensor(rows(xo, n, k), as_rows(po[:, k % 2, :]), fc2b[:, 0:1],
                                                           rows(x2, n, k), ALU.add, ALU.add).then_inc(S["out_ready"], 1)
                        if i < BODY:
                            for par in range(2):
                                gate(s, i // UNITS, i % UNITS, par)



def layer1(nc, I, sem, sbt, pst, clear, c, IMG, STAT, out):
    ctx = ExitStack()
    ctx.__enter__()
    x_in = IMG[D]
    W1, W2, GW, GB = slice(0, 64), slice(64, 128), slice(128, 129), slice(129, 130)
    prm = sbt(ctx, "prm", [P, 130])
    mom = sbt(ctx, "mom", [P, 130])
    w1t = sbt(ctx, "w1t", [P, HID])
    w2n = sbt(ctx, "w2n", [P, HID])
    w1p = sbt(ctx, "w1p", [P, 2, HID])
    w2b = sbt(ctx, "w2b", [P, 2, HID])
    gram = sbt(ctx, "gram", [P, N, P + 1])
    gm = sbt(ctx, "gm", [P, N, 65])
    cov = sbt(ctx, "cov", [P, N, 64])
    mub = sbt(ctx, "mub", [P, N, 64])
    mg = sbt(ctx, "mg", [P, N])
    rstd = sbt(ctx, "rstd", [P, N])
    sc = sbt(ctx, "sc", [P, N])
    bi = sbt(ctx, "bi", [P, N])
    coef = sbt(ctx, "coef", [P, N])
    run = sbt(ctx, "run", [P, 2])
    ab = sbt(ctx, "ab", [P, 2])
    abb = sbt(ctx, "abb", [P, 2, 64])
    dbias = sbt(ctx, "dbias", [P, 1])
    acc = sbt(ctx, "acc", [P, N, 130])
    m_loaded, m_link = sem("m_loaded"), sem("m_link")
    S = {k: sem("m_" + k) for k in """in_loaded0 in_loaded1 out_stored0 out_stored1 turned copied gram_done summed
        h_done gelu_ready z_ready zz_ready den_ready gz_ready density_ready tail_ready inverse_ready phi_ready
        dgelu_ready y_done y_ready stats_ready d_done dh_ready ef_done out_ready
        turned_x turned_y turned_g0 turned_g1 turned_d0 turned_d1
        copied_x copied_y copied_g0 copied_g1 copied_d0 copied_d1""".split()}
    allsems = [m_loaded, m_link, *S.values()]
    env = (nc, sbt, pst, clear, c, S, allsems)

    clear(*allsems)
    with ExitStack() as ph:
        w2 = sbt(ph, "w2", [64, HID])
        g1 = sbt(ph, "g1", [16, 64])
        g1t = sbt(ph, "g1t", [64, 16])
        g1b = sbt(ph, "g1b", [16, 1])
        g2 = sbt(ph, "g2", [16, 1])
        g2r = sbt(ph, "g2r", [16, P])
        g2b = sbt(ph, "g2b", [P, 1])
        res = sbt(ph, "res", [P, 1])
        own = sbt(ph, "own", [P, N, 65])
        mur = sbt(ph, "mur", [64, N, P])
        gg = sbt(ph, "gg", [16, N])
        mm = sbt(ph, "mm", [P, 64])
        first = ExitStack()
        ps = pst(first, "ps_m", [P, 2, 512])
        with nc.Block() as load:
            @load.sync
            def _(sp):
                k = [0]

                def get(dst, src):
                    sp.dma_start(dst, src).then_inc(m_loaded, 16)
                    k[0] += 1

                def column(name):
                    return I[name].rearrange("(c o) -> c o", o=1)

                get(prm[:, W1], I["m_w1"])
                get(prm[:, GW], column("m_gn_w"))
                get(prm[:, GB], column("m_gn_b"))
                get(w2[:, :], I["m_w2"])
                get(g1[:, :], I["m_g1_w"])
                get(g1b[:, :], column("m_g1_b"))
                get(g2[:, :], I["m_g2_w"].rearrange("a c -> c a"))
                get(g2b[:, :], column("m_g2_b").to_broadcast([P, 1]))
                get(res[:, :], column("m_residual_scale").to_broadcast([P, 1]))
                for h in range(2):
                    get(run[64 * h:64 * h + 64, 0:1], column("m_running_mean"))
                    get(run[64 * h:64 * h + 64, 1:2], column("m_running_var"))
                sp.wait_ge(m_loaded, 16 * k[0])

            @load.gpsimd
            def _(pool):
                pool.memset(mom[:, :], 0.0)
                pool.memset(w1p[:, :, :], 0.0)
                pool.memset(w2b[:, :, :], 0.0)
                pool.memset(gram[:, :, :], 0.0)

        with nc.Block() as turn:
            @turn.tensor
            def _(pe):
                nc.tensor.transpose(ps[:, 0, 0:64], w2[:, :], c("ident", 0, 64)[:, 0:64])
                nc.tensor.transpose(ps[0:64, 1, 0:16], g1[:, :], c("ident", 0, 16)[:, 0:16])

        with nc.Block() as keep:
            @keep.vector
            def _(dve):
                nc.vector.tensor_copy(prm[:, W2], ps[:, 0, 0:64])
                nc.vector.tensor_copy(g1t[:, :], ps[0:64, 1, 0:16])
                nc.vector.tensor_copy(g2r[:, :], g2[:, 0:1].to_broadcast([16, P]))

        first.close()
        gram_pass(*env, x_in, gram)
        ps = pst(ph, "ps_m", [P, 8, 512])

        clear(m_link)
        with nc.Block() as blocks:
            @blocks.vector
            def _(dve):
                for n in range(N):
                    for h in range(2):
                        hp = slice(64 * h, 64 * h + 64)
                        nc.vector.tensor_copy(own[hp, n, 0:64], gram[hp, n, 64 * h:64 * h + 64])
                    nc.vector.tensor_copy(own[:, n, 64:65], gram[:, n, P:P + 1])

        with nc.Block() as parities:
            @parities.tensor
            def _(pe):
                for n in range(N):
                    nc.tensor.matmul(ps[:, n, 0:65], c("pair"), own[:, n, :], start=True, stop=True)

        clear(m_link)
        with nc.Block() as means:
            @means.vector
            def _(dve):
                step = Link(nc, m_link, dve)
                for n in range(N):
                    step(nc.vector.tensor_scalar_mul(gm[:, n, :], ps[:, n, 0:65], 1.0 / PIX))
                    nc.vector.tensor_copy(mur[:, n, :], gm[0:64, n, 64:65].to_broadcast([64, P]))

        with nc.Block() as spread:
            @spread.tensor
            def _(pe):
                for n in range(N):
                    nc.tensor.matmul(ps[:, 2 + n, 0:64], mur[:, n, :], c("ident", 0, 64)[:, 0:64], start=True, stop=True)
                    nc.tensor.matmul(ps[0:16, 4, n:n + 1], g1t[:, :], gm[0:64, n, 64:65], start=True, stop=True)

        clear(m_link)
        with nc.Block() as covariance:
            @covariance.vector
            def _(dve):
                step = Link(nc, m_link, dve)
                for n in range(N):
                    step(nc.vector.tensor_copy(mub[:, n, :], ps[:, 2 + n, 0:64]))
                    step(nc.vector.tensor_scalar(mm[:, :], mub[:, n, :], gm[:, n, 64:65], None, ALU.mult))
                    step(nc.vector.tensor_tensor(cov[:, n, :], gm[:, n, 0:64], mm[:, :], ALU.subtract))

            @covariance.scalar
            def _(act):
                nc.scalar.activation(gg[:, :], ps[0:16, 4, 0:N], ACT.Gelu, bias=g1b[:, 0:1])

        with nc.Block() as gate:
            @gate.tensor
            def _(pe):
                nc.tensor.matmul(ps[:, 5, 0:N], g2r[:, :], gg[:, :], start=True, stop=True)

        with nc.Block() as sigmoid:
            @sigmoid.scalar
            def _(act):
                nc.scalar.activation(coef[:, :], ps[:, 5, 0:N], ACT.Sigmoid, bias=g2b[:, 0:1])

        with nc.Block() as scale:
            @scale.vector
            def _(dve):
                nc.vector.tensor_scalar(coef[:, :], coef[:, :], res[:, 0:1], None, ALU.mult)

    def prepare():
        with ExitStack() as ph:
            dup = sbt(ph, "dup", [P, 2, 2, 64])
            hm = sbt(ph, "hm", [P, N])
            wc = sbt(ph, "wc", [P, N, 64])
            wh = sbt(ph, "wh", [P, 64])
            size = sbt(ph, "size", [P, 4])
            t = sbt(ph, "t", [P, N])
            ps = pst(ph, "ps_p", [P, 8, 512])
            clear(m_link)
            with nc.Block() as double:
                @double.vector
                def _(dve):
                    step = Link(nc, m_link, dve)
                    for i, w in enumerate((W1, W2)):
                        nc.vector.tensor_copy(dup[:, i, :, :], prm[:, None, w].to_broadcast([P, 2, 64]))
                    step(nc.vector.tensor_reduce(size[:, 0:1], prm[:, W1], AX.X, ALU.max))
                    step(nc.vector.tensor_reduce(size[:, 1:2], prm[:, W1], AX.X, ALU.min))
                    step(nc.vector.tensor_scalar_mul(size[:, 1:2], size[:, 1:2], -1.0))
                    nc.vector.tensor_tensor(size[:, 0:1], size[:, 0:1], size[:, 1:2], ALU.max)
            with nc.Block() as turn:
                @turn.tensor
                def _(pe):
                    for i in range(2):
                        nc.tensor.transpose(ps[:, i, 0:P], dup[:, i, :, :].rearrange("o a c -> o (a c)"), c("ident"))
                    nc.tensor.matmul(ps[:, 7, 0:1], c("group"), size[:, 0:1], start=True, stop=True)
            clear(m_link)
            with nc.Block() as keep:
                @keep.vector
                def _(dve):
                    step = Link(nc, m_link, dve)
                    nc.vector.tensor_copy(w1t[:, :], ps[:, 0, 0:P])
                    for par in range(2):
                        hp = slice(64 * par, 64 * par + 64)
                        nc.vector.tensor_copy(w1p[hp, par, :], ps[hp, 0, 0:P])
                    nc.vector.tensor_copy(w2n[:, :], ps[:, 1, 0:P])
                    step(nc.vector.tensor_scalar(size[:, 1:2], ps[:, 7, 0:1], 1e-15, None, ALU.max))
                    step(nc.vector.reciprocal(size[:, 2:3], size[:, 1:2]))
                    nc.vector.tensor_scalar(wh[:, :], prm[:, W1], size[:, 2:3], None, ALU.mult)
                    nc.vector.tensor_scalar(size[:, 3:4], size[:, 2:3], size[:, 2:3], GN_EPS, ALU.mult, ALU.mult)
            with nc.Block() as moments:
                @moments.tensor
                def _(pe):
                    for n in range(N):
                        nc.tensor.matmul(ps[:, 2, n:n + 1], w1t[0:64, :], gm[0:64, n, 64:65], start=True, stop=True)
                        nc.tensor.matmul(ps[:, 3 + n, 0:64], w1t[0:64, :], cov[0:64, n, :], start=True, stop=True)
            clear(m_link)
            with nc.Block() as own_variance:
                @own_variance.vector
                def _(dve):
                    step = Link(nc, m_link, dve)
                    nc.vector.tensor_scalar(hm[:, :], ps[:, 2, 0:N], size[:, 2:3], None, ALU.mult)
                    for n in range(N):
                        step(nc.vector.scalar_tensor_tensor(wc[:, n, :], ps[:, 3 + n, 0:64], size[:, 2:3], wh[:, :],
                                                            ALU.mult, ALU.mult))
                    nc.vector.reduce_sum(rstd[:, :], wc[:, :, :], AX.X)
            with nc.Block() as group_mean:
                @group_mean.tensor
                def _(pe):
                    nc.tensor.matmul(ps[:, 5, 0:N], c("group"), hm[:, :], start=True, stop=True)
            clear(m_link)
            with nc.Block() as spread:
                @spread.vector
                def _(dve):
                    step = Link(nc, m_link, dve)
                    step(nc.vector.tensor_scalar_mul(mg[:, :], ps[:, 5, 0:N], 1.0 / GROUP))
                    step(nc.vector.tensor_tensor(t[:, :], hm[:, :], mg[:, :], ALU.subtract))
                    step(nc.vector.tensor_tensor(t[:, :], t[:, :], t[:, :], ALU.mult))
                    step(nc.vector.tensor_tensor(t[:, :], t[:, :], rstd[:, :], ALU.add))
                    nc.vector.tensor_scalar(mg[:, :], mg[:, :], size[:, 1:2], None, ALU.mult)
            with nc.Block() as group_variance:
                @group_variance.tensor
                def _(pe):
                    nc.tensor.matmul(ps[:, 6, 0:N], c("group"), t[:, :], start=True, stop=True)
            clear(m_link)
            with nc.Block() as positive:
                @positive.vector
                def _(dve):
                    nc.vector.tensor_scalar(t[:, :], ps[:, 6, 0:N], 1.0 / GROUP, 0.0, ALU.mult, ALU.max)
            with nc.Block() as root:
                @root.scalar
                def _(act):
                    nc.scalar.activation(t[:, :], t[:, :], ACT.Sqrt, bias=size[:, 3:4])
            clear(m_link)
            with nc.Block() as affine:
                @affine.vector
                def _(dve):
                    step = Link(nc, m_link, dve)
                    step(nc.vector.tensor_scalar(t[:, :], t[:, :], size[:, 1:2], None, ALU.mult))
                    step(nc.vector.reciprocal(rstd[:, :], t[:, :]))
                    step(nc.vector.tensor_scalar(t[:, :], t[:, :], DEVIATION_MAX, None, ALU.is_le))
                    step(nc.vector.tensor_tensor(rstd[:, :], rstd[:, :], t[:, :], ALU.mult))
                    step(nc.vector.tensor_scalar(sc[:, :], rstd[:, :], prm[:, GW], None, ALU.mult))
                    step(nc.vector.tensor_tensor(t[:, :], mg[:, :], sc[:, :], ALU.mult))
                    step(nc.vector.tensor_scalar(bi[:, :], t[:, :], prm[:, GB], -1.0, ALU.subtract, ALU.mult))

    def loss_gradient():
        with ExitStack() as ph:
            st = sbt(ph, "st", [P, N, STRIPS * UNITS * 6])
            mv = sbt(ph, "mv", [P, N, 2])
            t = sbt(ph, "t", [P, 8])
            q = sbt(ph, "q", [P, N])
            abr = sbt(ph, "abr", [64, 2, P])
            ps = pst(ph, "ps_l", [P, 8, 512])
            clear(m_loaded)
            with nc.Block() as load:
                @load.sync
                def _(sp):
                    for n in range(N):
                        sp.dma_start(st[:, n, :], STAT[n].rearrange("p s k -> p (s k)")).then_inc(m_loaded, 16)
                    sp.wait_ge(m_loaded, 16 * N)
            with nc.Block() as merge:
                @merge.vector
                def _(dve):
                    for n in range(N):
                        nc.vector.bn_aggr(mv[:, n, :], st[:, n, :])
            with nc.Block() as mean:
                @mean.tensor
                def _(pe):
                    nc.tensor.matmul(ps[:, 0, 0:N], c("pair"), mv[:, :, 0], start=True, stop=True)
            clear(m_link)
            with nc.Block() as deviations:
                @deviations.vector
                def _(dve):
                    step = Link(nc, m_link, dve)
                    step(nc.vector.reduce_sum(t[:, 0:1], ps[:, 0, 0:N], AX.X))
                    step(nc.vector.tensor_scalar_mul(t[:, 0:1], t[:, 0:1], 1.0 / (2 * N)))
                    step(nc.vector.tensor_scalar(q[:, :], mv[:, :, 0], t[:, 0:1], None, ALU.subtract))
                    step(nc.vector.tensor_tensor(q[:, :], q[:, :], q[:, :], ALU.mult))
                    step(nc.vector.tensor_tensor(q[:, :], q[:, :], mv[:, :, 1], ALU.add))
            with nc.Block() as variance:
                @variance.tensor
                def _(pe):
                    nc.tensor.matmul(ps[:, 1, 0:N], c("pair"), q[:, :], start=True, stop=True)
            clear(m_link)
            count = N * PIX
            with nc.Block() as coefficients:
                @coefficients.vector
                def _(dve):
                    step = Link(nc, m_link, dve)
                    step(nc.vector.reduce_sum(t[:, 1:2], ps[:, 1, 0:N], AX.X))
                    step(nc.vector.tensor_scalar_mul(t[:, 1:2], t[:, 1:2], count / (count - 1.0) / (2 * N)))
                    step(nc.vector.tensor_scalar_add(t[:, 2:3], run[:, 1:2], 1e-8))
                    step(nc.vector.reciprocal(t[:, 3:4], t[:, 2:3]))
                    step(nc.vector.tensor_tensor(t[:, 4:5], t[:, 1:2], t[:, 3:4], ALU.mult))
                    step(nc.vector.tensor_scalar_add(t[:, 4:5], t[:, 4:5], -1.0))
                    step(nc.vector.tensor_tensor(t[:, 4:5], t[:, 4:5], t[:, 3:4], ALU.mult))
                    step(nc.vector.tensor_scalar_mul(ab[:, 1:2], t[:, 4:5], 4.0 / C / (count - 1)))
                    step(nc.vector.tensor_tensor(t[:, 5:6], t[:, 0:1], run[:, 0:1], ALU.subtract))
                    step(nc.vector.tensor_scalar_mul(t[:, 5:6], t[:, 5:6], 2.0 / C / count))
                    step(nc.vector.tensor_tensor(t[:, 6:7], ab[:, 1:2], t[:, 0:1], ALU.mult))
                    step(nc.vector.tensor_tensor(ab[:, 0:1], t[:, 5:6], t[:, 6:7], ALU.subtract))
                    for i in range(2):
                        nc.vector.tensor_copy(abr[:, i, :], ab[0:64, i:i + 1].to_broadcast([64, P]))
                    for par in range(2):
                        hp = slice(64 * par, 64 * par + 64)
                        nc.vector.tensor_scalar(w2b[hp, par, :], w2n[hp, :], ab[hp, 1:2], None, ALU.mult)
                    nc.vector.memset(acc[:, :, :], 0.0)
            with nc.Block() as spread:
                @spread.tensor
                def _(pe):
                    for i in range(2):
                        nc.tensor.matmul(ps[:, 2 + i, 0:64], abr[:, i, :], c("ident", 0, 64)[:, 0:64], start=True, stop=True)
                    nc.tensor.matmul(ps[:, 4, 0:1], w2n[0:64, :], ab[0:64, 0:1], start=True, stop=True)
            with nc.Block() as keep:
                @keep.vector
                def _(dve):
                    nc.vector.tensor_copy(abb[:, :, :], ps[:, 2:4, 0:64])
                    nc.vector.tensor_copy(dbias[:, :], ps[:, 4, 0:1])

    def descend():
        with ExitStack() as ph:
            gr = sbt(ph, "gr", [P, 130])
            t = sbt(ph, "t", [P, N, 64])
            u = sbt(ph, "u", [P, N, 64])
            q = sbt(ph, "q", [P, N])
            th = sbt(ph, "th", [P, N])
            gs = sbt(ph, "gs", [P, 2, N])
            ms = sbt(ph, "ms", [P, 2, N])
            ps = pst(ph, "ps_d", [P, 8, 512])
            clear(m_link)
            with nc.Block() as outer:
                @outer.vector
                def _(dve):
                    step = Link(nc, m_link, dve)
                    step(nc.vector.tensor_tensor(gr[:, W2], acc[:, 0, 65:129], acc[:, 1, 65:129], ALU.add))
                    step(nc.vector.tensor_tensor(q[:, 0:1], acc[:, 0, 129:130], acc[:, 1, 129:130], ALU.add))
                    step(nc.vector.tensor_tensor(gr[:, W2], gr[:, W2], abb[:, 1, :], ALU.mult))
                    step(nc.vector.tensor_scalar(t[:, 0, :], abb[:, 0, :], q[:, 0:1], None, ALU.mult))
                    step(nc.vector.tensor_tensor(gr[:, W2], gr[:, W2], t[:, 0, :], ALU.add))
                    step(nc.vector.tensor_tensor(gr[:, GB], acc[:, 0, 64:65], acc[:, 1, 64:65], ALU.add))
                    for n in range(N):
                        step(nc.vector.tensor_tensor(t[:, n, :], acc[:, n, 0:64], prm[:, W1], ALU.mult))
                    step(nc.vector.reduce_sum(q[:, :], t[:, :, :], AX.X))
                    step(nc.vector.tensor_tensor(th[:, :], mg[:, :], acc[:, :, 64], ALU.mult))
                    step(nc.vector.tensor_tensor(th[:, :], q[:, :], th[:, :], ALU.subtract))
                    step(nc.vector.tensor_tensor(th[:, :], th[:, :], rstd[:, :], ALU.mult))
                    step(nc.vector.reduce_sum(gr[:, GW], th[:, :], AX.X))
                    step(nc.vector.tensor_scalar(gs[:, 0, :], acc[:, :, 64], prm[:, GW], None, ALU.mult))
                    step(nc.vector.tensor_scalar(gs[:, 1, :], th[:, :], prm[:, GW], None, ALU.mult))
            with nc.Block() as groups:
                @groups.tensor
                def _(pe):
                    nc.tensor.matmul(ps[:, 0, 0:2 * N], c("group"), gs[:, :, :].rearrange("p a n -> p (a n)"),
                                     start=True, stop=True)
                    for n in range(N):
                        nc.tensor.matmul(ps[:, 1 + n, 0:64], w1t[0:64, :], gm[0:64, n, 0:64], start=True, stop=True)
            clear(m_link)
            with nc.Block() as inner:
                @inner.vector
                def _(dve):
                    step = Link(nc, m_link, dve)
                    step(nc.vector.tensor_scalar_mul(ms[:, :, :].rearrange("p a n -> p (a n)"), ps[:, 0, 0:2 * N], 1.0 / GROUP))
                    for n in range(N):
                        step(nc.vector.tensor_scalar(u[:, n, :], mub[:, n, :], mg[:, n:n + 1], None, ALU.mult))
                        step(nc.vector.tensor_tensor(u[:, n, :], ps[:, 1 + n, 0:64], u[:, n, :], ALU.subtract))
                        step(nc.vector.tensor_scalar(u[:, n, :], u[:, n, :], rstd[:, n:n + 1], ms[:, 1, n:n + 1],
                                                     ALU.mult, ALU.mult))
                        step(nc.vector.tensor_scalar(t[:, n, :], mub[:, n, :], ms[:, 0, n:n + 1], None, ALU.mult))
                        step(nc.vector.tensor_tensor(u[:, n, :], u[:, n, :], t[:, n, :], ALU.add))
                        step(nc.vector.tensor_scalar(t[:, n, :], acc[:, n, 0:64], prm[:, GW], None, ALU.mult))
                        step(nc.vector.tensor_tensor(t[:, n, :], t[:, n, :], u[:, n, :], ALU.subtract))
                        step(nc.vector.tensor_scalar(t[:, n, :], t[:, n, :], rstd[:, n:n + 1], None, ALU.mult))
                    step(nc.vector.tensor_tensor(gr[:, W1], t[:, 0, :], t[:, 1, :], ALU.add))
                    step(nc.vector.tensor_scalar_mul(mom[:, :], mom[:, :], MOM))
                    step(nc.vector.tensor_tensor(mom[:, :], mom[:, :], gr[:, :], ALU.add))
                    step(nc.vector.tensor_scalar_mul(gr[:, :], mom[:, :], LR))
                    step(nc.vector.tensor_tensor(prm[:, :], prm[:, :], gr[:, :], ALU.subtract))

    with nc.Fori(0, STEPS):
        prepare()
        forward(*env, x_in, prm, w1p, sc, bi, STAT, None, None)
        loss_gradient()
        backward(*env, x_in, prm, w1p, w2b, sc, bi, dbias, acc)
        descend()
    prepare()
    forward(*env, x_in, prm, w1p, sc, bi, None, coef, out)
    ctx.close()


def gram_pass(nc, sbt, pst, clear, c, S, allsems, x_in, gram):
    clear(*allsems, start={S[k]: BODY for k in ("turned", "copied", "gram_done", "summed")})
    with ExitStack() as ph:
        xs = sbt(ph, "xs", [P, N, SRP, W])
        xt = sbt(ph, "xt", [P, 2, 4, P + 1])
        pt = pst(ph, "ps_t", [P, 2, 512])
        pg = pst(ph, "ps_g", [P, 2, 512])
        with nc.Block() as ones:
            @ones.vector
            def _(dve):
                nc.vector.memset(xt[:, :, :, P:P + 1], 1.0)
        with nc.Block() as block:
            @block.sync
            def _(sp):
                with sp.Fori(0, STRIPS) as s:
                    for n in range(N):
                        sp.wait_ge(S["turned"], first_unit(s, n) + LAST)
                        sp.dma_start(xs[:, n, :, :], x_in[n, :, bass.ds(s * SRP + 1, SRP), :]
                                     ).then_inc(S[f"in_loaded{n}"], 16)

            @block.tensor
            def _(pe):
                def turn(s, n, k):
                    if k == 0:
                        pe.wait_ge(S[f"in_loaded{n}"], s * 16 + 16)
                    pe.wait_ge(S["copied"], first_unit(s, n) + k + FREE)
                    cols = rows(xs, n, k).rearrange("p r w -> p (r w)")
                    for b in range(4):
                        mm = nc.tensor.transpose(pt[:, k % 2, P * b:P * b + P], cols[:, P * b:P * b + P], c("ident"))
                    mm.then_inc(S["turned"], 1)

                def product(s, n, k):
                    u = first_unit(s, n) + k
                    pe.wait_ge(S["copied"], u + DONE)
                    if k == 0:
                        pe.wait_ge(S["summed"], s * N + n - 1 + BODY)
                    for b in range(4):
                        mm = nc.tensor.matmul(pg[:, n, 0:P + 1], xt[:, k % 2, b, 0:P], xt[:, k % 2, b, :],
                                              start=(k + b == 0), stop=(k == UNITS - 1 and b == 3))
                    mm.then_inc(S["gram_done"], 1)

                with pe.Fori(0, STRIPS) as s:
                    for i in range(BODY + 1):
                        if i < BODY:
                            turn(s, i // UNITS, i % UNITS)
                        if i >= 1:
                            product(s, (i - 1) // UNITS, (i - 1) % UNITS)

            @block.scalar
            def _(act):
                with act.Fori(0, STRIPS) as s:
                    for n in range(N):
                        for k in range(UNITS):
                            u = first_unit(s, n) + k
                            act.wait_ge(S["turned"], u + DONE)
                            act.wait_ge(S["gram_done"], u + FREE)
                            nc.scalar.copy(xt[:, k % 2, :, 0:P], pt[:, k % 2, :].rearrange("p (b c) -> p b c", b=4)
                                           ).then_inc(S["copied"], 1)

            @block.vector
            def _(dve):
                with dve.Fori(0, STRIPS) as s:
                    for n in range(N):
                        dve.wait_ge(S["gram_done"], first_unit(s, n) + UNITS - 1 + DONE)
                        dve.wait_ge(S["summed"], s * N + n - 1 + BODY)
                        nc.vector.tensor_tensor(gram[:, n, :], gram[:, n, :], pg[:, n, 0:P + 1], ALU.add
                                                ).then_inc(S["summed"], 1)


def hidden_on_pe(nc, pe, S, u, s, n, k, w1p, xs, ph):
    if k == 0:
        pe.wait_ge(S[f"in_loaded{n}"], s * 16 + 16)
    for par in range(2):
        mm = nc.tensor.matmul(ph[:, par, :], w1p[:, par, :], rows(xs, n, k), start=True, stop=True)
    mm.then_inc(S["h_done"], 1)


def forward(nc, sbt, pst, clear, c, S, allsems, x_in, prm, w1p, sc, bi, STAT, coef, out):
    names = "h_done gelu_ready y_done y_ready stats_ready out_ready".split()
    last = out is not None
    clear(*allsems, start={**{S[k]: BODY for k in names}, S["out_stored0"]: 32, S["out_stored1"]: 32})
    per_store = 32 if last else 16
    if not last:
        clear(S["out_stored0"], S["out_stored1"], start={S["out_stored0"]: 16, S["out_stored1"]: 16})
    with ExitStack() as ctx:
        xs = sbt(ctx, "xs", [P, N, SRP, W])
        g = sbt(ctx, "g", [P, 2, 2, COLS])
        ys = sbt(ctx, "ys", [P, N, SRP, W])
        st = sbt(ctx, "stats", [P, N, UNITS * 6])
        ph = pst(ctx, "ps_h", [P, 2, 2, COLS])
        py = pst(ctx, "ps_y", [P, 2, COLS])
        with nc.Block() as block:
            @block.sync
            def _(sp):
                def load(s, n):
                    sp.wait_ge(S["y_ready"], first_unit(s, n) + LAST)
                    sp.dma_start(xs[:, n, :, :], x_in[n, :, bass.ds(s * SRP + 1, SRP), :]
                                 ).then_inc(S[f"in_loaded{n}"], 16)

                def store(s, n):
                    if last:
                        sp.wait_ge(S["y_ready"], first_unit(s, n) + UNITS - 1 + DONE)
                        image = out[n].rearrange("c (r p) w -> p c r w", p=2)
                        for par in range(2):
                            sp.dma_start(image[par, :, bass.ds(s * SRP, SRP), :], ys[64 * par:64 * par + 64, n, :, :]
                                         ).then_inc(S[f"out_stored{n}"], 16)
                    else:
                        sp.wait_ge(S["stats_ready"], first_unit(s, n) + UNITS - 1 + DONE)
                        sp.dma_start(STAT[n, :, s, :], st[:, n, :]).then_inc(S[f"out_stored{n}"], 16)

                run_strips(sp, load, store)
                for n in range(N):
                    sp.wait_ge(S[f"out_stored{n}"], per_store * (STRIPS + 1))

            @block.tensor
            def _(pe):
                def hidden(s, n, k):
                    u = first_unit(s, n) + k
                    pe.wait_ge(S["gelu_ready"], u + FREE)
                    hidden_on_pe(nc, pe, S, u, s, n, k, w1p, xs, ph[:, k % 2, :, :])

                def project(s, n, k):
                    u = first_unit(s, n) + k
                    pe.wait_ge(S["gelu_ready"], u + DONE)
                    pe.wait_ge(S["y_ready"], u + FREE)
                    for par in range(2):
                        mm = nc.tensor.matmul(py[64 * par:64 * par + 64, k % 2, :], prm[:, 64:128], g[:, k % 2, par, :],
                                              start=True, stop=True)
                    mm.then_inc(S["y_done"], 1)

                with pe.Fori(0, STRIPS) as s:
                    for i in range(BODY + 1):
                        if i < BODY:
                            hidden(s, i // UNITS, i % UNITS)
                        if i >= 1:
                            project(s, (i - 1) // UNITS, (i - 1) % UNITS)

            @block.scalar
            def _(act):
                with act.Fori(0, STRIPS) as s:
                    for n in range(N):
                        for k in range(UNITS):
                            u = first_unit(s, n) + k
                            act.wait_ge(S["h_done"], u + DONE)
                            act.wait_ge(S["y_done"], u + FREE)
                            nc.scalar.activation(g[:, k % 2, :, :], ph[:, k % 2, :, :], ACT.Gelu, bias=bi[:, n:n + 1],
                                                 scale=sc[:, n:n + 1]).then_inc(S["gelu_ready"], 1)

            @block.vector
            def _(dve):
                with dve.Fori(0, STRIPS) as s:
                    for n in range(N):
                        for k in range(UNITS):
                            u = first_unit(s, n) + k
                            dve.wait_ge(S["y_done"], u + DONE)
                            if k == 0 and last:
                                dve.wait_ge(S[f"out_stored{n}"], s * 32 + 32)
                            if last:
                                nc.vector.scalar_tensor_tensor(rows(ys, n, k), as_rows(py[:, k % 2, :]), coef[:, n:n + 1],
                                                               rows(xs, n, k), ALU.mult, ALU.add).then_inc(S["y_ready"], 1)
                            else:
                                dve.wait_ge(S["stats_ready"], u + FREE)
                                nc.vector.tensor_tensor(rows(ys, n, k), as_rows(py[:, k % 2, :]), rows(xs, n, k), ALU.add
                                                        ).then_inc(S["y_ready"], 1)
                                dve.wait_ge(S["y_ready"], u + DONE)
                                if k == 0:
                                    dve.wait_ge(S[f"out_stored{n}"], s * 16 + 16)
                                nc.vector.bn_stats(st[:, n, 6 * k:6 * k + 6], rows(ys, n, k).rearrange("p r w -> p (r w)")
                                                   ).then_inc(S["stats_ready"], 1)


def backward(nc, sbt, pst, clear, c, S, allsems, x_in, prm, w1p, w2b, sc, bi, dbias, acc):
    names = """h_done gelu_ready z_ready zz_ready den_ready gz_ready density_ready tail_ready inverse_ready phi_ready
        dgelu_ready y_done y_ready d_done dh_ready ef_done summed
        turned_x turned_y turned_g0 turned_g1 turned_d0 turned_d1
        copied_x copied_y copied_g0 copied_g1 copied_d0 copied_d1""".split()
    clear(*allsems, start={S[k]: BODY for k in names})
    RING, LAG = BODY, 3
    assert BODY == 4

    def steps(eng, step):
        for i in range(BODY):
            step(0, i, lambda lag: i >= lag)
        with eng.Fori(1, STRIPS) as s:
            for i in range(BODY):
                step(s, i, lambda lag: True)
        for i in range(BODY):
            step(STRIPS, i, lambda lag: i < lag)

    def place(i, lag=0):
        return divmod((i - lag) % BODY, UNITS)

    with ExitStack() as ctx:
        xs = sbt(ctx, "xs", [P, N, SRP, W])
        g = sbt(ctx, "g", [P, RING, 2, COLS])
        z = sbt(ctx, "z", [P, RING, 2, COLS])
        zz = sbt(ctx, "zz", [P, RING, 2, COLS])
        den = sbt(ctx, "den", [P, RING, 2, COLS])
        gz = sbt(ctx, "gz", [P, RING, 2, COLS])
        ys = sbt(ctx, "ys", [P, RING, COLS])
        dh = sbt(ctx, "dh", [P, 2, 2, COLS])
        xt = sbt(ctx, "xt", [P, RING, 4, 2, 65])
        yt = sbt(ctx, "yt", [P, 4, 2, 65])
        gt = sbt(ctx, "gt", [P, 2, 4, HID])
        dt = sbt(ctx, "dt", [P, 2, 4, HID])
        ph = pst(ctx, "ps_h", [P, 2, COLS])
        pd = pst(ctx, "ps_d", [P, 2, COLS])
        py = pst(ctx, "ps_y", [P, COLS])
        pt = pst(ctx, "ps_t", [P, 2, 512])
        pe_ = pst(ctx, "ps_e", [P, 512])
        with nc.Block() as ones:
            @ones.vector
            def _(dve):
                for r in range(RING):
                    nc.vector.memset(xt[:, r, :, :, 64:65], 1.0)
                nc.vector.memset(yt[:, :, :, 64:65], 1.0)

        with nc.Block() as block:
            @block.sync
            def _(sp):
                with sp.Fori(0, STRIPS) as s:
                    for n in range(N):
                        sp.wait_ge(S["y_ready"], first_unit(s, n) + LAST)
                        sp.dma_start(xs[:, n, :, :], x_in[n, :, bass.ds(s * SRP + 1, SRP), :]
                                     ).then_inc(S[f"in_loaded{n}"], 16)

            @block.tensor
            def _(pe):
                def turn(src, slot, turned):
                    for b in range(4):
                        mm = nc.tensor.transpose(pt[:, slot, P * b:P * b + P], src[:, P * b:P * b + P], c("ident"))
                    mm.then_inc(S[turned], 1)

                def step(s, i, real):
                    u = s * BODY + i
                    v, r = u - LAG, (i - LAG) % RING
                    n, k = place(i)
                    nv, kv = place(i, LAG)
                    front, back = real(0), real(LAG)
                    if back:
                        pe.wait_ge(S["y_ready"], v + DONE)
                        pe.wait_ge(S["dh_ready"], v - 1 + DONE)
                        for par in range(2):
                            mm = nc.tensor.matmul(pd[:, par, :], w2b[:, par, :], ys[:, r, :], start=True, stop=True)
                        mm.then_inc(S["d_done"], 1)
                        pe.wait_ge(S["copied_d0"], v - 1 + DONE)
                        turn(g[:, r, 0, :], 0, "turned_g0")
                        pe.wait_ge(S["copied_d1"], v - 1 + DONE)
                        if not real(LAG + 1):
                            pe.wait_ge(S["copied_x"], u - 1 + DONE)
                        turn(g[:, r, 1, :], 1, "turned_g1")
                    if front:
                        pe.wait_ge(S["zz_ready"], u - 1 + DONE)
                        hidden_on_pe(nc, pe, S, u, s, n, k, w1p, xs, ph)
                    if back:
                        pe.wait_ge(S["copied_g0"], v + DONE)
                        turn(ys[:, r, :], 0, "turned_y")
                    if front:
                        if back:
                            pe.wait_ge(S["copied_g1"], v + DONE)
                        else:
                            pe.wait_ge(S["copied_x"], u - 1 + DONE)
                        turn(rows(xs, n, k).rearrange("p r w -> p (r w)"), 1, "turned_x")
                    if back:
                        pe.wait_ge(S["copied_y"], v + DONE)
                        pe.wait_ge(S["dh_ready"], v + DONE)
                        turn(dh[:, kv % 2, 0, :], 0, "turned_d0")
                        if front:
                            pe.wait_ge(S["copied_x"], u + DONE)
                        else:
                            pe.wait_ge(S["copied_g1"], v + DONE)
                        turn(dh[:, kv % 2, 1, :], 1, "turned_d1")
                    if front:
                        pe.wait_ge(S["gelu_ready"], u + DONE)
                        pe.wait_ge(S["y_ready"], u - 1 + DONE)
                        for par in range(2):
                            mm = nc.tensor.matmul(py[64 * par:64 * par + 64, :], prm[:, 64:128], g[:, i, par, :],
                                                  start=True, stop=True)
                        mm.then_inc(S["y_done"], 1)
                    if back:
                        pe.wait_ge(S["copied_d0"], v + DONE)
                        pe.wait_ge(S["copied_d1"], v + DONE)
                        if kv == 0:
                            pe.wait_ge(S["summed"], s * N + (i - LAG) // UNITS - 1 + DONE)
                        for b in range(4):
                            for par in range(2):
                                to, at = (31, 0) if par == 0 else (0, 34)
                                flat = xt[:, r, b, :, :].rearrange("p a c -> p (a c)")
                                nc.tensor.matmul(pe_[:, to:to + 96], dt[:, par, b, :], flat[:, at:at + 96],
                                                 start=(kv + par + b == 0), stop=False, skip_group_check=True)
                                flat = yt[:, b, :, :].rearrange("p a c -> p (a c)")
                                mm = nc.tensor.matmul(pe_[:, 128 + to:224 + to], gt[:, par, b, :], flat[:, at:at + 96],
                                                      start=False, stop=(kv == UNITS - 1 and par == 1 and b == 3),
                                                      skip_group_check=True)
                        mm.then_inc(S["ef_done"], 1)

                steps(pe, step)

            @block.scalar
            def _(act):
                def copy_hidden(v, dst, slot, name):
                    act.wait_ge(S["turned_" + name], v + DONE)
                    nc.scalar.copy(dst, pt[:, slot, :].rearrange("p (b c) -> p b c", b=4)
                                   ).then_inc(S["copied_" + name], 1)

                def copy_channels(v, dst, slot, name):
                    act.wait_ge(S["turned_" + name], v + DONE)
                    nc.scalar.copy(dst, pt[:, slot, :].rearrange("p (b a c) -> p b a c", b=4, a=2)
                                   ).then_inc(S["copied_" + name], 1)

                def step(s, i, real):
                    u = s * BODY + i
                    v = u - LAG
                    n, k = place(i)
                    front, back = real(0), real(LAG)

                    def affine(dst, func, name):
                        nc.scalar.activation(dst[:, i, :, :], ph[:, :, :], func, bias=bi[:, n:n + 1],
                                             scale=sc[:, n:n + 1]).then_inc(S[name], 1)

                    if back:
                        act.wait_ge(S["ef_done"], v - 1 + DONE)
                        copy_hidden(v, gt[:, 0, :, :], 0, "g0")
                        copy_hidden(v, gt[:, 1, :, :], 1, "g1")
                    if front:
                        act.wait_ge(S["h_done"], u + DONE)
                        act.wait_ge(S["turned_g1"], u - RING + DONE)
                        act.wait_ge(S["dgelu_ready"], u - RING + DONE)
                        affine(g, ACT.Gelu, "gelu_ready")
                    if back:
                        copy_channels(v, yt[:, :, :, 0:64], 0, "y")
                    if front:
                        act.wait_ge(S["ef_done"], u - RING + DONE)
                        copy_channels(u, xt[:, i, :, :, 0:64], 1, "x")
                        affine(z, ACT.Identity, "z_ready")
                    if back:
                        copy_hidden(v, dt[:, 1, :, :], 1, "d1")
                    if front:
                        affine(zz, ACT.Square, "zz_ready")
                        act.wait_ge(S["zz_ready"], u + DONE)
                        nc.scalar.activation(den[:, i, :, :], zz[:, i, :, :], ACT.Identity, bias=c("tiny")
                                             ).then_inc(S["den_ready"], 1)
                        if i % 2 == 1:
                            act.wait_ge(S["den_ready"], u + DONE)
                            for j in (i - 1, i):
                                nc.scalar.activation(zz[:, j, :, :], zz[:, j, :, :], ACT.Exp, bias=c("log_peak"),
                                                     scale=-0.5).then_inc(S["density_ready"], 1)

                steps(act, step)

            @block.gpsimd
            def _(pool):
                def step(s, i, real):
                    u = s * BODY + i
                    if real(2):
                        w, r = u - 2, (i - 2) % RING
                        pool.wait_ge(S["density_ready"], w + DONE)
                        pool.wait_ge(S["gz_ready"], w + DONE)
                        nc.gpsimd.tensor_tensor(z[:, r, :, :], zz[:, r, :, :], z[:, r, :, :], ALU.mult
                                                ).then_inc(S["tail_ready"], 1)
                        pool.wait_ge(S["tail_ready"], w + DONE)
                        pool.wait_ge(S["phi_ready"], w + DONE)
                        nc.gpsimd.tensor_tensor(gz[:, r, :, :], gz[:, r, :, :], z[:, r, :, :], ALU.add
                                                ).then_inc(S["dgelu_ready"], 1)
                    if real(0):
                        pool.wait_ge(S["z_ready"], u + DONE)
                        pool.wait_ge(S["dh_ready"], u - RING + DONE)
                        nc.gpsimd.tensor_tensor(gz[:, i, :, :], g[:, i, :, :], z[:, i, :, :], ALU.mult
                                                ).then_inc(S["gz_ready"], 1)

                steps(pool, step)

            @block.vector
            def _(dve):
                def step(s, i, real):
                    u = s * BODY + i
                    v, w = u - LAG, u - 1
                    nw, kw = place(i, 1)
                    r = (i - 1) % RING
                    if real(LAG):
                        j, slot = (i - LAG) % RING, (i - LAG) % 2
                        dve.wait_ge(S["d_done"], v + DONE)
                        dve.wait_ge(S["dgelu_ready"], v + DONE)
                        dve.wait_ge(S["turned_d1"], v - 2 + DONE)
                        nc.vector.scalar_tensor_tensor(dh[:, slot, :, :].rearrange("p a c -> p (a c)"),
                                                       pd[:, :, :].rearrange("p a c -> p (a c)"), dbias[:, 0:1],
                                                       gz[:, j, :, :].rearrange("p a c -> p (a c)"),
                                                       ALU.add, ALU.mult).then_inc(S["dh_ready"], 1)
                    if real(1):
                        dve.wait_ge(S["y_done"], w + DONE)
                        dve.wait_ge(S["turned_y"], w - RING + DONE)
                        nc.vector.tensor_tensor(as_rows(ys[:, r, :]), as_rows(py[:, :]), rows(xs, nw, kw), ALU.add
                                                ).then_inc(S["y_ready"], 1)
                    if real(BODY) and i % UNITS == UNITS - 1:
                        n = i // UNITS
                        sums = s * N + n - N
                        dve.wait_ge(S["ef_done"], u - BODY + DONE)
                        dve.wait_ge(S["summed"], sums - 1 + DONE)
                        nc.vector.tensor_tensor(acc[:, n, :].rearrange("p (a c) -> p a c", a=2),
                                                acc[:, n, :].rearrange("p (a c) -> p a c", a=2),
                                                pe_[:, 0:256].rearrange("p (a c) -> p a c", a=2)[:, :, 31:96], ALU.add
                                                ).then_inc(S["summed"], 1)
                    if real(1):
                        dve.wait_ge(S["den_ready"], w + DONE)
                        nc.vector.reciprocal(den[:, r, 0, :], den[:, r, 0, :])
                    if real(LAG):
                        dve.wait_ge(S["turned_d0"], v + DONE)
                        dve.wait_ge(S["ef_done"], v - 1 + DONE)
                        nc.vector.tensor_copy(dt[:, 0, :, :], pt[:, 0, :].rearrange("p (b c) -> p b c", b=4)
                                              ).then_inc(S["copied_d0"], 1)
                    if real(1):
                        nc.vector.reciprocal(den[:, r, 1, :], den[:, r, 1, :]).then_inc(S["inverse_ready"], 1)
                        dve.wait_ge(S["inverse_ready"], w + DONE)
                        dve.wait_ge(S["gz_ready"], w + DONE)
                        nc.vector.scalar_tensor_tensor(gz[:, r, :, :], gz[:, r, :, :], TINY / 2, den[:, r, :, :],
                                                       ALU.add, ALU.mult).then_inc(S["phi_ready"], 1)

                steps(dve, step)
_INS = ["x"] + [f"L0_conv_{k}" for k in "pos_w pos_b ln1_g ln1_b qkv_w qkv_b lepe_w lepe_b wo_w wo_b ln2_g ln2_b fc1_w fc1_b pw_w dw_w dw_b fc2_w fc2_b".split()] + [
    f"L1_conv_{k}" for k in "w1 gn_w gn_b w2 g1_w g1_b g2_w g2_b running_mean running_var residual_scale".split()]


def kernel(**inputs):
    import concourse.bacc as _bacc
    from concourse import mybir as _mybir
    from concourse.bass_utils import run_bass_kernel_spmd as _run

    nc = _bacc.Bacc("TRN2", target_bir_lowering=False, num_devices=1)
    arrays, args = {}, {}
    for name in _INS:
        a = np.ascontiguousarray(inputs[name])
        arrays[f"in_{name}"] = a
        args[name.replace("L0_conv_", "").replace("L1_conv_", "m_")] = nc.dram_tensor(
            f"in_{name}", a.shape, _mybir.dt.from_np(a.dtype), kind="ExternalInput").ap()
    cst, _ = constants()
    arrays["in_constants"] = cst
    args["cst"] = nc.dram_tensor("in_constants", cst.shape, _mybir.dt.float32, kind="ExternalInput").ap()
    out = nc.dram_tensor("out_image", [N, C, H, W], _mybir.dt.float32, kind="ExternalOutput").ap()
    build(nc, args, out)
    r = _run(nc, [arrays], core_ids=[0])
    return r.results[0]["out_image"]
```

```python
import numpy as np
import concourse.bass as bass
from concourse import mybir
from contextlib import ExitStack

N, C, H, W, D = 2, 64, 256, 256, 2
P = 128
RP = H // 2
SRP = 8
STRIPS = RP // SRP
UNIT = 2
UNITS = SRP // UNIT
COLS = UNIT * W
PADW = W + 4
HEADS, TOPK, SUB, NW = 8, 4, 16, 8
WINDOWS = NW * NW
WRP, WW = RP // NW, W // NW
WPIX = WRP * WW
KEYS = TOPK * SUB
LN_EPS, GN_EPS = 1e-6, 1e-5
HID, GROUP = 128, 16
PIX = H * W
TINY = 1e-30
INV_SQRT_2PI = 0.3989422804014327
DEVIATION_MAX = (3.4028234e38 / (GROUP * PIX)) ** 0.5
LR, MOM, STEPS = 0.01, 0.9, 2

fp32 = mybir.dt.float32
u32 = mybir.dt.uint32
ALU = mybir.AluOpType
ACT = mybir.ActivationFunctionType
AX = mybir.AxisListType


def constants():
    p = np.arange(P)
    eye = np.eye(P)
    half = (p[:, None] // 64 == p[None, :] // 64)
    col = np.arange(512)
    parts = {
        "ident": eye,
        "ident2": np.vstack([np.eye(64)] * 2),
        "center": eye - half / 64.0,
        "mean": half / 64.0,
        "pairmean": np.vstack([np.eye(64)] * 2) / 64.0,
        "group": (p[:, None] // GROUP == p[None, :] // GROUP) * 1.0,
        "headmask": np.vstack([(p[:64, None] // 8 == col[None, :] // 64)] * 2) * 1.0,
        "vmask": (col[None, :64] % 16 // 8 == p[:, None] // 64) * 1.0,
        "expand": 16.0 * (p[:, None] == (p[None, :] // SUB) % TOPK) + (p[:, None] == 8) * (p[None, :] % SUB),
        "pair": np.tile(np.eye(64), (2, 2)),
        "eps": np.full((P, 1), LN_EPS),
        "tiny": np.full((P, 1), TINY),
        "log_peak": np.full((P, 1), np.log(INV_SQRT_2PI)),
        "minus": -1.0 * (p[:, None] - 96 == col[None, :] // 64),
    }
    at, n = {}, 0
    for name, a in parts.items():
        at[name] = (n, n + a.shape[1])
        n += a.shape[1]
    return np.ascontiguousarray(np.hstack(list(parts.values())).astype(np.float32)), at


def build(nc, I, out):
    ctx = ExitStack()
    with ctx:
        build_in(nc, I, out, ctx)


class Link:

    def __init__(self, nc, sem, eng):
        self.sem, self.eng, self.n = sem, eng, 0

    def __call__(self, ins):
        ins.then_inc(self.sem, 1)
        self.n += 1
        self.eng.wait_ge(self.sem, self.n)


def build_in(nc, I, out, ctx):
    _, at = constants()

    def sem(name):
        return ctx.enter_context(nc.semaphore(name))

    def dram(name, shape):
        return nc.dram_tensor(name, shape, fp32, kind="Internal").ap()

    taken = {}

    def fresh(name):
        taken[name] = taken.get(name, 0) + 1
        return f"{name}_{taken[name]}"

    def sbt(c, name, shape, dt=fp32):
        return c.enter_context(nc.sbuf_tensor(fresh(name), shape, dt))

    def pst(c, name, shape):
        return c.enter_context(nc.psum_tensor(fresh(name), shape, fp32))

    def clear(*sems, start={}):
        with nc.Block() as reset:
            @reset.gpsimd
            def _(pool):
                for s in sems:
                    pool.sem_clear(s)
                for s, v in start.items():
                    pool.sem_inc(s, v)

    IMG = dram("IMG", [D + 1, N, P, RP + 2, W])
    X1 = dram("X1", [N, P, RP, W])
    XH = dram("XH", [N, P, RP + 2, W])
    AO = dram("AO", [N, P, RP, W])
    X2 = dram("X2", [N, P, RP, W])
    XH2 = dram("XH2", [N, P, RP + 2, W])
    POOL = dram("POOL", [N, P, RP // 4, W // 8])
    TAB = [dram(f"TAB{n}", [WINDOWS * SUB, P]) for n in range(N)]
    IDX = nc.dram_tensor("IDX", [N, WINDOWS, P], u32, kind="Internal").ap()
    AW = dram("AW", [N, WINDOWS, 64, 512])
    VW = dram("VW", [N, WINDOWS, P, 256])
    STAT = dram("STAT", [N, P, STRIPS, UNITS * 6])

    cst = sbt(ctx, "cst", [P, I["cst"].shape[1]])

    def c(name, p0=0, p1=P):
        return cst[p0:p1, at[name][0]:at[name][1]]

    ident = c("ident")
    s_init = sem("s_init")

    with ExitStack() as ph:
        zero = sbt(ph, "zero", [P, W])
        zeroed = sem("zeroed")
        with nc.Block() as block:
            @block.vector
            def _(dve):
                nc.vector.memset(zero[:, :], 0.0).then_inc(zeroed, 1)

            @block.sync
            def _(sp):
                k = 1
                sp.dma_start(cst[:, :], I["cst"]).then_inc(s_init, 16)
                xv = I["x"].rearrange("n c (r p) w -> n p c r w", p=2)
                for n in range(N):
                    for p in range(2):
                        sp.dma_start(IMG[0, n, 64 * p:64 * p + 64, 1:RP + 1, :], xv[n, p]).then_inc(s_init, 16)
                        k += 1
                sp.wait_ge(zeroed, 1)
                for n in range(N):
                    for a in [IMG[d, n] for d in range(D + 1)] + [XH[n], XH2[n]]:
                        for r in (0, RP + 1):
                            sp.dma_start(a[:, r, :], zero[:, :]).then_inc(s_init, 16)
                            k += 1
                sp.wait_ge(s_init, 16 * k)

    layer0(nc, I, sem, sbt, pst, clear, c, IMG, X1, XH, AO, X2, XH2, POOL, TAB, IDX, AW, VW)
    layer1(nc, I, sem, sbt, pst, clear, c, IMG, STAT, out)


def layer0(nc, I, sem, sbt, pst, clear, c, IMG, X1, XH, AO, X2, XH2, POOL, TAB, IDX, AW, VW):
    ident = c("ident")
    ctx = ExitStack()
    ctx.__enter__()
    posm = sbt(ctx, "posm", [P, 2, 4, P])
    posb = sbt(ctx, "posb", [P, 1])
    lepm = sbt(ctx, "lepm", [P, 3, 7, P])
    wodn = sbt(ctx, "wodn", [P, P])
    glum = sbt(ctx, "glum", [P, 2, 2, 4, HID])
    wn = sbt(ctx, "wn", [P, 448])
    wt = sbt(ctx, "wt", [P, 5, 2, 64])
    wod = sbt(ctx, "wod", [P, P])
    gvm = sbt(ctx, "gvm", [P, 2, HID])
    attb = sbt(ctx, "attb", [P, 1])
    fc2 = sbt(ctx, "fc2", [HID, 64])
    fc2b = sbt(ctx, "fc2b", [P, 1])
    dwb = sbt(ctx, "dwb", [HID, 1])
    w_loaded, link = sem("w_loaded"), sem("link")
    S = {k: sem(k) for k in """in_loaded0 in_loaded1 out_stored0 out_stored1
        values_loaded0 values_loaded1 x_stored0 x_stored1 conv_done x_ready centred squared var_done sd_ready rstd_ready xhat_ready plus_ready pooled_ready
        scored max_ready max_turned max_copied shifted probs_ready av_done recip_ready attn_ready
        idx_loaded0 idx_loaded1 rows_known k_turned k_masked a_done a_copied v_masked
        tiles_ready xbranch_done vbranch_done middle_ready partial_ready conv_ready gelu_ready gated fc2_done out_ready""".split()}
    gathered = [sem(f"gathered{n}") for n in range(N)]
    allsems = [w_loaded, link, *S.values()]

    with nc.Fori(0, D) as d:
        weights(nc, I, d, sbt, pst, clear, c, w_loaded, link, allsems,
                posm, posb, lepm, glum, gvm, wn, wt, wod, wodn, attb, fc2, fc2b, dwb)
        positional(nc, d, sbt, pst, clear, c, S, allsems, posm, posb, IMG, X1, XH, POOL)
        for n in range(N):
            routing(nc, n, sbt, pst, clear, c, w_loaded, link, wn, POOL, TAB, IDX)
        matrices(nc, d, sbt, pst, clear, c, S, allsems, gathered, wt, TAB, IDX, AW, VW)
        attention(nc, sbt, pst, clear, c, S, allsems, XH, AW, VW, AO)
        mixing(nc, sbt, pst, clear, c, S, allsems, lepm, wod, wodn, attb, XH, AO, X1, X2, XH2)
        glu(nc, d, sbt, pst, clear, c, S, allsems, glum, gvm, fc2, fc2b, dwb, XH2, X2, IMG)
    ctx.close()


def weights(nc, I, d, sbt, pst, clear, c, w_loaded, link, allsems,
            posm, posb, lepm, glum, gvm, wn, wt, wod, wodn, attb, fc2, fc2b, dwb):
    ident = c("ident")
    MS = [64, 64, 64, 128, 128]
    AT = [0, 64, 128, 192, 320]
    clear(*allsems)
    with ExitStack() as ph:
        raw = sbt(ph, "raw", [64, 448])
        wg = sbt(ph, "wg", [64, 448])
        lng = sbt(ph, "lng", [64, 2])
        lnb = sbt(ph, "lnb", [64, 2])
        bias = sbt(ph, "bias", [P, 5])
        sh = sbt(ph, "sh", [P, 5])
        rs = sbt(ph, "rs", [P, 5])
        posw = sbt(ph, "posw", [P, 3, 3])
        posp = sbt(ph, "posp", [P, 3, 4])
        posh = sbt(ph, "posh", [P, 3])
        lepw = sbt(ph, "lepw", [64, 25])
        lepb = sbt(ph, "lepb", [64, 1])
        wo2 = sbt(ph, "wo2", [64, 2, 64])
        wob = sbt(ph, "wob", [P, 1])
        lrhs = sbt(ph, "lrhs", [64, 32, 64])
        lt = sbt(ph, "lt", [P, 32, 64])
        pw = sbt(ph, "pw", [P, P])
        pwt = sbt(ph, "pwt", [P, P])
        wpt = sbt(ph, "wpt", [P, P])
        dw = sbt(ph, "dw", [P, 9])
        dwd = sbt(ph, "dwd", [P, 9, P])
        w9 = sbt(ph, "w9", [P, 9, P])
        glt = sbt(ph, "glt", [P, 4, 3, HID])
        outer = sbt(ph, "outer", [P, 4, HID])
        let = sbt(ph, "let", [P, 3, 5, P])
        louter = sbt(ph, "louter", [P, 3, P])
        ps = pst(ph, "ps_w", [P, 8, 512])

        with nc.Block() as load:
            @load.gpsimd
            def _(pool):
                pool.memset(wod[:, :], 0.0).then_inc(link, 1)
                pool.memset(posm[:, :, :, :], 0.0)
                pool.memset(let[:, :, :, :], 0.0)
                pool.memset(glt[:, :, :, :], 0.0)
                pool.memset(gvm[:, :, :], 0.0)
                pool.memset(lrhs[:, :, :], 0.0)
                pool.memset(bias[:, :], 0.0)
                pool.memset(sh[:, :], 0.0)
                pool.memset(wt[:, :, :, :], 0.0).then_inc(link, 1)

            @load.sync
            def _(sp):
                k = [0]

                def get(dst, src):
                    sp.dma_start(dst, src).then_inc(w_loaded, 16)
                    k[0] += 1

                def column(name, a=0, b=None):
                    v = I[name][d, a:b] if b else I[name][d]
                    return v.rearrange("(c o) -> c o", o=1)

                get(raw[:, 0:192], I["qkv_w"][d])
                get(raw[:, 192:448], I["fc1_w"][d])
                for i in range(2):
                    get(lng[:, i:i + 1], column(f"ln{i + 1}_g"))
                    get(lnb[:, i:i + 1], column(f"ln{i + 1}_b"))
                get(lepw[:, :], I["lepe_w"][d].rearrange("c o a b -> c (o a b)"))
                get(lepb[:, :], column("lepe_b"))
                get(pw[:, :], I["pw_w"][d].rearrange("o i a b -> o (i a b)"))
                get(dw[:, :], I["dw_w"][d].rearrange("c o a b -> c (o a b)"))
                get(dwb[:, :], column("dw_b"))
                get(fc2[:, :], I["fc2_w"][d])
                for h in range(2):
                    hp = slice(64 * h, 64 * h + 64)
                    get(posw[hp, :, :].rearrange("c a b -> c (a b)"), I["pos_w"][d].rearrange("c o a b -> c (o a b)"))
                    get(posb[hp, :], column("pos_b"))
                    get(wob[hp, :], column("wo_b"))
                    get(fc2b[hp, :], column("fc2_b"))
                    get(wo2[:, h, :], I["wo_w"][d])
                sp.wait_ge(link, 2)
                for h in range(2):
                    for j in range(4):
                        q = 32 * j + 16 * h
                        get(wod[q:q + 16, 64 * h:64 * h + 64], I["wo_w"][d, 16 * j:16 * j + 16, :])
                for i in range(5):
                    src = column("qkv_b", AT[i], AT[i] + 64) if i < 3 else column("fc1_b", 128 * (i - 3), 128 * (i - 2))
                    get(bias[0:MS[i], i:i + 1], src)
                sp.wait_ge(w_loaded, 16 * k[0])

        clear(link)
        with nc.Block() as fold:
            @fold.vector
            def _(dve):
                step = Link(nc, link, dve)
                nc.vector.tensor_scalar(wg[:, 0:192], raw[:, 0:192], lng[:, 0:1], None, ALU.mult)
                nc.vector.tensor_scalar(wg[:, 192:448], raw[:, 192:448], lng[:, 1:2], None, ALU.mult)
                nc.vector.tensor_tensor(lrhs[:, 0:25, :], wo2[:, 0:1, :].to_broadcast([64, 25, 64]),
                                        lepw[:, :, None].to_broadcast([64, 25, 64]), ALU.mult)
                nc.vector.tensor_tensor(dwd[:, :, :], ident[:, None, :].to_broadcast([P, 9, P]),
                                        dw[:, :, None].to_broadcast([P, 9, P]), ALU.mult)
                step(nc.vector.tensor_scalar_add(posw[:, 1, 1:2], posw[:, 1, 1:2], 1.0))
                step(nc.vector.tensor_copy(posp[:, :, 0], posw[:, :, 0]))
                step(nc.vector.tensor_copy(posp[:, :, 3], posw[:, :, 2]))
                step(nc.vector.tensor_tensor(posh[:, :], posw[:, :, 0], posw[:, :, 2], ALU.add))
                step(nc.vector.tensor_scalar_mul(posh[:, :], posh[:, :], 0.5))
                for t, half in ((1, 0.5), (2, -0.5)):
                    step(nc.vector.scalar_tensor_tensor(posp[:, :, t], posw[:, :, 1], half, posh[:, :],
                                                        ALU.mult, ALU.add))
                for j in range(2):
                    hp = slice(64 * j, 64 * j + 64)
                    for g in range(2):
                        for par in range(2):
                            t = 2 * g + j - par
                            if 0 <= t < 3:
                                nc.vector.tensor_tensor(
                                    posm[hp, g, :, 64 * par:64 * par + 64],
                                    c("ident2")[hp, None, :].to_broadcast([64, 4, 64]),
                                    posp[hp, t, :, None].to_broadcast([64, 4, 64]), ALU.mult)

        with nc.Block() as turn:
            @turn.tensor
            def _(pe):
                for i in range(5):
                    w = slice(AT[i], AT[i] + MS[i])
                    nc.tensor.transpose(ps[0:MS[i], 0, 64 * i:64 * i + 64], wg[:, w], ident[0:64, 0:64])
                    nc.tensor.matmul(ps[0:MS[i], 1, i:i + 1], raw[:, w], lnb[:, (i > 2):(i > 2) + 1],
                                     start=True, stop=True)
                nc.tensor.matmul(ps[:, 2, 0:1], wo2[:, :, :].rearrange("c a o -> c (a o)"), lepb[:, :],
                                 start=True, stop=True)
                nc.tensor.transpose(ps[:, 3, 0:P], pw[:, :], ident)

        clear(link)
        with nc.Block() as tilde:
            @tilde.vector
            def _(dve):
                step = Link(nc, link, dve)
                nc.vector.tensor_copy(pwt[:, :], ps[:, 3, 0:P])
                nc.vector.tensor_tensor(attb[:, :], ps[:, 2, 0:1], wob[:, :], ALU.add)
                for i in range(5):
                    m = slice(0, MS[i])
                    step(nc.vector.reduce_sum(rs[m, i:i + 1], ps[m, 0, 64 * i:64 * i + 64], AX.X))
                    step(nc.vector.tensor_tensor(sh[m, i:i + 1], ps[m, 1, i:i + 1], rs[m, i:i + 1], ALU.subtract))
                    step(nc.vector.tensor_tensor(sh[m, i:i + 1], sh[m, i:i + 1], bias[m, i:i + 1], ALU.add))
                    step(nc.vector.tensor_scalar_mul(sh[m, i:i + 1], sh[m, i:i + 1], 1.0 / C))
                    for b in range(2):
                        nc.vector.tensor_scalar(wt[m, i, b, :], ps[m, 0, 64 * i:64 * i + 64], sh[m, i:i + 1],
                                                C ** -0.5 if i == 0 else 1.0, ALU.add, ALU.mult)

        with nc.Block() as back:
            @back.tensor
            def _(pe):
                for i in range(5):
                    nc.tensor.transpose(ps[:, 0, AT[i]:AT[i] + MS[i]],
                                        wt[0:MS[i], i, :, :].rearrange("m a c -> m (a c)"), ident[0:MS[i], 0:MS[i]])
                for q in range(4):
                    nc.tensor.matmul(ps[:, 1 + q, :], wt[0:64, 2, :, :].rearrange("m a c -> m (a c)"),
                                     lrhs[:, 8 * q:8 * q + 8, :].rearrange("c t o -> c (t o)"), start=True, stop=True)
                nc.tensor.matmul(ps[:, 5, 0:P], pwt[:, :], wt[:, 3, :, :].rearrange("m a c -> m (a c)"),
                                 start=True, stop=True)

        with nc.Block() as keep:
            @keep.vector
            def _(dve):
                nc.vector.tensor_copy(wn[:, :], ps[:, 0, 0:448])
                nc.vector.tensor_copy(wpt[:, :], ps[:, 5, 0:P])

            @keep.scalar
            def _(act):
                for q in range(4):
                    nc.scalar.copy(lt[:, 8 * q:8 * q + 8, :], ps[:, 1 + q, :].rearrange("p (t o) -> p t o", t=8))

        with nc.Block() as taps:
            @taps.tensor
            def _(pe):
                for t in range(3):
                    nc.tensor.matmul(ps[:, t, 0:384], wpt[:, :],
                                     dwd[:, 3 * t:3 * t + 3, :].rearrange("p t o -> p (t o)"), start=True, stop=True)

            @taps.vector
            def _(dve):
                for j in range(2):
                    hp = slice(64 * j, 64 * j + 64)
                    for g in range(3):
                        for par in range(2):
                            t = 2 * g + j - par
                            if 0 <= t < 5:
                                nc.vector.tensor_copy(let[hp, g, :, 64 * par:64 * par + 64],
                                                      lt[hp, 5 * t:5 * t + 5, :])

        with nc.Block() as place:
            @place.vector
            def _(dve):
                for j in range(2):
                    hp = slice(64 * j, 64 * j + 64)
                    nc.vector.tensor_copy(gvm[hp, j, :], wn[hp, 320:448])
                    for par in range(2):
                        for gi in range(2):
                            t = 2 * (gi - 1 + par) + j - par + 1
                            if 0 <= t < 3:
                                nc.vector.tensor_copy(glt[hp, 2 * par + gi, :, :],
                                                      ps[hp, t, 0:384].rearrange("p (x o) -> p x o", x=3))

        clear(link)
        with nc.Block() as points:
            @points.vector
            def _(dve):
                step = Link(nc, link, dve)
                to = glum[:, :, :, :, :].rearrange("p a g t o -> p (a g) t o")
                nc.vector.tensor_copy(to[:, :, 0, :], glt[:, :, 0, :])
                nc.vector.tensor_copy(to[:, :, 3, :], glt[:, :, 2, :])
                step(nc.vector.tensor_tensor(outer[:, :, :], glt[:, :, 0, :], glt[:, :, 2, :], ALU.add))
                step(nc.vector.tensor_scalar_mul(outer[:, :, :], outer[:, :, :], 0.5))
                for t, half in ((1, 0.5), (2, -0.5)):
                    nc.vector.scalar_tensor_tensor(to[:, :, t, :], glt[:, :, 1, :], half, outer[:, :, :],
                                                   ALU.mult, ALU.add)
                nc.vector.tensor_scalar_mul(wodn[:, :], wod[:, :], -1.0)
                nc.vector.tensor_copy(lepm[:, :, 0, :], let[:, :, 0, :])
                nc.vector.tensor_copy(lepm[:, :, 3, :], let[:, :, 2, :])
                nc.vector.tensor_copy(lepm[:, :, 6, :], let[:, :, 4, :])
                nc.vector.tensor_scalar_mul(lepm[:, :, 4, :], let[:, :, 3, :], -1.0)
                nc.vector.tensor_tensor(lepm[:, :, 5, :], let[:, :, 3, :], let[:, :, 4, :], ALU.add)
                step(nc.vector.tensor_tensor(louter[:, :, :], let[:, :, 0, :], let[:, :, 2, :], ALU.add))
                step(nc.vector.tensor_scalar_mul(louter[:, :, :], louter[:, :, :], 0.5))
                for t, half in ((1, 0.5), (2, -0.5)):
                    nc.vector.scalar_tensor_tensor(lepm[:, :, t, :], let[:, :, 1, :], half, louter[:, :, :],
                                                   ALU.mult, ALU.add)



BODY = N * UNITS
DONE, FREE, LAST = BODY + 1, BODY - 1, UNITS
UNIT_SEMS = "rstd_ready conv_done x_ready centred squared var_done sd_ready xhat_ready plus_ready fc2_done out_ready".split()


def first_unit(s, n):
    return s * BODY + n * UNITS


def run_strips(sp, load, store):
    for n in range(N):
        load(0, n)
    with sp.Fori(0, STRIPS - 1) as s:
        for n in range(N):
            load(s + 1, n)
            store(s, n)
    for n in range(N):
        store(STRIPS - 1, n)


def in_steps(eng, depth, step):
    def steps(s, i, real):
        def at(lag):
            n, k = divmod((i - lag) % BODY, UNITS)
            return (s - (i < lag), n, k, s * BODY + i - lag) if real(lag) else None
        step(at)

    for i in range(BODY):
        steps(0, i, lambda lag: i >= lag)
    with eng.Fori(1, STRIPS) as s:
        for i in range(BODY):
            steps(s, i, lambda lag: True)
    for i in range(depth):
        steps(STRIPS, i, lambda lag: i < lag)


def rows(t, n, k):
    return t[:, n, UNIT * k:UNIT * k + UNIT, :]


def as_rows(a):
    return a.rearrange("p (r w) -> p r w", w=W)


def norm_on_pe(nc, pe, c, S, u, x, sq, pc, pv, n, k, step):
    if step == "centre":
        pe.wait_ge(S["x_ready"], u + DONE)
        pe.wait_ge(S["xhat_ready"], u + FREE)
        nc.tensor.matmul(pc[:, k % 2, :], c("center"), rows(x, n, k), start=True, stop=True).then_inc(S["centred"], 1)
    else:
        pe.wait_ge(S["squared"], u + DONE)
        pe.wait_ge(S["sd_ready"], u + FREE)
        nc.tensor.matmul(pv[:, k % 2, :], c("mean"), sq[:, k % 2, :], start=True, stop=True).then_inc(S["var_done"], 1)


def norm_on_dve(nc, dve, S, u, k, sd, rstd, xr, pc):
    dve.wait_ge(S["sd_ready"], u + DONE)
    dve.wait_ge(S["plus_ready"], u + FREE)
    nc.vector.reciprocal(rstd[:, k % 2, :], sd[:, k % 2, :]).then_inc(S["rstd_ready"], 1)
    dve.wait_ge(S["rstd_ready"], u + DONE)
    nc.vector.tensor_tensor(xr[:, k % 2, :], pc[:, k % 2, :], rstd[:, k % 2, :], ALU.mult).then_inc(S["xhat_ready"], 1)


def sqrt_on_act(nc, act, S, u, k, sd, pv, eps):
    act.wait_ge(S["var_done"], u + DONE)
    act.wait_ge(S["xhat_ready"], u + FREE)
    nc.scalar.activation(sd[:, k % 2, :], pv[:, k % 2, :], ACT.Sqrt, bias=eps).then_inc(S["sd_ready"], 1)


def square_on_act(nc, act, S, u, k, sq, pc):
    act.wait_ge(S["centred"], u + DONE)
    act.wait_ge(S["var_done"], u + FREE)
    nc.scalar.activation(sq[:, k % 2, :], pc[:, k % 2, :], ACT.Square).then_inc(S["squared"], 1)


def plus_on_act(nc, act, S, u, k, n, xr, xh):
    act.wait_ge(S["xhat_ready"], u + DONE)
    nc.scalar.add(rows(xh, n, k), as_rows(xr[:, k % 2, :]), 1.0).then_inc(S["plus_ready"], 1)


def input_sums(nc, pool, S, xs, xd, loads, used):
    T = W // 2
    with pool.Fori(0, STRIPS) as s:
        for n in range(N):
            pool.wait_ge(S[f"in_loaded{n}"], loads(s))
            last, value = used(s, n)
            pool.wait_ge(S[last], value)
            pairs = xs[:, n, :, :].rearrange("p r (w e) -> p e r w", e=2)
            d0, d1 = pairs[:, 1, :, 0:T], pairs[:, 0, :, 1:T + 1]
            d2, d3 = pairs[:, 1, :, 1:T + 1], pairs[:, 0, :, 2:T + 2]
            nc.gpsimd.tensor_tensor(xd[:, n, 0, :, :], d0, d2, ALU.subtract)
            nc.gpsimd.tensor_tensor(xd[:, n, 1, :, :], d1, d2, ALU.add)
            nc.gpsimd.tensor_tensor(xd[:, n, 2, :, :], d2, d1, ALU.subtract)
            nc.gpsimd.tensor_tensor(xd[:, n, 3, :, :], d1, d3, ALU.subtract).then_inc(S["tiles_ready"], 1)


def positional(nc, d, sbt, pst, clear, c, S, allsems, posm, posb, IMG, X1, XH, POOL):
    T = W // 2
    clear(*allsems, start={**{S[k]: BODY for k in UNIT_SEMS}, S["tiles_ready"]: N,
                           S["x_stored0"]: 16, S["x_stored1"]: 16,
                           S["out_stored0"]: 32, S["out_stored1"]: 32})
    with ExitStack() as ph:
        xs = sbt(ph, "p_xs", [P, N, SRP + 1, PADW])
        xd = sbt(ph, "p_xd", [P, N, 4, SRP + 1, T])
        middle = sbt(ph, "p_middle", [P, 2, 2, COLS // 2])
        partial = sbt(ph, "p_partial", [P, 2, 2, COLS // 2])
        x1 = sbt(ph, "p_x1", [P, N, SRP, W])
        sq = sbt(ph, "p_sq", [P, 2, COLS])
        sd = sbt(ph, "p_sd", [P, 2, COLS])
        rstd = sbt(ph, "p_rstd", [P, 2, COLS])
        xr = sbt(ph, "p_xr", [P, 2, COLS])
        xh = sbt(ph, "p_xh", [P, N, SRP, W])
        pooled = sbt(ph, "p_pool", [P, N, SRP // 4, W // 8])
        px = pst(ph, "ps_x", [P, 2, 4, COLS // 2])
        pc = pst(ph, "ps_c", [P, 2, COLS])
        pv = pst(ph, "ps_v", [P, 2, COLS])
        with nc.Block() as border:
            @border.vector
            def _(dve):
                nc.vector.memset(xs[:, :, :, 0:2], 0.0)
                nc.vector.memset(xs[:, :, :, PADW - 2:PADW], 0.0)

        with nc.Block() as block:
            @block.sync
            def _(sp):
                def load(s, n):
                    sp.wait_ge(S["tiles_ready"], s * N + n + 1)
                    for j in range(2):
                        sp.dma_start(xs[64 * j:64 * j + 64, n, :, 2:2 + W],
                                     IMG[d, n, 64 - 64 * j:128 - 64 * j, bass.ds(s * SRP + j, SRP + 1), :]
                                     ).then_inc(S[f"in_loaded{n}"], 16)

                def store(s, n):
                    sp.wait_ge(S["x_ready"], first_unit(s, n) + UNITS - 1 + DONE)
                    sp.dma_start(X1[n, :, bass.ds(s * SRP, SRP), :], x1[:, n, :, :]).then_inc(S[f"x_stored{n}"], 16)
                    sp.wait_ge(S["plus_ready"], first_unit(s, n) + UNITS - 1 + DONE)
                    sp.dma_start(XH[n, :, bass.ds(s * SRP + 1, SRP), :], xh[:, n, :, :]).then_inc(S[f"out_stored{n}"], 16)
                    sp.wait_ge(S["pooled_ready"], s * N + n + 1)
                    sp.dma_start(POOL[n, :, bass.ds(s * (SRP // 4), SRP // 4), :], pooled[:, n, :, :]).then_inc(S[f"out_stored{n}"], 16)

                run_strips(sp, load, store)
                for n in range(N):
                    sp.wait_ge(S[f"x_stored{n}"], 16 * (STRIPS + 1))
                    sp.wait_ge(S[f"out_stored{n}"], 32 * (STRIPS + 1))

            @block.tensor
            def _(pe):
                def conv(s, n, k):
                    u = first_unit(s, n) + k
                    if k == 0:
                        pe.wait_ge(S["tiles_ready"], s * N + n + N + 1)
                    pe.wait_ge(S["x_ready"], u + FREE)
                    for t in range(4):
                        for g in range(2):
                            mm = nc.tensor.matmul(px[:, k % 2, t, :], posm[:, g, t, :],
                                                  xd[:, n, t, UNIT * k + g:UNIT * k + g + UNIT, :],
                                                  start=(g == 0), stop=(g == 1))
                    mm.then_inc(S["conv_done"], 1)

                def step(at):
                    if at(0):
                        conv(*at(0)[:3])
                    for lag, part in ((1, "centre"), (2, "var")):
                        if at(lag):
                            _, n, k, u = at(lag)
                            norm_on_pe(nc, pe, c, S, u, x1, sq, pc, pv, n, k, part)

                in_steps(pe, 2, step)

            @block.gpsimd
            def _(pool):
                input_sums(nc, pool, S, xs, xd, lambda s: s * 32 + 32,
                           lambda s, n: ("conv_done", first_unit(s, n) + LAST))

            @block.scalar
            def _(act):
                def step(at):
                    if at(0):
                        _, n, k, u = at(0)
                        act.wait_ge(S["conv_done"], u + DONE)
                        act.wait_ge(S["x_ready"], u + FREE)
                        nc.scalar.copy(middle[:, k % 2, :, :], px[:, k % 2, 1:3, :]).then_inc(S["middle_ready"], 1)
                    if at(1):
                        _, n, k, u = at(1)
                        square_on_act(nc, act, S, u, k, sq, pc)
                    if at(2):
                        _, n, k, u = at(2)
                        sqrt_on_act(nc, act, S, u, k, sd, pv, c("eps"))
                    if at(3):
                        s, n, k, u = at(3)
                        if k == 0:
                            act.wait_ge(S[f"out_stored{n}"], s * 32 + 32)
                        plus_on_act(nc, act, S, u, k, n, xr, xh)

                in_steps(act, 3, step)

            @block.vector
            def _(dve):
                def pool_rows(s, n):
                    dve.wait_ge(S["plus_ready"], first_unit(s, n) + UNITS - 1 + DONE)
                    dve.wait_ge(S[f"out_stored{n}"], s * 32 + 32)
                    for q in range(SRP // 4):
                        ins = nc.vector.tensor_reduce(
                            pooled[:, n, q, :], xh[:, n, 4 * q:4 * q + 4, :].rearrange("p r (b x) -> p b r x", x=8),
                            AX.XY, ALU.add)
                    ins.then_inc(S["pooled_ready"], 1)

                def untangle(s, n, k):
                    u = first_unit(s, n) + k
                    m1, m2 = middle[:, k % 2, 0, :], middle[:, k % 2, 1, :]
                    dve.wait_ge(S["middle_ready"], u + 1)
                    nc.vector.scalar_tensor_tensor(partial[:, k % 2, 0, :], m1, posb[:, 0:1], m2, ALU.add, ALU.add)
                    nc.vector.scalar_tensor_tensor(partial[:, k % 2, 1, :], m1, posb[:, 0:1], m2, ALU.add, ALU.subtract
                                                   ).then_inc(S["partial_ready"], 1)
                    dve.wait_ge(S["partial_ready"], u + 1)
                    if k == 0:
                        dve.wait_ge(S[f"x_stored{n}"], s * 16 + 16)
                    both = rows(x1, n, k).rearrange("p r (w e) -> p e r w", e=2)
                    half = lambda a: a.rearrange("p (r w) -> p r w", w=T)
                    nc.vector.tensor_tensor(both[:, 0, :, :], half(partial[:, k % 2, 0, :]), half(px[:, k % 2, 0, :]), ALU.add)
                    nc.vector.tensor_tensor(both[:, 1, :, :], half(partial[:, k % 2, 1, :]), half(px[:, k % 2, 3, :]),
                                            ALU.subtract).then_inc(S["x_ready"], 1)

                def step(at):
                    if at(0):
                        untangle(*at(0)[:3])
                    if at(2):
                        _, n, k, u = at(2)
                        norm_on_dve(nc, dve, S, u, k, sd, rstd, xr, pc)
                    if at(4) and at(4)[2] == UNITS - 1:
                        pool_rows(*at(4)[:2])

                in_steps(dve, 4, step)


def routing(nc, n, sbt, pst, clear, c, w_loaded, link, wn, POOL, TAB, IDX):
    ident = c("ident")
    with ExitStack() as ph:
        sums = sbt(ph, "r_sums", [P, 1024])
        pm = sbt(ph, "r_pm", [64, WINDOWS, SUB])
        win = sbt(ph, "r_win", [64, WINDOWS])
        tab = sbt(ph, "r_tab", [P, 8, P])
        qk = sbt(ph, "r_qk", [64, 2, WINDOWS])
        lg = sbt(ph, "r_lg", [64, WINDOWS])
        top = sbt(ph, "r_top", [64, 8])
        best = sbt(ph, "r_best", [64, 8], u32)
        bestf = sbt(ph, "r_bestf", [64, 8])
        bt = sbt(ph, "r_bt", [P, WINDOWS])
        idx = sbt(ph, "r_idx", [WINDOWS, P], u32)
        ps = pst(ph, "ps_r", [P, 8, 512])
        clear(w_loaded)
        with nc.Block() as load:
            @load.sync
            def _(sp):
                sp.dma_start(sums[:, :], POOL[n].rearrange("p s b -> p (s b)")).then_inc(w_loaded, 16)
                sp.wait_ge(w_loaded, 16)

            @load.gpsimd
            def _(pool):
                pool.memset(bt[:, :], 1.0)
        with nc.Block() as mean:
            @mean.tensor
            def _(pe):
                for h in range(2):
                    nc.tensor.matmul(ps[0:64, h, :], c("pairmean"), sums[:, 512 * h:512 * h + 512], start=True, stop=True)
        clear(link)
        with nc.Block() as sort:
            @sort.vector
            def _(dve):
                step = Link(nc, link, dve)
                for wy in range(NW):
                    src = ps[0:64, wy // 4, 128 * (wy % 4):128 * (wy % 4) + 128]
                    ins = nc.vector.tensor_copy(
                        pm[:, NW * wy:NW * wy + NW, :].rearrange("c w (y x) -> c w y x", x=4),
                        src.rearrange("c (y w x) -> c w y x", y=4, x=4))
                    step(ins)
                step(nc.vector.reduce_sum(win[:, :], pm[:, :, :], AX.X))
                nc.vector.tensor_scalar_mul(win[:, :], win[:, :], 1.0 / SUB)
        with nc.Block() as project:
            @project.tensor
            def _(pe):
                rows_of = pm[:, :, :].rearrange("c w s -> c (w s)")
                for i in range(8):
                    nc.tensor.matmul(ps[:, i // 4, P * (i % 4):P * (i % 4) + P], rows_of[:, P * i:P * i + P],
                                     wn[0:64, 64:192], start=True, stop=True)
                for i in range(2):
                    nc.tensor.matmul(ps[0:64, 2 + i, 0:WINDOWS], wn[0:64, 64 * i:64 * i + 64], win[:, :],
                                     start=True, stop=True)
        clear(w_loaded)
        with nc.Block() as keep:
            @keep.vector
            def _(dve):
                for i in range(2):
                    nc.vector.tensor_copy(tab[:, 4 * i:4 * i + 4, :], ps[:, i, :].rearrange("p (t c) -> p t c", t=4))
                    nc.vector.tensor_copy(qk[:, i, :], ps[0:64, 2 + i, 0:WINDOWS])
        with nc.Block() as logits:
            @logits.sync
            def _(sp):
                sp.dma_start(TAB[n].rearrange("(t p) c -> p t c", p=P), tab[:, :, :]).then_inc(w_loaded, 16)
                sp.wait_ge(w_loaded, 16)

            @logits.tensor
            def _(pe):
                nc.tensor.matmul(ps[0:64, 4, 0:WINDOWS], qk[:, 0, :], qk[:, 1, :], start=True, stop=True)
        clear(link)
        with nc.Block() as choose:
            @choose.vector
            def _(dve):
                step = Link(nc, link, dve)
                step(nc.vector.tensor_copy(lg[:, :], ps[0:64, 4, 0:WINDOWS]))
                step(nc.vector.max(top[:, :], lg[:, :]))
                step(nc.vector.max_index(best[:, :], top[:, :], lg[:, :]))
                nc.vector.tensor_copy(bestf[:, :], best[:, :])
        with nc.Block() as turn:
            @turn.tensor
            def _(pe):
                nc.tensor.transpose(ps[0:8, 5, 0:64], bestf[:, :], ident[0:64, 0:64])
        with nc.Block() as keep_turned:
            @keep_turned.vector
            def _(dve):
                nc.vector.tensor_copy(bt[0:8, :], ps[0:8, 5, 0:64])
        with nc.Block() as expand:
            @expand.tensor
            def _(pe):
                nc.tensor.matmul(ps[0:WINDOWS, 6, 0:P], bt[:, :], c("expand"), start=True, stop=True)
        with nc.Block() as number:
            @number.vector
            def _(dve):
                nc.vector.tensor_copy(idx[:, :], ps[0:WINDOWS, 6, 0:P])
        clear(w_loaded)
        with nc.Block() as store:
            @store.sync
            def _(sp):
                sp.dma_start(IDX[n], idx[:, :]).then_inc(w_loaded, 16)
                sp.wait_ge(w_loaded, 16)


def matrices(nc, d, sbt, pst, clear, c, S, allsems, gathered, wt, TAB, IDX, AW, VW):
    per_window = "k_turned k_masked a_done a_copied v_masked".split()
    clear(*allsems, start={**{S[k]: N for k in per_window},
                           **{S[f"out_stored{n}"]: 32 for n in range(N)}})
    with ExitStack() as ph:
        idc = sbt(ph, "m_idc", [P, N, 1], u32)
        kv = [sbt(ph, f"m_kv{n}", [P, P]) for n in range(N)]
        kb = sbt(ph, "m_kb", [64, N, 512])
        aw = sbt(ph, "m_aw", [64, N, 512])
        vw = sbt(ph, "m_vw", [P, N, 2, 4, 32])
        pk = pst(ph, "ps_k", [P, N, 512])
        pa = pst(ph, "ps_a", [P, N, 512])
        idx1 = [sbt(ph, f"m_idx{n}", [P, 1], u32) for n in range(N)]
        with nc.Block() as zero:
            @zero.vector
            def _(dve):
                nc.vector.memset(vw[:, :, :, :, :], 0.0)

        with nc.Block() as block:
            @block.sync
            def _(sp):
                with sp.Fori(0, WINDOWS) as w:
                    for n in range(N):
                        sp.wait_ge(S["k_turned"], w * N + n + 1)
                        sp.dma_start(idx1[n][:, :], IDX[n, w].rearrange("(p o) -> p o", o=1)).then_inc(S[f"idx_loaded{n}"], 16)

            @block.gpsimd
            def _(pool):
                with pool.Fori(0, WINDOWS) as w:
                    for n in range(N):
                        pool.wait_ge(S["v_masked"], w * N + n + 1)
                        pool.wait_ge(S["k_turned"], w * N + n + 1)
                        pool.wait_ge(S[f"idx_loaded{n}"], w * 16 + 16)
                        pool.sem_inc(S["rows_known"], 1)
                        pool.indirect_dma_start(kv[n][:, :], None, TAB[n],
                                                bass.IndirectOffsetOnAxis(ap=idx1[n][:, 0:1], axis=0)
                                                ).then_inc(gathered[n], 16)

            @block.tensor
            def _(pe):
                with pe.Fori(0, WINDOWS) as w:
                    for n in range(N):
                        pe.wait_ge(gathered[n], (d * WINDOWS + w) * 16 + 16)
                        pe.wait_ge(S["k_masked"], w * N + n + 1)
                        nc.tensor.transpose(pk[:, n, 0:P], kv[n][:, :], c("ident")).then_inc(S["k_turned"], 1)
                    for n in range(N):
                        pe.wait_ge(S["k_masked"], w * N + n + 1 + N)
                        pe.wait_ge(S["a_copied"], w * N + n + 1)
                        nc.tensor.matmul(pa[:, n, :], wt[0:64, 0, :, :].rearrange("m a c -> m (a c)"), kb[:, n, :], start=True, stop=True
                                         ).then_inc(S["a_done"], 1)

            @block.vector
            def _(dve):
                with dve.Fori(0, WINDOWS) as w:
                    for n in range(N):
                        dve.wait_ge(S["k_turned"], w * N + n + 1 + N)
                        dve.wait_ge(S["a_done"], w * N + n + 1)
                        nc.vector.tensor_tensor(kb[:, n, :].rearrange("c (h k) -> c h k", h=HEADS),
                                                pk[0:64, n, None, 0:64].to_broadcast([64, HEADS, 64]),
                                                c("headmask", 0, 64).rearrange("c (h k) -> c h k", h=HEADS), ALU.mult
                                                ).then_inc(S["k_masked"], 1)
                    for n in range(N):
                        dve.wait_ge(gathered[n], (d * WINDOWS + w) * 16 + 16)
                        dve.wait_ge(S[f"out_stored{n}"], w * 32 + 32)
                        for h in range(2):
                            ins = nc.vector.tensor_tensor(vw[:, n, h, :, 16 * h:16 * h + 16],
                                                          kv[n][:, 64:128].rearrange("p (j i) -> p j i", j=4),
                                                          c("vmask").rearrange("p (j i) -> p j i", j=4), ALU.mult)
                        ins.then_inc(S["v_masked"], 1)

            @block.scalar
            def _(act):
                with act.Fori(0, WINDOWS) as w:
                    for n in range(N):
                        act.wait_ge(S["a_done"], w * N + n + 1 + N)
                        act.wait_ge(S[f"out_stored{n}"], w * 32 + 32)
                        nc.scalar.copy(aw[:, n, :], pa[0:64, n, :]).then_inc(S["a_copied"], 1)
                        act.wait_ge(S["a_copied"], w * N + n + 1 + N)
                        act.dma_start(AW[n, w], aw[:, n, :]).then_inc(S[f"out_stored{n}"], 16)
                        act.wait_ge(S["v_masked"], w * N + n + 1 + N)
                        act.dma_start(VW[n, w], vw[:, n, :, :, :].rearrange("p h j c -> p (h j c)")).then_inc(S[f"out_stored{n}"], 16)
                for n in range(N):
                    act.wait_ge(S[f"out_stored{n}"], 32 * (WINDOWS + 1))


def attention(nc, sbt, pst, clear, c, S, allsems, XH, AW, VW, AO):
    T, HALF = 8, 2
    TD, TF = N * T + 1, N * T - 1
    HD = N * HALF + 1
    QD, QF = 2 * N * HALF + 1, 2 * N * HALF - 1
    ND = N + 1
    MR = 96
    clear(*allsems, start={**{S[k]: N * T for k in ("scored", "max_ready")},
                           **{S[k]: N * HALF for k in "max_turned max_copied av_done".split()},
                           **{S[k]: N for k in "recip_ready attn_ready".split()},
                           **{S[k]: 2 * N * HALF for k in ("shifted", "probs_ready")},
                           S["out_stored0"]: 16, S["out_stored1"]: 16})
    with ExitStack() as ph:
        xw = sbt(ph, "a_xw", [MR + HEADS, N, HALF * WPIX])
        aw = sbt(ph, "a_aw", [MR + HEADS, N, 512])
        vw = sbt(ph, "a_vw", [P, N, HALF, 4, 32])
        ones = sbt(ph, "a_ones", [P, HALF, 4, 32])
        mx = sbt(ph, "a_mx", [P, N, T, HEADS])
        pr = sbt(ph, "a_pr", [P, HALF, 4, WPIX])
        rc = sbt(ph, "a_rc", [P, WPIX])
        ao = sbt(ph, "a_ao", [P, N, WPIX])
        ps = pst(ph, "ps_s", [P, 2, 512])
        pk = pst(ph, "ps_t", [P, 2, 2, WPIX])
        po = pst(ph, "ps_o", [P, 2, WPIX])
        pm = ps
        with nc.Block() as fixed:
            @fixed.vector
            def _(dve):
                nc.vector.memset(xw[64:MR, :, :], 0.0)
                nc.vector.memset(aw[64:MR, :, :], 0.0)
                nc.vector.memset(ones[:, :, :, :], 0.0)

        with nc.Block() as masks:
            @masks.vector
            def _(dve):
                for n in range(N):
                    nc.vector.tensor_copy(aw[MR:MR + HEADS, n, :], c("minus", MR, MR + HEADS))
                for h in range(HALF):
                    nc.vector.tensor_copy(ones[:, h, :, 16 * h:16 * h + 16], c("vmask").rearrange("p (j i) -> p j i", j=4))

        with nc.Block() as block:
            def half(w, n, h):
                return w * (N * HALF) + n * HALF + h

            @block.sync
            def _(sp):
                def load(wy, wx, n):
                    w = sp.snap(wy * NW + wx)
                    sp.wait_ge(S["shifted"], 2 * half(w, n, 0) - 2 * N * HALF + 3 + QD)
                    sp.dma_start(aw[0:64, n, :], AW[n, w]).then_inc(S[f"in_loaded{n}"], 16)
                    for h in range(HALF):
                        sp.dma_start(xw[0:64, n, WPIX * h:WPIX * h + WPIX].rearrange("c (r x) -> c r x", x=WW),
                                     XH[n, 64 * h:64 * h + 64, bass.ds(wy * WRP + 1, WRP), bass.ds(wx * WW, WW)]
                                     ).then_inc(S[f"in_loaded{n}"], 16)
                    sp.wait_ge(S["av_done"], half(w, n, 0) + 2)
                    sp.dma_start(vw[:, n, :, :, :].rearrange("p h j c -> p (h j c)"), VW[n, w]
                                 ).then_inc(S[f"values_loaded{n}"], 16)

                with sp.Fori(0, NW) as wy:
                    with sp.Fori(0, NW) as wx:
                        for n in range(N):
                            load(wy, wx, n)

            @block.scalar
            def _(act):
                def copy_max(w, n, h):
                    act.wait_ge(S["max_turned"], half(w, n, h) + HD)
                    nc.scalar.copy(xw[MR:MR + HEADS, n, WPIX * h:WPIX * h + WPIX], pm[0:8, h, :]
                                   ).then_inc(S["max_copied"], 1)

                def exps(w, n, h):
                    act.wait_ge(S["av_done"], half(w, n, h) - 2 + HD)
                    for b in range(2):
                        act.wait_ge(S["shifted"], 2 * half(w, n, h) + b + QD)
                        nc.scalar.activation(pr[:, h, 2 * b:2 * b + 2, :], pk[:, b, :, :], ACT.Exp
                                             ).then_inc(S["probs_ready"], 1)

                def store(w, wy, wx, n):
                    act.wait_ge(S["attn_ready"], w * N + n + ND)
                    act.dma_start(AO[n, :, bass.ds(wy * WRP, WRP), bass.ds(wx * WW, WW)],
                                  ao[:, n, :].rearrange("c (r x) -> c r x", x=WW)).then_inc(S[f"out_stored{n}"], 16)

                def window(wy, wx, last=False):
                    w = wy * NW + wx if last else act.snap(wy * NW + wx)
                    exps(w, 0, 0)
                    exps(w, 0, 1)
                    copy_max(w, 1, 0)
                    copy_max(w, 1, 1)
                    exps(w, 1, 0)
                    store(w, wy, wx, 0)
                    exps(w, 1, 1)
                    if not last:
                        copy_max(w + 1, 0, 0)
                        copy_max(w + 1, 0, 1)
                    store(w, wy, wx, 1)

                copy_max(0, 0, 0)
                copy_max(0, 0, 1)
                with act.Fori(0, NW - 1) as wy:
                    with act.Fori(0, NW) as wx:
                        window(wy, wx)
                with act.Fori(0, NW - 1) as wx:
                    window(NW - 1, wx)
                window(NW - 1, NW - 1, last=True)
                for n in range(N):
                    act.wait_ge(S[f"out_stored{n}"], 16 * (WINDOWS + 1))

            @block.tensor
            def _(pe):
                def by_pixel(w, n, t):
                    i = w * (N * T) + n * T + t
                    if t == 0:
                        pe.wait_ge(S[f"in_loaded{n}"], w * 48 + 48)
                        pe.wait_ge(S["max_copied"], half(w, n, 0) - 1 + HD)
                    pe.wait_ge(S["max_ready"], i + TF)
                    nc.tensor.matmul(ps[:, t % 2, :], xw[0:MR, n, P * t:P * t + P], aw[0:MR, n, :], start=True, stop=True
                                     ).then_inc(S["scored"], 1)

                def turn(w, n, h):
                    pe.wait_ge(S["max_ready"], w * (N * T) + n * T + T - 1 + TD)
                    for q in range(4):
                        mm = nc.tensor.transpose(pm[0:8, h, P * q:P * q + P], mx[:, n, 4 * h + q, :], c("ident"))
                    mm.then_inc(S["max_turned"], 1)

                def by_key(w, n, h):
                    pe.wait_ge(S["max_copied"], half(w, n, h) + HD)
                    for b in range(2):
                        pe.wait_ge(S["probs_ready"], 2 * half(w, n, h) + b + QF)
                        for q in range(2):
                            j = 2 * b + q
                            mm = nc.tensor.matmul(pk[:, b, q, :], aw[:, n, P * j:P * j + P],
                                                  xw[:, n, WPIX * h:WPIX * h + WPIX], start=True, stop=True)
                        mm.then_inc(S["shifted"], 1)

                def sum_up(w, n, h):
                    pe.wait_ge(S["probs_ready"], 2 * half(w, n, h) + 1 + QD)
                    if h == 0:
                        pe.wait_ge(S[f"values_loaded{n}"], w * 16 + 16)
                        pe.wait_ge(S["attn_ready"], w * N + n - 1 + ND)
                    for kind, matrix in enumerate((vw[:, n, :, :, :], ones)):
                        for j in range(4):
                            mm = nc.tensor.matmul(po[32 * j:32 * j + 32, kind, :], matrix[:, h, j, :], pr[:, h, j, :],
                                                  start=(h == 0), stop=(h == 1))
                    mm.then_inc(S["av_done"], 1)

                def maxima(w, n, tiles):
                    for t in tiles:
                        by_pixel(w, n, t)

                def turns(w, n):
                    for h in range(HALF):
                        turn(w, n, h)

                def window(w, n, following):
                    by_key(w, n, 0)
                    if following:
                        maxima(*following, range(2))
                    by_key(w, n, 1)
                    if following:
                        maxima(*following, range(2, T))
                    sum_up(w, n, 0)
                    if following:
                        turns(*following)
                    sum_up(w, n, 1)

                maxima(0, 0, range(T))
                turns(0, 0)
                with pe.Fori(0, WINDOWS - 1) as w:
                    window(w, 0, (w, 1))
                    window(w, 1, (w + 1, 0))
                window(WINDOWS - 1, 0, (WINDOWS - 1, 1))
                window(WINDOWS - 1, 1, None)

            @block.vector
            def _(dve):
                def maxima(w, n):
                    for t in range(T):
                        dve.wait_ge(S["scored"], w * (N * T) + n * T + t + TD)
                        nc.vector.reduce_max(mx[:, n, t, :], ps[:, t % 2, :].rearrange("p (h k) -> p h k", h=HEADS), AX.X
                                             ).then_inc(S["max_ready"], 1)

                def divide(w, n):
                    i = w * N + n
                    dve.wait_ge(S["av_done"], half(w, n, 1) + HD)
                    dve.wait_ge(S[f"out_stored{n}"], w * 16 + 16)
                    dve.wait_ge(S["attn_ready"], i - 1 + ND)
                    nc.vector.reciprocal(rc[:, :], po[:, 1, :]).then_inc(S["recip_ready"], 1)
                    dve.wait_ge(S["recip_ready"], i + ND)
                    nc.vector.tensor_tensor(ao[:, n, :], po[:, 0, :], rc[:, :], ALU.mult
                                            ).then_inc(S["attn_ready"], 1)

                maxima(0, 0)
                with dve.Fori(0, WINDOWS - 1) as w:
                    maxima(w, 1)
                    divide(w, 0)
                    maxima(w + 1, 0)
                    divide(w, 1)
                maxima(WINDOWS - 1, 1)
                divide(WINDOWS - 1, 0)
                divide(WINDOWS - 1, 1)


def mixing(nc, sbt, pst, clear, c, S, allsems, lepm, wod, wodn, attb, XH, AO, X1, X2, XH2):
    clear(*allsems, start={**{S[k]: BODY for k in UNIT_SEMS}, S["x_stored0"]: 16, S["x_stored1"]: 16,
                           S["out_stored0"]: 16, S["out_stored1"]: 16})
    T = W // 2
    with ExitStack() as ph:
        xs = sbt(ph, "x_xs", [P, N, SRP + 2, PADW])
        xd = sbt(ph, "x_xd", [P, N, 5, SRP + 2, W // 2 + 1])
        middle = sbt(ph, "x_middle", [P, 2, 2, COLS // 2])
        partial = sbt(ph, "x_partial", [P, 2, COLS // 2])
        xc = sbt(ph, "x_xc", [P, COLS])
        ao = sbt(ph, "x_ao", [P, N, SRP, W])
        x1 = sbt(ph, "x_x1", [P, N, SRP, W])
        x2 = sbt(ph, "x_x2", [P, N, SRP, W])
        sq = sbt(ph, "x_sq", [P, 2, COLS])
        sd = sbt(ph, "x_sd", [P, 2, COLS])
        xr = sbt(ph, "x_xr", [P, 2, COLS])
        xh = sbt(ph, "x_xh", [P, N, SRP, W])
        px = pst(ph, "ps_x", [P, 2, 4, COLS // 2])
        pc = pst(ph, "ps_c", [P, 2, COLS])
        pv = pst(ph, "ps_v", [P, 2, COLS])
        with nc.Block() as border:
            @border.vector
            def _(dve):
                nc.vector.memset(xs[:, :, :, 0:2], 0.0)
                nc.vector.memset(xs[:, :, :, PADW - 2:PADW], 0.0)

        with nc.Block() as block:
            @block.sync
            def _(sp):
                def load(s, n):
                    sp.wait_ge(S["conv_done"], first_unit(s, n) + LAST)
                    sp.wait_ge(S["x_ready"], first_unit(s, n) + LAST)
                    for dst, src in ((xs[:, n, :, 2:2 + W], XH[n, :, bass.ds(s * SRP, SRP + 2), :]),
                                     (ao[:, n, :, :], AO[n, :, bass.ds(s * SRP, SRP), :]),
                                     (x1[:, n, :, :], X1[n, :, bass.ds(s * SRP, SRP), :])):
                        sp.dma_start(dst, src).then_inc(S[f"in_loaded{n}"], 16)

                def store(s, n):
                    sp.wait_ge(S["x_ready"], first_unit(s, n) + UNITS - 1 + DONE)
                    sp.dma_start(X2[n, :, bass.ds(s * SRP, SRP), :], x2[:, n, :, :]).then_inc(S[f"x_stored{n}"], 16)
                    sp.wait_ge(S["plus_ready"], first_unit(s, n) + UNITS - 1 + DONE)
                    sp.dma_start(XH2[n, :, bass.ds(s * SRP + 1, SRP), :], xh[:, n, :, :]).then_inc(S[f"out_stored{n}"], 16)

                run_strips(sp, load, store)
                for n in range(N):
                    sp.wait_ge(S[f"x_stored{n}"], 16 * (STRIPS + 1))
                    sp.wait_ge(S[f"out_stored{n}"], 16 * (STRIPS + 1))

            @block.tensor
            def _(pe):
                def conv(s, n, k):
                    u = first_unit(s, n) + k
                    if k == 0:
                        pe.wait_ge(S["tiles_ready"], s * N + n + 1)
                    pe.wait_ge(S["x_ready"], u + FREE)
                    r = UNIT * k
                    d4 = xs[:, n, :, :].rearrange("p r (w e) -> p e r w", e=2)[:, 0, :, 2:2 + T]
                    attention = rows(ao, n, k).rearrange("p r (w e) -> p e r w", e=2)
                    at = lambda t, x=0: lambda g: xd[:, n, t, r + g:r + g + UNIT, x:x + T]
                    terms = (((0, at(0)), (4, at(2, 1))), ((1, at(1)), (5, lambda g: d4[:, r + g:r + g + UNIT, :])),
                             ((2, at(2)),), ((3, at(3)), (6, at(4))))
                    for a, pair in enumerate(terms):
                        if a in (0, 3):
                            nc.tensor.matmul(px[:, k % 2, a, :], (wod if a == 0 else wodn)[:, :],
                                             attention[:, a % 2, :, :], start=True, stop=False)
                        for q, source in pair:
                            for g in range(3):
                                mm = nc.tensor.matmul(px[:, k % 2, a, :], lepm[:, g, q, :], source(g),
                                                      start=(a in (1, 2) and g == 0 and q == pair[0][0]),
                                                      stop=(g == 2 and q == pair[-1][0]))
                    mm.then_inc(S["conv_done"], 1)

                def step(at):
                    if at(0):
                        conv(*at(0)[:3])
                    for lag, part in ((1, "centre"), (2, "var")):
                        if at(lag):
                            _, n, k, u = at(lag)
                            norm_on_pe(nc, pe, c, S, u, x2, sq, pc, pv, n, k, part)

                in_steps(pe, 2, step)

            @block.gpsimd
            def _(pool):
                with pool.Fori(0, STRIPS) as s:
                    for n in range(N):
                        pool.wait_ge(S[f"in_loaded{n}"], s * 48 + 48)
                        pool.wait_ge(S["conv_done"], first_unit(s, n) + LAST)
                        pairs = xs[:, n, :, :].rearrange("p r (w e) -> p e r w", e=2)
                        even, odd = pairs[:, 0, :, :], pairs[:, 1, :, :]
                        d0, d1, d2, d3 = even[:, :, 0:T], odd[:, :, 0:T], even[:, :, 1:T + 1], odd[:, :, 1:T + 1]
                        d4, d5 = even[:, :, 2:T + 2], odd[:, :, 2:T + 2]
                        nc.gpsimd.tensor_tensor(xd[:, n, 0, :, 0:T], d0, d2, ALU.subtract)
                        nc.gpsimd.tensor_tensor(xd[:, n, 1, :, 0:T], d1, d2, ALU.add)
                        nc.gpsimd.tensor_tensor(xd[:, n, 2, :, :], even[:, :, 1:T + 2], odd[:, :, 0:T + 1], ALU.subtract)
                        nc.gpsimd.tensor_tensor(xd[:, n, 3, :, 0:T], d1, d3, ALU.subtract)
                        nc.gpsimd.tensor_tensor(xd[:, n, 4, :, 0:T], d4, d5, ALU.subtract
                                                ).then_inc(S["tiles_ready"], 1)

            @block.scalar
            def _(act):
                def step(at):
                    if at(0):
                        _, n, k, u = at(0)
                        act.wait_ge(S["conv_done"], u + DONE)
                        act.wait_ge(S["x_ready"], u + FREE)
                        nc.scalar.copy(middle[:, k % 2, :, :], px[:, k % 2, 1:3, :]).then_inc(S["middle_ready"], 1)
                    if at(1):
                        _, n, k, u = at(1)
                        square_on_act(nc, act, S, u, k, sq, pc)
                    if at(2):
                        _, n, k, u = at(2)
                        sqrt_on_act(nc, act, S, u, k, sd, pv, c("eps"))
                    if at(3):
                        s, n, k, u = at(3)
                        if k == 0:
                            act.wait_ge(S[f"out_stored{n}"], s * 16 + 16)
                        plus_on_act(nc, act, S, u, k, n, xr, xh)

                in_steps(act, 3, step)

            @block.vector
            def _(dve):
                def untangle(s, n, k):
                    u = first_unit(s, n) + k
                    a1, a2 = middle[:, k % 2, 0, :], middle[:, k % 2, 1, :]
                    dve.wait_ge(S["middle_ready"], u + 1)
                    nc.vector.scalar_tensor_tensor(partial[:, 0, :], a1, attb[:, 0:1], a2, ALU.add, ALU.add)
                    nc.vector.scalar_tensor_tensor(partial[:, 1, :], a1, attb[:, 0:1], a2, ALU.add, ALU.subtract
                                                   ).then_inc(S["partial_ready"], 1)
                    dve.wait_ge(S["partial_ready"], u + 1)
                    both = xc[:, :].rearrange("p (w e) -> p e w", e=2)
                    nc.vector.tensor_tensor(both[:, 0, :], partial[:, 0, :], px[:, k % 2, 0, :], ALU.add)
                    nc.vector.tensor_tensor(both[:, 1, :], partial[:, 1, :], px[:, k % 2, 3, :], ALU.subtract
                                            ).then_inc(S["conv_ready"], 1)
                    dve.wait_ge(S["conv_ready"], u + 1)
                    if k == 0:
                        dve.wait_ge(S[f"x_stored{n}"], s * 16 + 16)
                    nc.vector.tensor_tensor(rows(x2, n, k), as_rows(xc[:, :]), rows(x1, n, k), ALU.add
                                            ).then_inc(S["x_ready"], 1)

                def step(at):
                    if at(0):
                        untangle(*at(0)[:3])
                    if at(2):
                        _, n, k, u = at(2)
                        norm_on_dve(nc, dve, S, u, k, sd, sd, xr, pc)

                in_steps(dve, 2, step)


def glu(nc, d, sbt, pst, clear, c, S, allsems, glum, gvm, fc2, fc2b, dwb, XH2, X2, IMG):
    PBODY = 2 * BODY
    PD, PF = PBODY + 1, PBODY - 1
    clear(*allsems, start={**{S[k]: BODY for k in ("fc2_done", "out_ready")},
                           **{S[k]: PBODY for k in "xbranch_done vbranch_done conv_ready gelu_ready gated".split()},
                           S["out_stored0"]: 16, S["out_stored1"]: 16})
    with ExitStack() as ph:
        xs = sbt(ph, "g_xs", [P, N, SRP + 2, PADW])
        xd = sbt(ph, "g_xd", [P, N, 4, SRP + 2, W // 2])
        x2 = sbt(ph, "g_x2", [P, N, SRP, W])
        middle = sbt(ph, "g_middle", [HID, 2, 2, COLS // 2])
        partial = sbt(ph, "g_partial", [HID, 2, 2, COLS // 2])
        xc = sbt(ph, "g_xc", [HID, 2, COLS])
        ge = sbt(ph, "g_ge", [HID, 2, COLS])
        gv = sbt(ph, "g_gv", [HID, 2, COLS])
        xo = sbt(ph, "g_xo", [P, N, SRP, W])
        px = pst(ph, "ps_x", [HID, 2, 4, COLS // 2])
        pv = pst(ph, "ps_v", [HID, 2, COLS])
        po = pst(ph, "ps_o", [P, 2, COLS])
        with nc.Block() as border:
            @border.vector
            def _(dve):
                nc.vector.memset(xs[:, :, :, 0:2], 0.0)
                nc.vector.memset(xs[:, :, :, PADW - 2:PADW], 0.0)

        with nc.Block() as block:
            @block.sync
            def _(sp):
                def load(s, n):
                    sp.wait_ge(S["vbranch_done"], 2 * (first_unit(s, n) + LAST))
                    sp.dma_start(xs[:, n, :, 2:2 + W], XH2[n, :, bass.ds(s * SRP, SRP + 2), :]
                                 ).then_inc(S[f"in_loaded{n}"], 16)
                    sp.wait_ge(S["out_ready"], first_unit(s, n) + LAST)
                    sp.dma_start(x2[:, n, :, :], X2[n, :, bass.ds(s * SRP, SRP), :]).then_inc(S[f"in_loaded{n}"], 16)

                def store(s, n):
                    sp.wait_ge(S["out_ready"], first_unit(s, n) + UNITS - 1 + DONE)
                    sp.dma_start(IMG[d + 1, n, :, bass.ds(s * SRP + 1, SRP), :], xo[:, n, :, :]
                                 ).then_inc(S[f"out_stored{n}"], 16)

                run_strips(sp, load, store)
                for n in range(N):
                    sp.wait_ge(S[f"out_stored{n}"], 16 * (STRIPS + 1))

            @block.tensor
            def _(pe):
                def branches(s, n, k, par):
                    v = 2 * (first_unit(s, n) + k) + par
                    if k + par == 0:
                        pe.wait_ge(S["tiles_ready"], s * N + n + 1)
                    pe.wait_ge(S["conv_ready"], v + PF)
                    for t in range(4):
                        for g in range(2):
                            r = UNIT * k + g + par
                            mm = nc.tensor.matmul(px[:, par, t, :], glum[:, par, g, t, :], xd[:, n, t, r:r + UNIT, :],
                                                  start=(g == 0), stop=(g == 1))
                    mm.then_inc(S["xbranch_done"], 1)
                    pe.wait_ge(S["gated"], v + PF)
                    nc.tensor.matmul(pv[:, par, :], gvm[:, par, :],
                                     xs[:, n, UNIT * k + 1:UNIT * k + 1 + UNIT, 2:2 + W], start=True, stop=True
                                     ).then_inc(S["vbranch_done"], 1)

                def project(s, n, k):
                    u = first_unit(s, n) + k
                    pe.wait_ge(S["out_ready"], u + FREE)
                    for par in range(2):
                        pe.wait_ge(S["gated"], 2 * u + par + PD)
                        mm = nc.tensor.matmul(po[64 * par:64 * par + 64, k % 2, :], fc2[:, :], gv[:, par, :],
                                              start=True, stop=True)
                    mm.then_inc(S["fc2_done"], 1)

                with pe.Fori(0, STRIPS) as s:
                    for i in range(BODY + 1):
                        if i < BODY:
                            for par in range(2):
                                branches(s, i // UNITS, i % UNITS, par)
                        if i >= 1:
                            project(s, (i - 1) // UNITS, (i - 1) % UNITS)

            @block.gpsimd
            def _(pool):
                input_sums(nc, pool, S, xs, xd, lambda s: s * 32 + 32,
                           lambda s, n: ("xbranch_done", 2 * (first_unit(s, n) + LAST)))

            @block.scalar
            def _(act):
                with act.Fori(0, STRIPS) as s:
                    for n in range(N):
                        for k in range(UNITS):
                            for par in range(2):
                                v = 2 * (first_unit(s, n) + k) + par
                                act.wait_ge(S["xbranch_done"], v + PD)
                                act.wait_ge(S["conv_ready"], v + PF)
                                nc.scalar.copy(middle[:, par, :, :], px[:, par, 1:3, :]).then_inc(S["middle_ready"], 1)
                                act.wait_ge(S["conv_ready"], v + PD)
                                act.wait_ge(S["gated"], v + PF)
                                nc.scalar.activation(ge[:, par, :], xc[:, par, :], ACT.Gelu, bias=dwb[:, 0:1]
                                                     ).then_inc(S["gelu_ready"], 1)

            @block.vector
            def _(dve):
                def gate(s, n, k, par):
                    u = first_unit(s, n) + k
                    dve.wait_ge(S["gelu_ready"], 2 * u + par + PD)
                    dve.wait_ge(S["vbranch_done"], 2 * u + par + PD)
                    dve.wait_ge(S["fc2_done"], u - 1 + DONE)
                    nc.vector.tensor_tensor(gv[:, par, :], pv[:, par, :], ge[:, par, :], ALU.mult
                                            ).then_inc(S["gated"], 1)

                def untangle(s, n, k, par):
                    v = 2 * (first_unit(s, n) + k) + par
                    m1, m2 = middle[:, par, 0, :], middle[:, par, 1, :]
                    dve.wait_ge(S["middle_ready"], v + 1)
                    nc.vector.tensor_tensor(partial[:, par, 0, :], m1, m2, ALU.add)
                    nc.vector.tensor_tensor(partial[:, par, 1, :], m1, m2, ALU.subtract
                                            ).then_inc(S["partial_ready"], 1)
                    dve.wait_ge(S["partial_ready"], v + 1)
                    dve.wait_ge(S["gelu_ready"], v + PF)
                    out = xc[:, par, :].rearrange("p (w e) -> p e w", e=2)
                    nc.vector.tensor_tensor(out[:, 0, :], partial[:, par, 0, :], px[:, par, 0, :], ALU.add)
                    nc.vector.tensor_tensor(out[:, 1, :], partial[:, par, 1, :], px[:, par, 3, :], ALU.subtract
                                            ).then_inc(S["conv_ready"], 1)

                def add(s, n, k):
                    u = first_unit(s, n) + k
                    dve.wait_ge(S["fc2_done"], u + DONE)
                    if k == 0:
                        dve.wait_ge(S[f"out_stored{n}"], s * 16 + 16)
                    nc.vector.scalar_tensor_tensor(rows(xo, n, k), as_rows(po[:, k % 2, :]), fc2b[:, 0:1],
                                                   rows(x2, n, k), ALU.add, ALU.add).then_inc(S["out_ready"], 1)

                with dve.Fori(0, STRIPS) as s:
                    for h in range(PBODY + 1):
                        i, par = divmod(h, 2)
                        if h < PBODY:
                            untangle(s, i // UNITS, i % UNITS, par)
                        if h >= 1:
                            i, par = divmod(h - 1, 2)
                            gate(s, i // UNITS, i % UNITS, par)
                            if par == 0 and i >= 1:
                                add(s, (i - 1) // UNITS, (i - 1) % UNITS)
                    add(s, N - 1, UNITS - 1)
def layer1(nc, I, sem, sbt, pst, clear, c, IMG, STAT, out):
    ctx = ExitStack()
    ctx.__enter__()
    x_in = IMG[D]
    W1, W2, GW, GB = slice(0, 64), slice(64, 128), slice(128, 129), slice(129, 130)
    prm = sbt(ctx, "prm", [P, 130])
    mom = sbt(ctx, "mom", [P, 130])
    w1t = sbt(ctx, "w1t", [P, HID])
    w2n = sbt(ctx, "w2n", [P, HID])
    w1p = sbt(ctx, "w1p", [P, 2, HID])
    w2b = sbt(ctx, "w2b", [P, 2, HID])
    gram = sbt(ctx, "gram", [P, N, P + 1])
    gm = sbt(ctx, "gm", [P, N, 65])
    cov = sbt(ctx, "cov", [P, N, 64])
    mub = sbt(ctx, "mub", [P, N, 64])
    mg = sbt(ctx, "mg", [P, N])
    rstd = sbt(ctx, "rstd", [P, N])
    sc = sbt(ctx, "sc", [P, N])
    bi = sbt(ctx, "bi", [P, N])
    coef = sbt(ctx, "coef", [P, N])
    run = sbt(ctx, "run", [P, 2])
    ab = sbt(ctx, "ab", [P, 2])
    abb = sbt(ctx, "abb", [P, 2, 64])
    dbias = sbt(ctx, "dbias", [P, 1])
    acc = sbt(ctx, "acc", [P, N, 130])
    m_loaded, m_link = sem("m_loaded"), sem("m_link")
    S = {k: sem("m_" + k) for k in """in_loaded0 in_loaded1 out_stored0 out_stored1 turned copied gram_done summed
        h_done gelu_ready z_ready zz_ready den_ready gz_ready density_ready tail_ready inverse_ready phi_ready
        dgelu_ready y_done y_ready stats_ready d_done dh_ready ef_done out_ready
        turned_x turned_y turned_g0 turned_g1 turned_d0 turned_d1
        copied_x copied_y copied_g0 copied_g1 copied_d0 copied_d1""".split()}
    allsems = [m_loaded, m_link, *S.values()]
    env = (nc, sbt, pst, clear, c, S, allsems)

    clear(*allsems)
    with ExitStack() as ph:
        w2 = sbt(ph, "w2", [64, HID])
        g1 = sbt(ph, "g1", [16, 64])
        g1t = sbt(ph, "g1t", [64, 16])
        g1b = sbt(ph, "g1b", [16, 1])
        g2 = sbt(ph, "g2", [16, 1])
        g2r = sbt(ph, "g2r", [16, P])
        g2b = sbt(ph, "g2b", [P, 1])
        res = sbt(ph, "res", [P, 1])
        own = sbt(ph, "own", [P, N, 65])
        mur = sbt(ph, "mur", [64, N, P])
        gg = sbt(ph, "gg", [16, N])
        mm = sbt(ph, "mm", [P, 64])
        first = ExitStack()
        ps = pst(first, "ps_m", [P, 2, 512])
        with nc.Block() as load:
            @load.sync
            def _(sp):
                k = [0]

                def get(dst, src):
                    sp.dma_start(dst, src).then_inc(m_loaded, 16)
                    k[0] += 1

                def column(name):
                    return I[name].rearrange("(c o) -> c o", o=1)

                get(prm[:, W1], I["m_w1"])
                get(prm[:, GW], column("m_gn_w"))
                get(prm[:, GB], column("m_gn_b"))
                get(w2[:, :], I["m_w2"])
                get(g1[:, :], I["m_g1_w"])
                get(g1b[:, :], column("m_g1_b"))
                get(g2[:, :], I["m_g2_w"].rearrange("a c -> c a"))
                get(g2b[:, :], column("m_g2_b").to_broadcast([P, 1]))
                get(res[:, :], column("m_residual_scale").to_broadcast([P, 1]))
                for h in range(2):
                    get(run[64 * h:64 * h + 64, 0:1], column("m_running_mean"))
                    get(run[64 * h:64 * h + 64, 1:2], column("m_running_var"))
                sp.wait_ge(m_loaded, 16 * k[0])

            @load.gpsimd
            def _(pool):
                pool.memset(mom[:, :], 0.0)
                pool.memset(w1p[:, :, :], 0.0)
                pool.memset(w2b[:, :, :], 0.0)
                pool.memset(gram[:, :, :], 0.0)

        with nc.Block() as turn:
            @turn.tensor
            def _(pe):
                nc.tensor.transpose(ps[:, 0, 0:64], w2[:, :], c("ident", 0, 64)[:, 0:64])
                nc.tensor.transpose(ps[0:64, 1, 0:16], g1[:, :], c("ident", 0, 16)[:, 0:16])

        with nc.Block() as keep:
            @keep.vector
            def _(dve):
                nc.vector.tensor_copy(prm[:, W2], ps[:, 0, 0:64])
                nc.vector.tensor_copy(g1t[:, :], ps[0:64, 1, 0:16])
                nc.vector.tensor_copy(g2r[:, :], g2[:, 0:1].to_broadcast([16, P]))

        first.close()
        gram_pass(*env, x_in, gram)
        ps = pst(ph, "ps_m", [P, 8, 512])

        clear(m_link)
        with nc.Block() as blocks:
            @blocks.vector
            def _(dve):
                for n in range(N):
                    for h in range(2):
                        hp = slice(64 * h, 64 * h + 64)
                        nc.vector.tensor_copy(own[hp, n, 0:64], gram[hp, n, 64 * h:64 * h + 64])
                    nc.vector.tensor_copy(own[:, n, 64:65], gram[:, n, P:P + 1])

        with nc.Block() as parities:
            @parities.tensor
            def _(pe):
                for n in range(N):
                    nc.tensor.matmul(ps[:, n, 0:65], c("pair"), own[:, n, :], start=True, stop=True)

        clear(m_link)
        with nc.Block() as means:
            @means.vector
            def _(dve):
                step = Link(nc, m_link, dve)
                for n in range(N):
                    step(nc.vector.tensor_scalar_mul(gm[:, n, :], ps[:, n, 0:65], 1.0 / PIX))
                    nc.vector.tensor_copy(mur[:, n, :], gm[0:64, n, 64:65].to_broadcast([64, P]))

        with nc.Block() as spread:
            @spread.tensor
            def _(pe):
                for n in range(N):
                    nc.tensor.matmul(ps[:, 2 + n, 0:64], mur[:, n, :], c("ident", 0, 64)[:, 0:64], start=True, stop=True)
                    nc.tensor.matmul(ps[0:16, 4, n:n + 1], g1t[:, :], gm[0:64, n, 64:65], start=True, stop=True)

        clear(m_link)
        with nc.Block() as covariance:
            @covariance.vector
            def _(dve):
                step = Link(nc, m_link, dve)
                for n in range(N):
                    step(nc.vector.tensor_copy(mub[:, n, :], ps[:, 2 + n, 0:64]))
                    step(nc.vector.tensor_scalar(mm[:, :], mub[:, n, :], gm[:, n, 64:65], None, ALU.mult))
                    step(nc.vector.tensor_tensor(cov[:, n, :], gm[:, n, 0:64], mm[:, :], ALU.subtract))

            @covariance.scalar
            def _(act):
                nc.scalar.activation(gg[:, :], ps[0:16, 4, 0:N], ACT.Gelu, bias=g1b[:, 0:1])

        with nc.Block() as gate:
            @gate.tensor
            def _(pe):
                nc.tensor.matmul(ps[:, 5, 0:N], g2r[:, :], gg[:, :], start=True, stop=True)

        with nc.Block() as sigmoid:
            @sigmoid.scalar
            def _(act):
                nc.scalar.activation(coef[:, :], ps[:, 5, 0:N], ACT.Sigmoid, bias=g2b[:, 0:1])

        with nc.Block() as scale:
            @scale.vector
            def _(dve):
                nc.vector.tensor_scalar(coef[:, :], coef[:, :], res[:, 0:1], None, ALU.mult)

    def prepare():
        with ExitStack() as ph:
            dup = sbt(ph, "dup", [P, 2, 2, 64])
            hm = sbt(ph, "hm", [P, N])
            wc = sbt(ph, "wc", [P, N, 64])
            wh = sbt(ph, "wh", [P, 64])
            size = sbt(ph, "size", [P, 4])
            t = sbt(ph, "t", [P, N])
            ps = pst(ph, "ps_p", [P, 8, 512])
            clear(m_link)
            with nc.Block() as double:
                @double.vector
                def _(dve):
                    step = Link(nc, m_link, dve)
                    for i, w in enumerate((W1, W2)):
                        nc.vector.tensor_copy(dup[:, i, :, :], prm[:, None, w].to_broadcast([P, 2, 64]))
                    step(nc.vector.tensor_reduce(size[:, 0:1], prm[:, W1], AX.X, ALU.max))
                    step(nc.vector.tensor_reduce(size[:, 1:2], prm[:, W1], AX.X, ALU.min))
                    step(nc.vector.tensor_scalar_mul(size[:, 1:2], size[:, 1:2], -1.0))
                    nc.vector.tensor_tensor(size[:, 0:1], size[:, 0:1], size[:, 1:2], ALU.max)
            with nc.Block() as turn:
                @turn.tensor
                def _(pe):
                    for i in range(2):
                        nc.tensor.transpose(ps[:, i, 0:P], dup[:, i, :, :].rearrange("o a c -> o (a c)"), c("ident"))
                    nc.tensor.matmul(ps[:, 7, 0:1], c("group"), size[:, 0:1], start=True, stop=True)
            clear(m_link)
            with nc.Block() as keep:
                @keep.vector
                def _(dve):
                    step = Link(nc, m_link, dve)
                    nc.vector.tensor_copy(w1t[:, :], ps[:, 0, 0:P])
                    for par in range(2):
                        hp = slice(64 * par, 64 * par + 64)
                        nc.vector.tensor_copy(w1p[hp, par, :], ps[hp, 0, 0:P])
                    nc.vector.tensor_copy(w2n[:, :], ps[:, 1, 0:P])
                    step(nc.vector.tensor_scalar(size[:, 1:2], ps[:, 7, 0:1], 1e-15, None, ALU.max))
                    step(nc.vector.reciprocal(size[:, 2:3], size[:, 1:2]))
                    nc.vector.tensor_scalar(wh[:, :], prm[:, W1], size[:, 2:3], None, ALU.mult)
                    nc.vector.tensor_scalar(size[:, 3:4], size[:, 2:3], size[:, 2:3], GN_EPS, ALU.mult, ALU.mult)
            with nc.Block() as moments:
                @moments.tensor
                def _(pe):
                    for n in range(N):
                        nc.tensor.matmul(ps[:, 2, n:n + 1], w1t[0:64, :], gm[0:64, n, 64:65], start=True, stop=True)
                        nc.tensor.matmul(ps[:, 3 + n, 0:64], w1t[0:64, :], cov[0:64, n, :], start=True, stop=True)
            clear(m_link)
            with nc.Block() as own_variance:
                @own_variance.vector
                def _(dve):
                    step = Link(nc, m_link, dve)
                    nc.vector.tensor_scalar(hm[:, :], ps[:, 2, 0:N], size[:, 2:3], None, ALU.mult)
                    for n in range(N):
                        step(nc.vector.scalar_tensor_tensor(wc[:, n, :], ps[:, 3 + n, 0:64], size[:, 2:3], wh[:, :],
                                                            ALU.mult, ALU.mult))
                    nc.vector.reduce_sum(rstd[:, :], wc[:, :, :], AX.X)
            with nc.Block() as group_mean:
                @group_mean.tensor
                def _(pe):
                    nc.tensor.matmul(ps[:, 5, 0:N], c("group"), hm[:, :], start=True, stop=True)
            clear(m_link)
            with nc.Block() as spread:
                @spread.vector
                def _(dve):
                    step = Link(nc, m_link, dve)
                    step(nc.vector.tensor_scalar_mul(mg[:, :], ps[:, 5, 0:N], 1.0 / GROUP))
                    step(nc.vector.tensor_tensor(t[:, :], hm[:, :], mg[:, :], ALU.subtract))
                    step(nc.vector.tensor_tensor(t[:, :], t[:, :], t[:, :], ALU.mult))
                    step(nc.vector.tensor_tensor(t[:, :], t[:, :], rstd[:, :], ALU.add))
                    nc.vector.tensor_scalar(mg[:, :], mg[:, :], size[:, 1:2], None, ALU.mult)
            with nc.Block() as group_variance:
                @group_variance.tensor
                def _(pe):
                    nc.tensor.matmul(ps[:, 6, 0:N], c("group"), t[:, :], start=True, stop=True)
            clear(m_link)
            with nc.Block() as positive:
                @positive.vector
                def _(dve):
                    nc.vector.tensor_scalar(t[:, :], ps[:, 6, 0:N], 1.0 / GROUP, 0.0, ALU.mult, ALU.max)
            with nc.Block() as root:
                @root.scalar
                def _(act):
                    nc.scalar.activation(t[:, :], t[:, :], ACT.Sqrt, bias=size[:, 3:4])
            clear(m_link)
            with nc.Block() as affine:
                @affine.vector
                def _(dve):
                    step = Link(nc, m_link, dve)
                    step(nc.vector.tensor_scalar(t[:, :], t[:, :], size[:, 1:2], None, ALU.mult))
                    step(nc.vector.reciprocal(rstd[:, :], t[:, :]))
                    step(nc.vector.tensor_scalar(t[:, :], t[:, :], DEVIATION_MAX, None, ALU.is_le))
                    step(nc.vector.tensor_tensor(rstd[:, :], rstd[:, :], t[:, :], ALU.mult))
                    step(nc.vector.tensor_scalar(sc[:, :], rstd[:, :], prm[:, GW], None, ALU.mult))
                    step(nc.vector.tensor_tensor(t[:, :], mg[:, :], sc[:, :], ALU.mult))
                    step(nc.vector.tensor_scalar(bi[:, :], t[:, :], prm[:, GB], -1.0, ALU.subtract, ALU.mult))

    def loss_gradient():
        with ExitStack() as ph:
            st = sbt(ph, "st", [P, N, STRIPS * UNITS * 6])
            mv = sbt(ph, "mv", [P, N, 2])
            t = sbt(ph, "t", [P, 8])
            q = sbt(ph, "q", [P, N])
            abr = sbt(ph, "abr", [64, 2, P])
            ps = pst(ph, "ps_l", [P, 8, 512])
            clear(m_loaded)
            with nc.Block() as load:
                @load.sync
                def _(sp):
                    for n in range(N):
                        sp.dma_start(st[:, n, :], STAT[n].rearrange("p s k -> p (s k)")).then_inc(m_loaded, 16)
                    sp.wait_ge(m_loaded, 16 * N)
            with nc.Block() as merge:
                @merge.vector
                def _(dve):
                    for n in range(N):
                        nc.vector.bn_aggr(mv[:, n, :], st[:, n, :])
            with nc.Block() as mean:
                @mean.tensor
                def _(pe):
                    nc.tensor.matmul(ps[:, 0, 0:N], c("pair"), mv[:, :, 0], start=True, stop=True)
            clear(m_link)
            with nc.Block() as deviations:
                @deviations.vector
                def _(dve):
                    step = Link(nc, m_link, dve)
                    step(nc.vector.reduce_sum(t[:, 0:1], ps[:, 0, 0:N], AX.X))
                    step(nc.vector.tensor_scalar_mul(t[:, 0:1], t[:, 0:1], 1.0 / (2 * N)))
                    step(nc.vector.tensor_scalar(q[:, :], mv[:, :, 0], t[:, 0:1], None, ALU.subtract))
                    step(nc.vector.tensor_tensor(q[:, :], q[:, :], q[:, :], ALU.mult))
                    step(nc.vector.tensor_tensor(q[:, :], q[:, :], mv[:, :, 1], ALU.add))
            with nc.Block() as variance:
                @variance.tensor
                def _(pe):
                    nc.tensor.matmul(ps[:, 1, 0:N], c("pair"), q[:, :], start=True, stop=True)
            clear(m_link)
            count = N * PIX
            with nc.Block() as coefficients:
                @coefficients.vector
                def _(dve):
                    step = Link(nc, m_link, dve)
                    step(nc.vector.reduce_sum(t[:, 1:2], ps[:, 1, 0:N], AX.X))
                    step(nc.vector.tensor_scalar_mul(t[:, 1:2], t[:, 1:2], count / (count - 1.0) / (2 * N)))
                    step(nc.vector.tensor_scalar_add(t[:, 2:3], run[:, 1:2], 1e-8))
                    step(nc.vector.reciprocal(t[:, 3:4], t[:, 2:3]))
                    step(nc.vector.tensor_tensor(t[:, 4:5], t[:, 1:2], t[:, 3:4], ALU.mult))
                    step(nc.vector.tensor_scalar_add(t[:, 4:5], t[:, 4:5], -1.0))
                    step(nc.vector.tensor_tensor(t[:, 4:5], t[:, 4:5], t[:, 3:4], ALU.mult))
                    step(nc.vector.tensor_scalar_mul(ab[:, 1:2], t[:, 4:5], 4.0 / C / (count - 1)))
                    step(nc.vector.tensor_tensor(t[:, 5:6], t[:, 0:1], run[:, 0:1], ALU.subtract))
                    step(nc.vector.tensor_scalar_mul(t[:, 5:6], t[:, 5:6], 2.0 / C / count))
                    step(nc.vector.tensor_tensor(t[:, 6:7], ab[:, 1:2], t[:, 0:1], ALU.mult))
                    step(nc.vector.tensor_tensor(ab[:, 0:1], t[:, 5:6], t[:, 6:7], ALU.subtract))
                    for i in range(2):
                        nc.vector.tensor_copy(abr[:, i, :], ab[0:64, i:i + 1].to_broadcast([64, P]))
                    for par in range(2):
                        hp = slice(64 * par, 64 * par + 64)
                        nc.vector.tensor_scalar(w2b[hp, par, :], w2n[hp, :], ab[hp, 1:2], None, ALU.mult)
                    nc.vector.memset(acc[:, :, :], 0.0)
            with nc.Block() as spread:
                @spread.tensor
                def _(pe):
                    for i in range(2):
                        nc.tensor.matmul(ps[:, 2 + i, 0:64], abr[:, i, :], c("ident", 0, 64)[:, 0:64], start=True, stop=True)
                    nc.tensor.matmul(ps[:, 4, 0:1], w2n[0:64, :], ab[0:64, 0:1], start=True, stop=True)
            with nc.Block() as keep:
                @keep.vector
                def _(dve):
                    nc.vector.tensor_copy(abb[:, :, :], ps[:, 2:4, 0:64])
                    nc.vector.tensor_copy(dbias[:, :], ps[:, 4, 0:1])

    def descend():
        with ExitStack() as ph:
            gr = sbt(ph, "gr", [P, 130])
            t = sbt(ph, "t", [P, N, 64])
            u = sbt(ph, "u", [P, N, 64])
            q = sbt(ph, "q", [P, N])
            th = sbt(ph, "th", [P, N])
            gs = sbt(ph, "gs", [P, 2, N])
            ms = sbt(ph, "ms", [P, 2, N])
            ps = pst(ph, "ps_d", [P, 8, 512])
            clear(m_link)
            with nc.Block() as outer:
                @outer.vector
                def _(dve):
                    step = Link(nc, m_link, dve)
                    step(nc.vector.tensor_tensor(gr[:, W2], acc[:, 0, 65:129], acc[:, 1, 65:129], ALU.add))
                    step(nc.vector.tensor_tensor(q[:, 0:1], acc[:, 0, 129:130], acc[:, 1, 129:130], ALU.add))
                    step(nc.vector.tensor_tensor(gr[:, W2], gr[:, W2], abb[:, 1, :], ALU.mult))
                    step(nc.vector.tensor_scalar(t[:, 0, :], abb[:, 0, :], q[:, 0:1], None, ALU.mult))
                    step(nc.vector.tensor_tensor(gr[:, W2], gr[:, W2], t[:, 0, :], ALU.add))
                    step(nc.vector.tensor_tensor(gr[:, GB], acc[:, 0, 64:65], acc[:, 1, 64:65], ALU.add))
                    for n in range(N):
                        step(nc.vector.tensor_tensor(t[:, n, :], acc[:, n, 0:64], prm[:, W1], ALU.mult))
                    step(nc.vector.reduce_sum(q[:, :], t[:, :, :], AX.X))
                    step(nc.vector.tensor_tensor(th[:, :], mg[:, :], acc[:, :, 64], ALU.mult))
                    step(nc.vector.tensor_tensor(th[:, :], q[:, :], th[:, :], ALU.subtract))
                    step(nc.vector.tensor_tensor(th[:, :], th[:, :], rstd[:, :], ALU.mult))
                    step(nc.vector.reduce_sum(gr[:, GW], th[:, :], AX.X))
                    step(nc.vector.tensor_scalar(gs[:, 0, :], acc[:, :, 64], prm[:, GW], None, ALU.mult))
                    step(nc.vector.tensor_scalar(gs[:, 1, :], th[:, :], prm[:, GW], None, ALU.mult))
            with nc.Block() as groups:
                @groups.tensor
                def _(pe):
                    nc.tensor.matmul(ps[:, 0, 0:2 * N], c("group"), gs[:, :, :].rearrange("p a n -> p (a n)"),
                                     start=True, stop=True)
                    for n in range(N):
                        nc.tensor.matmul(ps[:, 1 + n, 0:64], w1t[0:64, :], gm[0:64, n, 0:64], start=True, stop=True)
            clear(m_link)
            with nc.Block() as inner:
                @inner.vector
                def _(dve):
                    step = Link(nc, m_link, dve)
                    step(nc.vector.tensor_scalar_mul(ms[:, :, :].rearrange("p a n -> p (a n)"), ps[:, 0, 0:2 * N], 1.0 / GROUP))
                    for n in range(N):
                        step(nc.vector.tensor_scalar(u[:, n, :], mub[:, n, :], mg[:, n:n + 1], None, ALU.mult))
                        step(nc.vector.tensor_tensor(u[:, n, :], ps[:, 1 + n, 0:64], u[:, n, :], ALU.subtract))
                        step(nc.vector.tensor_scalar(u[:, n, :], u[:, n, :], rstd[:, n:n + 1], ms[:, 1, n:n + 1],
                                                     ALU.mult, ALU.mult))
                        step(nc.vector.tensor_scalar(t[:, n, :], mub[:, n, :], ms[:, 0, n:n + 1], None, ALU.mult))
                        step(nc.vector.tensor_tensor(u[:, n, :], u[:, n, :], t[:, n, :], ALU.add))
                        step(nc.vector.tensor_scalar(t[:, n, :], acc[:, n, 0:64], prm[:, GW], None, ALU.mult))
                        step(nc.vector.tensor_tensor(t[:, n, :], t[:, n, :], u[:, n, :], ALU.subtract))
                        step(nc.vector.tensor_scalar(t[:, n, :], t[:, n, :], rstd[:, n:n + 1], None, ALU.mult))
                    step(nc.vector.tensor_tensor(gr[:, W1], t[:, 0, :], t[:, 1, :], ALU.add))
                    step(nc.vector.tensor_scalar_mul(mom[:, :], mom[:, :], MOM))
                    step(nc.vector.tensor_tensor(mom[:, :], mom[:, :], gr[:, :], ALU.add))
                    step(nc.vector.tensor_scalar_mul(gr[:, :], mom[:, :], LR))
                    step(nc.vector.tensor_tensor(prm[:, :], prm[:, :], gr[:, :], ALU.subtract))

    with nc.Fori(0, STEPS):
        prepare()
        forward(*env, x_in, prm, w1p, sc, bi, STAT, None, None)
        loss_gradient()
        backward(*env, x_in, prm, w1p, w2b, sc, bi, dbias, acc)
        descend()
    prepare()
    forward(*env, x_in, prm, w1p, sc, bi, None, coef, out)
    ctx.close()


def gram_pass(nc, sbt, pst, clear, c, S, allsems, x_in, gram):
    clear(*allsems, start={S[k]: BODY for k in ("turned", "copied", "gram_done", "summed")})
    with ExitStack() as ph:
        xs = sbt(ph, "xs", [P, N, SRP, W])
        xt = sbt(ph, "xt", [P, 2, 4, P + 1])
        pt = pst(ph, "ps_t", [P, 2, 512])
        pg = pst(ph, "ps_g", [P, 2, 512])
        with nc.Block() as ones:
            @ones.vector
            def _(dve):
                nc.vector.memset(xt[:, :, :, P:P + 1], 1.0)
        with nc.Block() as block:
            @block.sync
            def _(sp):
                with sp.Fori(0, STRIPS) as s:
                    for n in range(N):
                        sp.wait_ge(S["turned"], first_unit(s, n) + LAST)
                        sp.dma_start(xs[:, n, :, :], x_in[n, :, bass.ds(s * SRP + 1, SRP), :]
                                     ).then_inc(S[f"in_loaded{n}"], 16)

            @block.tensor
            def _(pe):
                def turn(s, n, k):
                    if k == 0:
                        pe.wait_ge(S[f"in_loaded{n}"], s * 16 + 16)
                    pe.wait_ge(S["copied"], first_unit(s, n) + k + FREE)
                    cols = rows(xs, n, k).rearrange("p r w -> p (r w)")
                    for b in range(4):
                        mm = nc.tensor.transpose(pt[:, k % 2, P * b:P * b + P], cols[:, P * b:P * b + P], c("ident"))
                    mm.then_inc(S["turned"], 1)

                def product(s, n, k):
                    u = first_unit(s, n) + k
                    pe.wait_ge(S["copied"], u + DONE)
                    if k == 0:
                        pe.wait_ge(S["summed"], s * N + n - 1 + BODY)
                    for b in range(4):
                        mm = nc.tensor.matmul(pg[:, n, 0:P + 1], xt[:, k % 2, b, 0:P], xt[:, k % 2, b, :],
                                              start=(k + b == 0), stop=(k == UNITS - 1 and b == 3))
                    mm.then_inc(S["gram_done"], 1)

                with pe.Fori(0, STRIPS) as s:
                    for i in range(BODY + 1):
                        if i < BODY:
                            turn(s, i // UNITS, i % UNITS)
                        if i >= 1:
                            product(s, (i - 1) // UNITS, (i - 1) % UNITS)

            @block.scalar
            def _(act):
                with act.Fori(0, STRIPS) as s:
                    for n in range(N):
                        for k in range(UNITS):
                            u = first_unit(s, n) + k
                            act.wait_ge(S["turned"], u + DONE)
                            act.wait_ge(S["gram_done"], u + FREE)
                            nc.scalar.copy(xt[:, k % 2, :, 0:P], pt[:, k % 2, :].rearrange("p (b c) -> p b c", b=4)
                                           ).then_inc(S["copied"], 1)

            @block.vector
            def _(dve):
                with dve.Fori(0, STRIPS) as s:
                    for n in range(N):
                        dve.wait_ge(S["gram_done"], first_unit(s, n) + UNITS - 1 + DONE)
                        dve.wait_ge(S["summed"], s * N + n - 1 + BODY)
                        nc.vector.tensor_tensor(gram[:, n, :], gram[:, n, :], pg[:, n, 0:P + 1], ALU.add
                                                ).then_inc(S["summed"], 1)


def hidden_on_pe(nc, pe, S, u, s, n, k, w1p, xs, ph):
    if k == 0:
        pe.wait_ge(S[f"in_loaded{n}"], s * 16 + 16)
    for par in range(2):
        mm = nc.tensor.matmul(ph[:, par, :], w1p[:, par, :], rows(xs, n, k), start=True, stop=True)
    mm.then_inc(S["h_done"], 1)


def forward(nc, sbt, pst, clear, c, S, allsems, x_in, prm, w1p, sc, bi, STAT, coef, out):
    names = "h_done gelu_ready y_done y_ready stats_ready out_ready".split()
    last = out is not None
    clear(*allsems, start={**{S[k]: BODY for k in names}, S["out_stored0"]: 32, S["out_stored1"]: 32})
    per_store = 32 if last else 16
    if not last:
        clear(S["out_stored0"], S["out_stored1"], start={S["out_stored0"]: 16, S["out_stored1"]: 16})
    with ExitStack() as ctx:
        xs = sbt(ctx, "xs", [P, N, SRP, W])
        g = sbt(ctx, "g", [P, 2, 2, COLS])
        ys = sbt(ctx, "ys", [P, N, SRP, W])
        st = sbt(ctx, "stats", [P, N, UNITS * 6])
        ph = pst(ctx, "ps_h", [P, 2, 2, COLS])
        py = pst(ctx, "ps_y", [P, 2, COLS])
        with nc.Block() as block:
            @block.sync
            def _(sp):
                def load(s, n):
                    sp.wait_ge(S["y_ready"], first_unit(s, n) + LAST)
                    sp.dma_start(xs[:, n, :, :], x_in[n, :, bass.ds(s * SRP + 1, SRP), :]
                                 ).then_inc(S[f"in_loaded{n}"], 16)

                def store(s, n):
                    if last:
                        sp.wait_ge(S["y_ready"], first_unit(s, n) + UNITS - 1 + DONE)
                        image = out[n].rearrange("c (r p) w -> p c r w", p=2)
                        for par in range(2):
                            sp.dma_start(image[par, :, bass.ds(s * SRP, SRP), :], ys[64 * par:64 * par + 64, n, :, :]
                                         ).then_inc(S[f"out_stored{n}"], 16)
                    else:
                        sp.wait_ge(S["stats_ready"], first_unit(s, n) + UNITS - 1 + DONE)
                        sp.dma_start(STAT[n, :, s, :], st[:, n, :]).then_inc(S[f"out_stored{n}"], 16)

                run_strips(sp, load, store)
                for n in range(N):
                    sp.wait_ge(S[f"out_stored{n}"], per_store * (STRIPS + 1))

            @block.tensor
            def _(pe):
                def hidden(s, n, k):
                    u = first_unit(s, n) + k
                    pe.wait_ge(S["gelu_ready"], u + FREE)
                    hidden_on_pe(nc, pe, S, u, s, n, k, w1p, xs, ph[:, k % 2, :, :])

                def project(s, n, k):
                    u = first_unit(s, n) + k
                    pe.wait_ge(S["gelu_ready"], u + DONE)
                    pe.wait_ge(S["y_ready"], u + FREE)
                    for par in range(2):
                        mm = nc.tensor.matmul(py[64 * par:64 * par + 64, k % 2, :], prm[:, 64:128], g[:, k % 2, par, :],
                                              start=True, stop=True)
                    mm.then_inc(S["y_done"], 1)

                with pe.Fori(0, STRIPS) as s:
                    for i in range(BODY + 1):
                        if i < BODY:
                            hidden(s, i // UNITS, i % UNITS)
                        if i >= 1:
                            project(s, (i - 1) // UNITS, (i - 1) % UNITS)

            @block.scalar
            def _(act):
                with act.Fori(0, STRIPS) as s:
                    for n in range(N):
                        for k in range(UNITS):
                            u = first_unit(s, n) + k
                            act.wait_ge(S["h_done"], u + DONE)
                            act.wait_ge(S["y_done"], u + FREE)
                            nc.scalar.activation(g[:, k % 2, :, :], ph[:, k % 2, :, :], ACT.Gelu, bias=bi[:, n:n + 1],
                                                 scale=sc[:, n:n + 1]).then_inc(S["gelu_ready"], 1)

            @block.vector
            def _(dve):
                with dve.Fori(0, STRIPS) as s:
                    for n in range(N):
                        for k in range(UNITS):
                            u = first_unit(s, n) + k
                            dve.wait_ge(S["y_done"], u + DONE)
                            if k == 0 and last:
                                dve.wait_ge(S[f"out_stored{n}"], s * 32 + 32)
                            if last:
                                nc.vector.scalar_tensor_tensor(rows(ys, n, k), as_rows(py[:, k % 2, :]), coef[:, n:n + 1],
                                                               rows(xs, n, k), ALU.mult, ALU.add).then_inc(S["y_ready"], 1)
                            else:
                                dve.wait_ge(S["stats_ready"], u + FREE)
                                nc.vector.tensor_tensor(rows(ys, n, k), as_rows(py[:, k % 2, :]), rows(xs, n, k), ALU.add
                                                        ).then_inc(S["y_ready"], 1)
                                dve.wait_ge(S["y_ready"], u + DONE)
                                if k == 0:
                                    dve.wait_ge(S[f"out_stored{n}"], s * 16 + 16)
                                nc.vector.bn_stats(st[:, n, 6 * k:6 * k + 6], rows(ys, n, k).rearrange("p r w -> p (r w)")
                                                   ).then_inc(S["stats_ready"], 1)


def backward(nc, sbt, pst, clear, c, S, allsems, x_in, prm, w1p, w2b, sc, bi, dbias, acc):
    names = """h_done gelu_ready z_ready zz_ready den_ready gz_ready density_ready tail_ready inverse_ready phi_ready
        dgelu_ready y_done y_ready d_done dh_ready ef_done summed
        turned_x turned_y turned_g0 turned_g1 turned_d0 turned_d1
        copied_x copied_y copied_g0 copied_g1 copied_d0 copied_d1""".split()
    clear(*allsems, start={S[k]: BODY for k in names})
    RING, LAG = 4, 3
    assert BODY % RING == 0

    def steps(eng, step):
        for i in range(BODY):
            step(0, i, lambda lag: i >= lag)
        with eng.Fori(1, STRIPS) as s:
            for i in range(BODY):
                step(s, i, lambda lag: True)
        for i in range(RING):
            step(STRIPS, i, lambda lag: i < lag)

    def place(i, lag=0):
        return divmod((i - lag) % BODY, UNITS)

    with ExitStack() as ctx:
        xs = sbt(ctx, "xs", [P, N, SRP, W])
        g = sbt(ctx, "g", [P, RING, 2, COLS])
        z = sbt(ctx, "z", [P, RING, 2, COLS])
        zz = sbt(ctx, "zz", [P, RING, 2, COLS])
        den = sbt(ctx, "den", [P, RING, 2, COLS])
        gz = sbt(ctx, "gz", [P, RING, 2, COLS])
        ys = sbt(ctx, "ys", [P, RING, COLS])
        dh = sbt(ctx, "dh", [P, 2, 2, COLS])
        xt = sbt(ctx, "xt", [P, RING, 4, 2, 65])
        yt = sbt(ctx, "yt", [P, 4, 2, 65])
        gt = sbt(ctx, "gt", [P, 2, 4, HID])
        dt = sbt(ctx, "dt", [P, 2, 4, HID])
        ph = pst(ctx, "ps_h", [P, 2, COLS])
        pd = pst(ctx, "ps_d", [P, 2, COLS])
        py = pst(ctx, "ps_y", [P, COLS])
        pt = pst(ctx, "ps_t", [P, 2, 512])
        pe_ = pst(ctx, "ps_e", [P, 512])
        with nc.Block() as ones:
            @ones.vector
            def _(dve):
                for r in range(RING):
                    nc.vector.memset(xt[:, r, :, :, 64:65], 1.0)
                nc.vector.memset(yt[:, :, :, 64:65], 1.0)

        with nc.Block() as block:
            @block.sync
            def _(sp):
                with sp.Fori(0, STRIPS) as s:
                    for n in range(N):
                        sp.wait_ge(S["y_ready"], first_unit(s, n) + LAST)
                        sp.dma_start(xs[:, n, :, :], x_in[n, :, bass.ds(s * SRP + 1, SRP), :]
                                     ).then_inc(S[f"in_loaded{n}"], 16)

            @block.tensor
            def _(pe):
                def turn(src, slot, turned):
                    for b in range(4):
                        mm = nc.tensor.transpose(pt[:, slot, P * b:P * b + P], src[:, P * b:P * b + P], c("ident"))
                    mm.then_inc(S[turned], 1)

                def step(s, i, real):
                    u = s * BODY + i
                    v, r = u - LAG, (i - LAG) % RING
                    n, k = place(i)
                    nv, kv = place(i, LAG)
                    front, back = real(0), real(LAG)
                    if back:
                        pe.wait_ge(S["y_ready"], v + DONE)
                        pe.wait_ge(S["dh_ready"], v - 1 + DONE)
                        for par in range(2):
                            mm = nc.tensor.matmul(pd[:, par, :], w2b[:, par, :], ys[:, r, :], start=True, stop=True)
                        mm.then_inc(S["d_done"], 1)
                        pe.wait_ge(S["copied_d0"], v - 1 + DONE)
                        turn(g[:, r, 0, :], 0, "turned_g0")
                        pe.wait_ge(S["copied_d1"], v - 1 + DONE)
                        if not real(LAG + 1):
                            pe.wait_ge(S["copied_x"], u - 1 + DONE)
                        turn(g[:, r, 1, :], 1, "turned_g1")
                    if front:
                        pe.wait_ge(S["zz_ready"], u - 1 + DONE)
                        hidden_on_pe(nc, pe, S, u, s, n, k, w1p, xs, ph)
                    if back:
                        pe.wait_ge(S["copied_g0"], v + DONE)
                        turn(ys[:, r, :], 0, "turned_y")
                    if front:
                        if back:
                            pe.wait_ge(S["copied_g1"], v + DONE)
                        else:
                            pe.wait_ge(S["copied_x"], u - 1 + DONE)
                        turn(rows(xs, n, k).rearrange("p r w -> p (r w)"), 1, "turned_x")
                    if back:
                        pe.wait_ge(S["copied_y"], v + DONE)
                        pe.wait_ge(S["dh_ready"], v + DONE)
                        turn(dh[:, kv % 2, 0, :], 0, "turned_d0")
                        if front:
                            pe.wait_ge(S["copied_x"], u + DONE)
                        else:
                            pe.wait_ge(S["copied_g1"], v + DONE)
                        turn(dh[:, kv % 2, 1, :], 1, "turned_d1")
                    if front:
                        pe.wait_ge(S["gelu_ready"], u + DONE)
                        pe.wait_ge(S["y_ready"], u - 1 + DONE)
                        for par in range(2):
                            mm = nc.tensor.matmul(py[64 * par:64 * par + 64, :], prm[:, 64:128], g[:, i % RING, par, :],
                                                  start=True, stop=True)
                        mm.then_inc(S["y_done"], 1)
                    if back:
                        pe.wait_ge(S["copied_d0"], v + DONE)
                        pe.wait_ge(S["copied_d1"], v + DONE)
                        if kv == 0:
                            pe.wait_ge(S["summed"], s * N + (i - LAG) // UNITS - 1 + DONE)
                        for b in range(4):
                            for par in range(2):
                                to, at = (31, 0) if par == 0 else (0, 34)
                                flat = xt[:, r, b, :, :].rearrange("p a c -> p (a c)")
                                nc.tensor.matmul(pe_[:, to:to + 96], dt[:, par, b, :], flat[:, at:at + 96],
                                                 start=(kv + par + b == 0), stop=False, skip_group_check=True)
                                flat = yt[:, b, :, :].rearrange("p a c -> p (a c)")
                                mm = nc.tensor.matmul(pe_[:, 128 + to:224 + to], gt[:, par, b, :], flat[:, at:at + 96],
                                                      start=False, stop=(kv == UNITS - 1 and par == 1 and b == 3),
                                                      skip_group_check=True)
                        mm.then_inc(S["ef_done"], 1)

                steps(pe, step)

            @block.scalar
            def _(act):
                def copy_hidden(v, dst, slot, name):
                    act.wait_ge(S["turned_" + name], v + DONE)
                    nc.scalar.copy(dst, pt[:, slot, :].rearrange("p (b c) -> p b c", b=4)
                                   ).then_inc(S["copied_" + name], 1)

                def copy_channels(v, dst, slot, name):
                    act.wait_ge(S["turned_" + name], v + DONE)
                    nc.scalar.copy(dst, pt[:, slot, :].rearrange("p (b a c) -> p b a c", b=4, a=2)
                                   ).then_inc(S["copied_" + name], 1)

                def step(s, i, real):
                    u = s * BODY + i
                    v = u - LAG
                    n, k = place(i)
                    front, back = real(0), real(LAG)

                    def affine(dst, func, name):
                        nc.scalar.activation(dst[:, i % RING, :, :], ph[:, :, :], func, bias=bi[:, n:n + 1],
                                             scale=sc[:, n:n + 1]).then_inc(S[name], 1)

                    if back:
                        act.wait_ge(S["ef_done"], v - 1 + DONE)
                        copy_hidden(v, gt[:, 0, :, :], 0, "g0")
                        copy_hidden(v, gt[:, 1, :, :], 1, "g1")
                    if front:
                        act.wait_ge(S["h_done"], u + DONE)
                        act.wait_ge(S["turned_g1"], u - RING + DONE)
                        act.wait_ge(S["dgelu_ready"], u - RING + DONE)
                        affine(g, ACT.Gelu, "gelu_ready")
                    if back:
                        copy_channels(v, yt[:, :, :, 0:64], 0, "y")
                    if front:
                        act.wait_ge(S["ef_done"], u - RING + DONE)
                        copy_channels(u, xt[:, i % RING, :, :, 0:64], 1, "x")
                        affine(z, ACT.Identity, "z_ready")
                    if back:
                        copy_hidden(v, dt[:, 1, :, :], 1, "d1")
                    if front:
                        affine(zz, ACT.Square, "zz_ready")
                        act.wait_ge(S["zz_ready"], u + DONE)
                        nc.scalar.activation(den[:, i % RING, :, :], zz[:, i % RING, :, :], ACT.Identity, bias=c("tiny")
                                             ).then_inc(S["den_ready"], 1)
                        if i % 2 == 1:
                            act.wait_ge(S["den_ready"], u + DONE)
                            for j in ((i - 1) % RING, i % RING):
                                nc.scalar.activation(zz[:, j, :, :], zz[:, j, :, :], ACT.Exp, bias=c("log_peak"),
                                                     scale=-0.5).then_inc(S["density_ready"], 1)

                steps(act, step)

            @block.gpsimd
            def _(pool):
                def step(s, i, real):
                    u = s * BODY + i
                    if real(2):
                        w, r = u - 2, (i - 2) % RING
                        pool.wait_ge(S["density_ready"], w + DONE)
                        pool.wait_ge(S["gz_ready"], w + DONE)
                        nc.gpsimd.tensor_tensor(z[:, r, :, :], zz[:, r, :, :], z[:, r, :, :], ALU.mult
                                                ).then_inc(S["tail_ready"], 1)
                        pool.wait_ge(S["tail_ready"], w + DONE)
                        pool.wait_ge(S["phi_ready"], w + DONE)
                        nc.gpsimd.tensor_tensor(gz[:, r, :, :], gz[:, r, :, :], z[:, r, :, :], ALU.add
                                                ).then_inc(S["dgelu_ready"], 1)
                    if real(0):
                        pool.wait_ge(S["z_ready"], u + DONE)
                        pool.wait_ge(S["dh_ready"], u - RING + DONE)
                        nc.gpsimd.tensor_tensor(gz[:, i % RING, :, :], g[:, i % RING, :, :], z[:, i % RING, :, :], ALU.mult
                                                ).then_inc(S["gz_ready"], 1)

                steps(pool, step)

            @block.vector
            def _(dve):
                def step(s, i, real):
                    u = s * BODY + i
                    v, w = u - LAG, u - 1
                    nw, kw = place(i, 1)
                    r = (i - 1) % RING
                    if real(LAG):
                        j, slot = (i - LAG) % RING, (i - LAG) % 2
                        dve.wait_ge(S["d_done"], v + DONE)
                        dve.wait_ge(S["dgelu_ready"], v + DONE)
                        dve.wait_ge(S["turned_d1"], v - 2 + DONE)
                        nc.vector.scalar_tensor_tensor(dh[:, slot, :, :].rearrange("p a c -> p (a c)"),
                                                       pd[:, :, :].rearrange("p a c -> p (a c)"), dbias[:, 0:1],
                                                       gz[:, j, :, :].rearrange("p a c -> p (a c)"),
                                                       ALU.add, ALU.mult).then_inc(S["dh_ready"], 1)
                    if real(1):
                        dve.wait_ge(S["y_done"], w + DONE)
                        dve.wait_ge(S["turned_y"], w - RING + DONE)
                        nc.vector.tensor_tensor(as_rows(ys[:, r, :]), as_rows(py[:, :]), rows(xs, nw, kw), ALU.add
                                                ).then_inc(S["y_ready"], 1)
                    n, k = place(i, RING)
                    if real(RING) and k == UNITS - 1:
                        sums = s * N + (i - RING) // UNITS
                        dve.wait_ge(S["ef_done"], u - RING + DONE)
                        dve.wait_ge(S["summed"], sums - 1 + DONE)
                        nc.vector.tensor_tensor(acc[:, n, :].rearrange("p (a c) -> p a c", a=2),
                                                acc[:, n, :].rearrange("p (a c) -> p a c", a=2),
                                                pe_[:, 0:256].rearrange("p (a c) -> p a c", a=2)[:, :, 31:96], ALU.add
                                                ).then_inc(S["summed"], 1)
                    if real(1):
                        dve.wait_ge(S["den_ready"], w + DONE)
                        nc.vector.reciprocal(den[:, r, 0, :], den[:, r, 0, :])
                    if real(LAG):
                        dve.wait_ge(S["turned_d0"], v + DONE)
                        dve.wait_ge(S["ef_done"], v - 1 + DONE)
                        nc.vector.tensor_copy(dt[:, 0, :, :], pt[:, 0, :].rearrange("p (b c) -> p b c", b=4)
                                              ).then_inc(S["copied_d0"], 1)
                    if real(1):
                        nc.vector.reciprocal(den[:, r, 1, :], den[:, r, 1, :]).then_inc(S["inverse_ready"], 1)
                        dve.wait_ge(S["inverse_ready"], w + DONE)
                        dve.wait_ge(S["gz_ready"], w + DONE)
                        nc.vector.scalar_tensor_tensor(gz[:, r, :, :], gz[:, r, :, :], TINY / 2, den[:, r, :, :],
                                                       ALU.add, ALU.mult).then_inc(S["phi_ready"], 1)

                steps(dve, step)
_INS = ["x"] + [f"L0_conv_{k}" for k in "pos_w pos_b ln1_g ln1_b qkv_w qkv_b lepe_w lepe_b wo_w wo_b ln2_g ln2_b fc1_w fc1_b pw_w dw_w dw_b fc2_w fc2_b".split()] + [
    f"L1_conv_{k}" for k in "w1 gn_w gn_b w2 g1_w g1_b g2_w g2_b running_mean running_var residual_scale".split()]


def kernel(**inputs):
    import concourse.bacc as _bacc
    from concourse import mybir as _mybir
    from concourse.bass_utils import run_bass_kernel_spmd as _run

    nc = _bacc.Bacc("TRN2", target_bir_lowering=False, num_devices=1)
    arrays, args = {}, {}
    for name in _INS:
        a = np.ascontiguousarray(inputs[name])
        arrays[f"in_{name}"] = a
        args[name.replace("L0_conv_", "").replace("L1_conv_", "m_")] = nc.dram_tensor(
            f"in_{name}", a.shape, _mybir.dt.from_np(a.dtype), kind="ExternalInput").ap()
    cst, _ = constants()
    arrays["in_constants"] = cst
    args["cst"] = nc.dram_tensor("in_constants", cst.shape, _mybir.dt.float32, kind="ExternalInput").ap()
    out = nc.dram_tensor("out_image", [N, C, H, W], _mybir.dt.float32, kind="ExternalOutput").ap()
    build(nc, args, out)
    r = _run(nc, [arrays], core_ids=[0])
    return r.results[0]["out_image"]
```
